# Optimizing a Trainium2 kernel written in Bass

```python
import numpy as np
import jax
import jax.numpy as jnp

def _softmax(x, axis=-1):
    return jax.nn.softmax(x, axis=axis)

def _gelu(x):
    return jax.nn.gelu(x, approximate=True)

def _silu(x):
    return jax.nn.silu(x)

def _sigmoid(x):
    return jax.nn.sigmoid(x)

def _layernorm(x, axis=-1, eps=1e-05):
    m = jnp.mean(x, axis=axis, keepdims=True)
    v = jnp.var(x, axis=axis, keepdims=True)
    return (x - m) / jnp.sqrt(v + eps)

def _scatter_add(tgt, idx, src, axis=0):
    return tgt.at[idx].add(src)

def _segment_sum(src, seg, n):
    return jax.ops.segment_sum(src, seg, n)
kernel_name = 'mk_adaln_d1_jaxref_r2_3463e7'

def setup_inputs(seed: int=0):
    np.random.seed(seed)
    _w = jnp.asarray

    def _L0_attn_setup():
        import jax, jax.numpy as jnp
        import numpy as np
        D_MODEL = 512
        N_HEAD = 16
        SEG = 128
        HEAD_DIM = D_MODEL // N_HEAD
        SCALE = 1.0 / HEAD_DIM ** 0.5
        key = jax.random.key(seed)
        ks = jax.random.split(key, 9)
        B, L, D = (4, 2048, D_MODEL)
        s = 1.0 / np.sqrt(D)
        x = jax.random.normal(ks[0], (B, L, D), dtype=jnp.float32)
        Wq = jax.random.uniform(ks[1], (D, D), jnp.float32, -s, s)
        bq = jax.random.uniform(ks[2], (D,), jnp.float32, -s, s)
        Wk = jax.random.uniform(ks[3], (D, D), jnp.float32, -s, s)
        bk = jax.random.uniform(ks[4], (D,), jnp.float32, -s, s)
        Wv = jax.random.uniform(ks[5], (D, D), jnp.float32, -s, s)
        bv = jax.random.uniform(ks[6], (D,), jnp.float32, -s, s)
        Wo = jax.random.uniform(ks[7], (D, D), jnp.float32, -s, s)
        bo = jax.random.uniform(ks[8], (D,), jnp.float32, -s, s)
        return {'x': x, 'Wq': Wq, 'bq': bq, 'Wk': Wk, 'bk': bk, 'Wv': Wv, 'bv': bv, 'Wo': Wo, 'bo': bo}
    _L0_attn_in = _L0_attn_setup()

    def _L0_ffn_setup():
        import jax, jax.numpy as jnp
        import numpy as np
        B, S, D, H, E = (8, 1024, 512, 2048, 16)
        key = jax.random.key(seed)
        ks = jax.random.split(key, 4)
        sd = 1.0 / np.sqrt(D).astype(np.float32)
        sh = 1.0 / np.sqrt(H).astype(np.float32)
        return {'x': jax.random.normal(ks[0], (B, S, D), jnp.float32), 'Wg': jax.random.normal(ks[1], (D, E), jnp.float32) * sd, 'bg': jnp.zeros((E,), jnp.float32), 'W1': jax.random.normal(ks[2], (E, D, H), jnp.float32) * sd, 'b1': jnp.zeros((E, H), jnp.float32), 'W2': jax.random.normal(ks[3], (E, H, D), jnp.float32) * sh, 'b2': jnp.zeros((E, D), jnp.float32)}
    _L0_ffn_in = _L0_ffn_setup()
    _L0_c = _w((lambda *s: np.random.randn(*s).astype(np.float32) * 0.05)(4, 512))
    _L0_wmod = _w((lambda *s: np.random.randn(*s).astype(np.float32) * 0.05)(512, 6 * 512) * 512 ** (-0.5))
    _d = {'L0_attn_x': _L0_attn_in['x'], 'L0_attn_Wq': _L0_attn_in['Wq'], 'L0_attn_bq': _L0_attn_in['bq'], 'L0_attn_Wk': _L0_attn_in['Wk'], 'L0_attn_bk': _L0_attn_in['bk'], 'L0_attn_Wv': _L0_attn_in['Wv'], 'L0_attn_bv': _L0_attn_in['bv'], 'L0_attn_Wo': _L0_attn_in['Wo'], 'L0_attn_bo': _L0_attn_in['bo'], 'L0_ffn_Wg': _L0_ffn_in['Wg'], 'L0_ffn_bg': _L0_ffn_in['bg'], 'L0_ffn_W1': _L0_ffn_in['W1'], 'L0_ffn_b1': _L0_ffn_in['b1'], 'L0_ffn_W2': _L0_ffn_in['W2'], 'L0_ffn_b2': _L0_ffn_in['b2'], 'L0_c': _L0_c, 'L0_wmod': _L0_wmod}
    _x0 = _d['L0_attn_x']
    _d['L0_attn_x'] = jax.random.normal(jax.random.fold_in(jax.random.key(seed), 1), (4, 2048, 512), dtype=_x0.dtype)
    del _x0
    return _d

def reference(L0_attn_x, L0_attn_Wq, L0_attn_bq, L0_attn_Wk, L0_attn_bk, L0_attn_Wv, L0_attn_bv, L0_attn_Wo, L0_attn_bo, L0_ffn_Wg, L0_ffn_bg, L0_ffn_W1, L0_ffn_b1, L0_ffn_W2, L0_ffn_b2, L0_c, L0_wmod):

    def _L0_attn_ref(x, Wq, bq, Wk, bk, Wv, bv, Wo, bo):
        import jax, jax.numpy as jnp
        import numpy as np
        D_MODEL = 512
        N_HEAD = 16
        SEG = 128
        HEAD_DIM = D_MODEL // N_HEAD
        SCALE = 1.0 / HEAD_DIM ** 0.5
        B, L, D = x.shape
        n_seg = L // SEG
        xs = x.reshape(B, n_seg, SEG, D)
        Q = jnp.einsum('bnsd,ed->bnse', xs, Wq) + bq
        K = jnp.einsum('bnsd,ed->bnse', xs, Wk) + bk
        V = jnp.einsum('bnsd,ed->bnse', xs, Wv) + bv
        scores = jnp.einsum('bnse,bnte->bnst', Q, K) * SCALE
        attn = jax.nn.softmax(scores, axis=-1)
        local = jnp.einsum('bnst,bnte->bnse', attn, V)
        summ = xs[:, :, 0, :]
        Qg = jnp.einsum('bnd,ed->bne', summ, Wq) + bq
        Kg = jnp.einsum('bnd,ed->bne', summ, Wk) + bk
        Vg = jnp.einsum('bnd,ed->bne', summ, Wv) + bv
        scores_g = jnp.einsum('bne,bme->bnm', Qg, Kg) * SCALE
        attn_g = jax.nn.softmax(scores_g, axis=-1)
        global_out = jnp.einsum('bnm,bme->bne', attn_g, Vg)
        out = local + global_out[:, :, None, :]
        out = out.reshape(B, L, D)
        return jnp.einsum('bld,ed->ble', out, Wo) + bo

    def _L0_ffn_ref(x, Wg, bg, W1, b1, W2, b2):
        import jax, jax.numpy as jnp
        import numpy as np
        B, S, D, H, E = (8, 1024, 512, 2048, 16)
        d = x.shape[-1]
        xf = x.reshape(-1, d)
        n_tok = xf.shape[0]
        n_exp = Wg.shape[1]
        cap = -(-n_tok // n_exp)
        score = jax.nn.softmax(xf @ Wg + bg, axis=-1)
        gate = jnp.max(score, axis=-1)
        idx = jnp.argmax(score, axis=-1)
        onehot = jax.nn.one_hot(idx, n_exp, dtype=jnp.int32)
        pos = jnp.sum((jnp.cumsum(onehot, axis=0) - 1) * onehot, axis=-1)
        keep = pos < cap
        safe_pos = jnp.where(keep, pos, cap - 1)
        buf = jnp.zeros((n_exp, cap, d), x.dtype).at[idx, safe_pos].add(jnp.where(keep[:, None], xf, 0.0))
        h = jax.nn.relu(jnp.einsum('ecd,edh->ech', buf, W1) + b1[:, None, :])
        y = jnp.einsum('ech,ehd->ecd', h, W2) + b2[:, None, :]
        out = y[idx, safe_pos] * gate[:, None]
        out = jnp.where(keep[:, None], out, 0.0)
        return out.reshape(x.shape)
    x = L0_attn_x
    mod = (_silu(L0_c) @ L0_wmod).reshape(L0_c.shape[0], 6, 1, -1)
    sa, ca, ga, sb, cb, gb = (mod[:, 0], mod[:, 1], mod[:, 2], mod[:, 3], mod[:, 4], mod[:, 5])
    ga = (2 * (ga >= 0) - 1) * jnp.maximum(jnp.abs(ga), 0.25)
    gb = (2 * (gb >= 0) - 1) * jnp.maximum(jnp.abs(gb), 0.25)
    h = _layernorm(x, axis=-1) * (1 + ca) + sa
    x = x + ga * _L0_attn_ref(h, L0_attn_Wq, L0_attn_bq, L0_attn_Wk, L0_attn_bk, L0_attn_Wv, L0_attn_bv, L0_attn_Wo, L0_attn_bo)
    h = _layernorm(x, axis=-1) * (1 + cb) + sb
    x = x + gb * _L0_ffn_ref(h, L0_ffn_Wg, L0_ffn_bg, L0_ffn_W1, L0_ffn_b1, L0_ffn_W2, L0_ffn_b2)
    return x

_drawn_inputs = setup_inputs


def setup_inputs(seed=0):
    import zlib

    import numpy as np

    out = dict(_drawn_inputs(seed))
    spreads = {'L0_ffn_bg': (0.0, 0.466), 'L0_ffn_b1': (0.0, 0.8), 'L0_ffn_b2': (0.0, 0.8)}
    factors = {'L0_attn_bq': 25.503, 'L0_attn_bk': 64.0, 'L0_attn_bv': 6.748, 'L0_attn_bo': 7.74}
    for name, (base, spread) in spreads.items():
        noise = np.random.default_rng([zlib.crc32(name.encode()), seed]).standard_normal(out[name].shape)
        drawn = base * np.exp(spread * noise) if base else spread * noise
        out[name] = jnp.asarray(drawn.astype(out[name].dtype))
    for name, factor in factors.items():
        out[name] = (out[name] * factor).astype(out[name].dtype)
    return out
```

```python
from contextlib import ExitStack

import concourse.bass as bass
from concourse import mybir

F32 = mybir.dt.float32
F32R = mybir.dt.float32r
BF16 = mybir.dt.bfloat16
I32 = mybir.dt.int32
ACT = mybir.ActivationFunctionType
ALU = mybir.AluOpType
AX_X = mybir.AxisListType.X

P = 128
GS = 4
ROWS = GS * P
HEAD_DIM = 32
SCALE = HEAD_DIM ** -0.5
EPS = 1e-5
GATE_FLOOR = 0.25
NO_TOKEN = 1 << 20
FAR_BELOW = -3.0e38
RT = 17

SA, CA, GA, SB, CB, GB, VC = range(7)


class Group:

    def __init__(self, half, par):
        self.half, self.par, self.n = half, par, half * 2 + par

    def plus(self, k):
        q = self.par + k
        return Group(self.half + q // 2, q % 2)


def build_block(nc, x, wq, bq, wk, bk, wv, bv, wo, bo, wg, bg, w1, b1, w2, b2, cond, wmod, out):
    NBATCH, L, D = x.shape
    T = NBATCH * L
    KC = D // P
    NG = T // ROWS
    GPB = L // ROWS
    NSEG = T // P
    E = wg.shape[1]
    H = w1.shape[2]
    CAP = -(-T // E)
    HB = 512
    NB = H // HB
    HC = HB // P
    assert D == 512 and ROWS == 512 and CAP == ROWS and KC == 4 and HC == 4 and NSEG == 64 and NB % 2 == 0

    x_rows = x.rearrange("b l d -> (b l) d")
    out_rows = out.rearrange("b l d -> (b l) d")

    mod_dram = nc.dram_tensor("mod_rows", (NBATCH, 7, D), F32, kind="Internal").ap()
    qc_dram = nc.dram_tensor("query_consts", (NBATCH, 1), F32, kind="Internal").ap()
    global_dram = nc.dram_tensor("global_rows", (NSEG * 3, D), BF16, kind="Internal").ap()
    h2_dram = nc.dram_tensor("h2_rows", (T, D), F32, kind="Internal").ap()
    table_dram = nc.dram_tensor("slot_table", (E * CAP, 2), I32, kind="Internal").ap()

    KB = 1024
    base = nc.sbuf_base + (-nc.sbuf_base) % 64
    limit = nc.sbuf_usable_end
    sizes = {F32: 4, F32R: 4, BF16: 2, I32: 4}
    cursor = [base]

    def at(name, shape, dt, offset):
        n = sizes[dt]
        for k in shape[1:]:
            n *= k
        assert offset + n <= limit, (name, offset + n - limit)
        return nc.alloc_sbuf_tensor_at(name, shape, dt, offset=offset), offset + n

    def keep(name, shape, dt):
        t, end = at(name, shape, dt, cursor[0])
        cursor[0] = end + (-end) % 32
        return t

    def region(kilobytes):
        start = cursor[0]
        cursor[0] += kilobytes * KB
        assert cursor[0] <= limit
        return start

    def over(start, *tensors):
        made = []
        for name, shape, dt in tensors:
            t, start = at(name, shape, dt, start)
            made.append(t)
        return made

    ident = keep("ident", [P, P], F32)
    tri = keep("tri", [P, P], BF16)
    ones = keep("ones", [P, P], BF16)
    seg_sel = keep("seg_sel", [P, GS, P], BF16)
    grows = [keep(f"grows{i}", [P, D], BF16) for i in range(2)]
    wg_pad = keep("wg_pad", [P, KC, P], F32)
    b1_col = keep("b1_col", [P, E * H // P], F32)
    tokids = keep("tokids", [P, NSEG], I32)
    eidx = keep("eidx", [P, GS, E], F32)
    bg_bc = keep("bg_bc", [P, E], F32)
    mod_col = keep("mod_col", [P, 2, KC, NBATCH], F32)
    u_col = keep("u_col", [P, KC], F32)
    bias_col = keep("bias_col", [P, 3 * KC], F32)
    qc_bc = keep("qc_bc", [P, NBATCH], F32)
    half_neg = keep("half_neg", [P, GS], F32)
    count = keep("count", [P, E], BF16)
    onehot = keep("onehot", [P, GS, E], BF16)
    lg, lg_d, lg_v, lg_e, lg_r = (keep(f"lg{i}", [P, GS, E], F32) for i in range(5))
    osum = keep("osum", [P, E], F32)
    per_tok = keep("per_tok", [P, 24, GS], F32)
    (LG_MX, V_MIN, RANK, OVER, SLOT_A, SLOT_B, LG_SUM, MX, MXC, NEGB, PSUMS, PREC, VE1, MN1, RS1, NR1,
     VE2, MN2, RS2, NR2, QC, QCS, QRAW) = (per_tok[:, i, :] for i in range(23))
    stats = [keep(f"stats{i}", [P, GS, 6], F32) for i in range(2)]
    mv = [keep(f"mv{i}", [P, GS, 2], F32) for i in range(2)]
    slot_i = [keep(f"slot_i{i}", [P, GS], I32) for i in range(2)]
    pay = [keep(f"pay{i}", [P, GS, 2], I32) for i in range(2)]
    bias_rows = keep("bias_rows", [3 * KC, P], F32)
    sc_t = keep("sc_t", [P, KC, NBATCH], F32)
    bk_cols = keep("bk_cols", [P, KC, NBATCH], F32)
    q_const = keep("q_const", [P, 4], F32)
    q_const_g = keep("q_const_g", [NSEG, 1], F32)
    one_row = keep("one_row", [1, NSEG], F32)
    tok_h = keep("tok_h", [P, GS], I32)
    tok_x = keep("tok_x", [P, GS], I32)

    r_m, r_v, r_xa, r_ht, r_split, r_xr = (region(16) for _ in range(6))
    r_gt, r_u, r_h2, r_h2t, r_p = region(8), region(16), region(16), region(8), region(6)
    r_tab, r_raw0 = region(32), region(8)

    full = [P, KC, D]
    m_hi, m_lo = over(r_m, ("m_hi", full, F32R), ("m_lo", full, F32R))
    v_hi, v_lo = over(r_v, ("v_hi", full, F32R), ("v_lo", full, F32R))
    xa = over(r_xa, ("xa0", full, F32), ("xa1", full, F32))
    ht = over(r_ht, ("ht0", full, F32), ("ht1", full, F32))
    ht_hi, ht_lo = over(r_split, ("ht_hi", full, F32R), ("ht_lo", full, F32R))
    xr = over(r_xr, ("xr0", full, F32), ("xr1", full, F32))
    gt, = over(r_gt, ("gt", full, F32))
    u_hi, u_lo = over(r_u, ("u_hi", full, F32R), ("u_lo", full, F32R))
    h2 = over(r_h2, ("h2_0", full, F32), ("h2_1", full, F32))
    h2t, = over(r_h2t, ("h2t", full, F32))
    seg_sq = [P, GS, P]
    prob, pt_hi, pt_lo = over(r_p, ("prob", seg_sq, F32), ("pt_hi", seg_sq, F32R), ("pt_lo", seg_sq, F32R))
    batch_rows = [P, NBATCH, D]
    ga_tab, cb_tab, sb_tab, vc_tab = over(r_tab, *((f"{k}_tab", batch_rows, F32) for k in ("ga", "cb", "sb", "vc")))

    wq_s, wk_s = over(r_xr, ("wq_s", full, F32), ("wk_s", full, F32))
    wv_s, wo_s = over(r_u, ("wv_s", full, F32), ("wo_s", full, F32))
    m_f, = over(r_gt, ("m_f", full, F32))
    wo_t, = over(r_h2t, ("wo_t", full, F32))
    vo_f, = over(r_raw0, ("vo_f", full, F32))
    wm_s = over(r_xa + 8 * KB, ("wm_s0", full, F32)) + over(r_ht + 8 * KB, ("wm_s1", full, F32))
    modr, sc_rows = over(r_h2, ("modr", [NBATCH, 7, D], F32), ("sc_rows", [NBATCH, D], F32))
    g_x, g_a, g_b = over(r_p, ("g_x", [NSEG, D], F32), ("g_a", [NSEG, D], F32), ("g_b", [NSEG, D], F32))
    b1_rows, bo_row, bqk, hg_t = over(r_tab, ("b1_rows", [P, 2, P], F32), ("bo_row", [1, D], F32),
                                      ("bqk", [NBATCH, 2, D], F32), ("hg_t", [P, KC, NSEG], F32))
    g_split, brow, u_row, gg_t = over(r_tab + 8 * KB, ("g_split", [NSEG, 3, D], BF16), ("brow", [1, D], F32),
                                      ("u_row", [1, D], F32), ("gg_t", [P, KC, NSEG], F32))

    sg, pg, pg_t, table_init = over(r_tab + 16 * KB, ("sg", [NSEG, NSEG], F32), ("pg", [NSEG, P], F32),
                                    ("pg_t", [NSEG, NSEG], F32), ("table_init", [P, E * CAP // P, 2], I32))
    sc_tmp, = over(r_raw0, ("sc_tmp", [NBATCH, D], F32))
    g_c, = over(r_split, ("g_c", [NSEG, D], F32))
    qc_junk = prob[:].rearrange("p s t -> p (s t)")
    QCS2 = [QC, QCS]

    raw = over(r_raw0, ("raw0", full, F32)) + over(r_xa, ("raw1", full, F32), ("raw2", full, F32)) \
        + over(r_ht, ("raw3", full, F32))
    w1_hi, w1_lo, w2_hi, w2_lo = [None] * 2, [None] * 2, [None] * 2, [None] * 2
    w1_hi[0], w1_lo[0] = over(r_m, ("w1_hi0", full, F32R), ("w1_lo0", full, F32R))
    w1_hi[1], w1_lo[1] = over(r_v, ("w1_hi1", full, F32R), ("w1_lo1", full, F32R))
    w2_hi[0], w2_lo[0] = over(r_split, ("w2_hi0", full, F32R), ("w2_lo0", full, F32R))
    w2_hi[1], w2_lo[1] = over(r_xr, ("w2_hi1", full, F32R), ("w2_lo1", full, F32R))
    h1_f, = over(r_ht + 8 * KB, ("h1_f", full, F32))
    xh, = over(r_gt, ("xh", full, F32))
    bt_hi, bt_lo = over(r_u, ("bt_hi", full, F32R), ("bt_lo", full, F32R))
    h1_hi, h1_lo = [None] * 2, [None] * 2
    h1_hi[0], h1_lo[0] = over(r_h2, ("h1_hi0", full, F32R), ("h1_lo0", full, F32R))
    xo, = over(r_h2t, ("xo", full, F32))
    gb_mix0, gb_mix1, b2_bc = over(r_p, ("gb_mix0", [P, D], F32), ("gb_mix1", [P, D], F32), ("b2_bc", [P, D], F32))
    gb_mix = [gb_mix0, gb_mix1]
    h1_hi[1], h1_lo[1], gb_tab, yo0, yo1, table, tok_f, coef, coef_t = over(
        r_tab, ("h1_hi1", full, F32R), ("h1_lo1", full, F32R), ("gb_tab", batch_rows, F32),
        ("yo0", [P, D], F32), ("yo1", [P, D], F32),
        ("table", [P, E, GS, 2], I32), ("tok_f", [P, E * GS], F32),
        ("coef", [P, NBATCH, E * GS], F32), ("coef_t", [P, 2, E * GS], F32))
    yo = [yo0, yo1]

    stack = ExitStack()
    banks = [stack.enter_context(nc.psum_tensor(f"bank{i}", [P, 512], F32)) for i in range(8)]
    big, (s_bank, pt_bank, lg_bank, pos_bank) = banks[:4], banks[4:]
    y_bank, h_bank = banks[:4], banks[4:]

    def sem(name):
        return stack.enter_context(nc.semaphore(name))

    made = sem("made")
    ident_made = sem("ident_made")
    init_made = sem("init_made")
    cond_in, bias_in, wq_in, wk_in, wv_in, wo_in, summ_in = (sem(f"{k}_in") for k in (
        "cond", "bias", "wq", "wk", "wv", "wo", "summ"))
    wm_in = [sem(f"wm_in{i}") for i in range(2)]
    wg_in, bg_in, bo_in, bqk_in, b1_in = (sem(f"{k}_in") for k in ("wg", "bg", "bo", "bqk", "b1"))
    pro_full, pro_evac = sem("pro_full"), sem("pro_evac")
    sc_step, sc_exp, sc_ready = sem("sc_step"), sem("sc_exp"), sem("sc_ready")
    m_step, v_step, m_split, v_split = sem("m_step"), sem("v_step"), sem("m_split"), sem("v_split")
    fix_step, mod_fixed, mod_stored = sem("fix_step"), sem("mod_fixed"), sem("mod_stored")
    brow_ready = sem("brow_ready")
    vcg_in, qcg_in = sem("vcg_in"), sem("qcg_in")
    tab_in, qc_in, late_tab_in = sem("tab_in"), sem("qc_in"), sem("late_tab_in")
    gsum_stats, gsum_rstd, gsum_xn, gsum_step = (sem(f"gsum_{k}") for k in ("stats", "rstd", "xn", "step"))
    gsum_masked, gsum_negb, gsum_exp, gsum_prob = (sem(f"gsum_{k}") for k in ("masked", "negb", "exp", "prob"))
    g_split_done, g_stored, table_cleared = sem("g_split_done"), sem("g_stored"), sem("table_cleared")

    x_in = [sem(f"x_in{i}") for i in range(2)]
    xr_in = [sem(f"xr_in{i}") for i in range(2)]
    grows_in = [sem(f"grows_in{i}") for i in range(2)]
    ln1_step, ln1_ready, ln1_rstd, xn_done = (sem(k) for k in ("ln1_step", "ln1_ready", "ln1_rstd", "xn_done"))
    t1_full, ht_full, ht_hi_done, ht_split, qc_raw, qc_ready = (sem(k) for k in (
        "t1_full", "ht_full", "ht_hi_done", "ht_split", "qc_raw", "qc_ready"))
    gt_full, gt_done, u_full, u_hi_done, u_split = (sem(k) for k in (
        "gt_full", "gt_done", "u_full", "u_hi_done", "u_split"))
    s_full, mx_step, negb_ready, exp_done, prec_ready, prob_ready = (sem(k) for k in (
        "s_full", "mx_step", "negb_ready", "exp_done", "prec_ready", "prob_ready"))
    pt_full, pt_hi_done, pt_split, av_full, av_taken = (sem(k) for k in (
        "pt_full", "pt_hi_done", "pt_split", "av_full", "av_taken"))
    x2_ready, ln2_step, ln2_ready, ln2_rstd, xn2_done, h2_scaled, h2_ready = (sem(k) for k in (
        "x2_ready", "ln2_step", "ln2_ready", "ln2_rstd", "xn2_done", "h2_scaled", "h2_ready"))
    x2_stored = [sem(f"x2_stored{i}") for i in range(2)]
    h2_stored = [sem(f"h2_stored{i}") for i in range(2)]
    h2t_full, h2t_done, lg_full, route, route_exp, pos_full = (sem(k) for k in (
        "h2t_full", "h2t_done", "lg_full", "route", "route_exp", "pos_full"))
    scattered = [sem(f"scattered{i}") for i in range(2)]

    table_in, gb_in, coef_step, coef_ready, tok_h_ready, tok_x_ready = (sem(k) for k in (
        "table_in", "gb_in", "coef_step", "coef_ready", "tok_h_ready", "tok_x_ready"))
    w1_in = [sem(f"w1_in{i}") for i in range(2)]
    w2_in = [sem(f"w2_in{i}") for i in range(2)]
    w1_hi_done, w1_split, w2_hi_done, w2_split = (sem(k) for k in (
        "w1_hi_done", "w1_split", "w2_hi_done", "w2_split"))
    xh_cleared, xh_in, xo_in, b2_in = sem("xh_cleared"), sem("xh_in"), sem("xo_in"), sem("b2_in")
    bt_full, bt_hi_done, bt_split = sem("bt_full"), sem("bt_hi_done"), sem("bt_split")
    h1_full, relu_done, h1_hi_done, h1_split, g2_done = (sem(k) for k in (
        "h1_full", "relu_done", "h1_hi_done", "h1_split", "g2_done"))
    y_full, y_taken, mix_step, mixed, y_scaled, y_ready = (sem(k) for k in (
        "y_full", "y_taken", "mix_step", "mixed", "y_scaled", "y_ready"))
    y_sent = [sem(f"y_sent{i}") for i in range(2)]

    sp_passed, dve_passed, pool_passed = sem("sp_passed"), sem("dve_passed"), sem("pool_passed")

    def wait_past(eng, s, n):
        if not isinstance(n, int) or n > 0:
            eng.wait_ge(s, n)

    def stand_alone(eng, passed):
        eng.sem_inc(passed, 1)

    def chunk(k):
        return slice(k * P, (k + 1) * P)

    def batch_of(g):
        return g.n // GPB

    def split3(pe, o, a_hi, a_lo, b_hi, b_lo, start, stop):
        pe.matmul(o, a_hi, b_hi, start=start, stop=False)
        pe.matmul(o, a_hi, b_lo, start=False, stop=False)
        return pe.matmul(o, a_lo, b_hi, start=False, stop=stop)

    (SCT, BCOL, MCH, UROW, V4, UCOL, MODS, MCOL, WOT, VCH, BROW, HGT, GROW, GGT, SG, UG, PGT, TG, B1T,
     PRO_END) = (0, 1, 2, 6, 7, 8, 9, 15, 16, 20, 24, 25, 26, 27, 28, 29, 30, 31, 32, 33)
    POOL_MADE = 8
    DVE_MADE = 9

    def results_done(eng, e, b):
        if b == 0:
            wait_past(eng, g2_done, (NB - 1) * e)
        elif b == 1:
            wait_past(eng, y_full, GS * e)
        else:
            eng.wait_ge(g2_done, (NB - 1) * e + b - 1)

    block = stack.enter_context(nc.Block())

    @block.sync
    def _(sp):
        def w_rows(w):
            return w.rearrange("(c p) n -> p c n", p=P)

        def group_rows(rows, g):
            return rows[bass.ds(g.n * ROWS, ROWS), :].rearrange("(s p) d -> p s d", p=P)

        def load_x(g):
            sp.dma_start(xa[g.par][:], group_rows(x_rows, g)).then_inc(x_in[g.par], 16)

        sp.dma_start(sc_rows[:], cond).then_inc(cond_in, 16)
        for i, b in enumerate((bq, bk, bv)):
            sp.dma_start(bias_rows[KC * i:KC * (i + 1), :], b.rearrange("(c p) -> c p", p=P)).then_inc(bias_in, 16)
        sp.dma_start(wk_s[:], w_rows(wk)).then_inc(wk_in, 16)
        sp.dma_start(wq_s[:], w_rows(wq)).then_inc(wq_in, 16)
        load_x(Group(0, 0))

        def load_wmod(m):
            if m >= 2:
                sp.wait_ge(pro_full, MODS + m - 1)
            sp.dma_start(wm_s[m % 2][:], wmod[:, m * D:(m + 1) * D].rearrange("(c p) n -> p c n", p=P)) \
                .then_inc(wm_in[m % 2], 16)

        load_wmod(0)
        load_wmod(1)
        for i, b in enumerate((bq, bk)):
            sp.dma_start(bqk[:, i, :], b.rearrange("(a d) -> a d", a=1).to_broadcast([NBATCH, D])).then_inc(bqk_in, 16)
        sp.dma_start(wo_s[:], w_rows(wo)).then_inc(wo_in, 16)
        sp.dma_start(wv_s[:], w_rows(wv)).then_inc(wv_in, 16)
        sp.dma_start(g_x[:], x_rows.rearrange("(n p) d -> n p d", p=P)[:, 0, :]).then_inc(summ_in, 16)
        sp.dma_start(bo_row[:], bo.rearrange("(a d) -> a d", a=1)).then_inc(bo_in, 16)
        sp.dma_start(bg_bc[:], bg.rearrange("(a d) -> a d", a=1).to_broadcast([P, E])).then_inc(bg_in, 16)
        sp.dma_start(b1_rows[:], b1.rearrange("e (c p) -> (e c) p", p=P).rearrange("(t r) p -> r t p", r=P)) \
            .then_inc(b1_in, 16)
        sp.wait_ge(init_made, 6)
        sp.dma_start(wg_pad[:, :, 0:E], wg.rearrange("(c p) e -> p c e", p=P)).then_inc(wg_in, 16)
        sp.dma_start(table_dram.rearrange("(p a) c -> p a c", p=P), table_init[:]).then_inc(table_cleared, 16)
        for m in range(2, 6):
            load_wmod(m)
        sp.wait_ge(mod_fixed, 1)
        sp.dma_start(mod_dram, modr[:]).then_inc(mod_stored, 16)
        sp.dma_start(qc_dram, q_const[0:NBATCH, 0:1]).then_inc(mod_stored, 16)
        sp.wait_ge(mod_stored, 32)

        def spread(row, n):
            return mod_dram[:, row, :].unsqueeze(0).to_broadcast([n, NBATCH, D])

        for b in range(NBATCH):
            seg = slice(b * (NSEG // NBATCH), (b + 1) * (NSEG // NBATCH))
            sp.dma_start(g_b[seg, :], mod_dram[b:b + 1, VC, :].to_broadcast([NSEG // NBATCH, D])).then_inc(vcg_in, 16)
            sp.dma_start(q_const_g[seg, :], qc_dram[b:b + 1, :].to_broadcast([NSEG // NBATCH, 1])).then_inc(qcg_in, 16)
        sp.dma_start(vc_tab[:], spread(VC, P)).then_inc(tab_in, 16)
        sp.dma_start(qc_bc[:], qc_dram.rearrange("b a -> a b").to_broadcast([P, NBATCH])).then_inc(qc_in, 16)
        sp.wait_ge(g_split_done, 1)
        sp.dma_start(global_dram.rearrange("(n t) d -> n t d", t=3), g_split[:]).then_inc(g_stored, 16)
        sp.wait_ge(pro_evac, PRO_END)
        load_x(Group(0, 1))
        sp.dma_start(ga_tab[:], spread(GA, P)).then_inc(late_tab_in, 16)
        sp.wait_ge(g_stored, 16)
        sp.dma_start(cb_tab[:], spread(CB, P)).then_inc(late_tab_in, 16)
        sp.wait_ge(table_cleared, 16)
        sp.dma_start(sb_tab[:], spread(SB, P)).then_inc(late_tab_in, 16)

        def iteration(i, cur, prev, load2):
            if load2:
                sp.wait_ge(t1_full, 4 * i.n + 4)
                sp.wait_ge(qc_raw, 4 * i.n + 4)
                load_x(i.plus(2))
            if cur:
                wait_past(sp, av_full, 4 * i.n - 4)
                sp.dma_start(grows[i.par][0:3 * GS, :], global_dram[bass.ds(i.n * 3 * GS, 3 * GS), :]) \
                    .then_inc(grows_in[i.par], 16)
                if not isinstance(i.n, int) or i.n >= 2:
                    sp.wait_ge(xn2_done, 4 * i.n - 4)
                    stand_alone(sp, sp_passed)
                    sp.wait_ge(x2_stored[i.par], 16 * i.half)
                sp.dma_start(xr[i.par][:], group_rows(x_rows, i)).then_inc(xr_in[i.par], 16)
            if prev:
                g = i.plus(-1)
                sp.wait_ge(x2_ready, 4 * g.n + 4)
                sp.dma_start(group_rows(out_rows, g), xr[g.par][:]).then_inc(x2_stored[g.par], 16)
                sp.wait_ge(h2_ready, 4 * g.n + 4)
                sp.dma_start(group_rows(h2_dram, g), h2[g.par][:]).then_inc(h2_stored[g.par], 16)

        iteration(Group(0, 0), True, False, True)
        iteration(Group(0, 1), True, True, True)
        with sp.Fori(1, NG // 2 - 1) as half:
            for par in range(2):
                iteration(Group(half, par), True, True, True)
        for n in range(NG - 2, NG):
            iteration(Group(n // 2, n % 2), True, True, False)
        iteration(Group(NG // 2, 0), False, True, False)

        def load_w1(n, par):
            sp.dma_start(raw[2 * par][:], w1_block(n)).then_inc(w1_in[par], 16)

        def load_w2(n, par):
            sp.dma_start(raw[2 * par + 1][:], w2_block(n)).then_inc(w2_in[par], 16)

        w1_flat = w1.rearrange("e d h -> (e d) h")
        w2_flat = w2.rearrange("e h d -> (e h) d")

        def w1_block(n):
            e, b = n
            return w1_flat[bass.ds(e * D, D), b * HB:(b + 1) * HB].rearrange("(c p) h -> p c h", p=P)

        def w2_block(n):
            e, b = n
            return w2_flat[bass.ds(e * H + b * HB, HB), :].rearrange("(c p) d -> p c d", p=P)

        sp.wait_ge(s_full, NG)
        sp.wait_ge(qc_raw, 4 * NG)
        load_w1((0, 0), 0)
        load_w2((0, 0), 0)
        load_w1((0, 1), 1)
        load_w2((0, 1), 1)
        sp.wait_ge(h2_ready, 4 * NG)
        for par in range(2):
            sp.wait_ge(scattered[par], 16 * GS * (NG // 2))
        sp.dma_start(table[:], table_dram.rearrange("(e p j) c -> p e j c", p=P, j=GS)).then_inc(table_in, 16)
        sp.dma_start(gb_tab[:], spread(GB, P)).then_inc(gb_in, 16)
        sp.dma_start(b2_bc[:], b2[0:1, :].to_broadcast([P, D])).then_inc(b2_in, 16)

        def expert(e, first, last):
            for b in range(NB):
                n = e * NB + b
                ahead = (e, b + 2) if b + 2 < NB else (e + 1, b + 2 - NB)
                if not (last and b + 2 >= NB):
                    sp.wait_ge(w1_split, n + 1)
                    load_w1(ahead, b % 2)
                    sp.wait_ge(w2_split, n + 1)
                    load_w2(ahead, b % 2)
                if b == 1 and not first:
                    sp.wait_ge(y_taken, 4 * e)
                    stand_alone(sp, sp_passed)
                    sp.dma_start(b2_bc[:], b2[bass.ds(e, 1), :].to_broadcast([P, D])).then_inc(b2_in, 16)

        expert(0, True, False)
        with sp.Fori(1, E - 1) as e:
            expert(e, False, False)
        expert(E - 1, False, True)
        for par in range(2):
            sp.wait_ge(x2_stored[par], 16 * (NG // 2))
            sp.wait_ge(y_sent[par], 16 * 2 * E)

    @block.tensor
    def _(pe):
        def product(q, last):
            last.then_inc(pro_full, 1)

        def bank_free(q):
            wait_past(pe, pro_evac, q - 7)

        pe.wait_ge(ident_made, 2)
        pe.wait_ge(sc_ready, 1)
        for k in range(KC):
            last = pe.transpose(banks[SCT % 8][:, k * NBATCH:(k + 1) * NBATCH], sc_rows[:, chunk(k)],
                                ident[0:NBATCH, 0:NBATCH])
        product(SCT, last)
        pe.wait_ge(bias_in, 48)
        product(BCOL, pe.transpose(banks[BCOL % 8][:, 0:3 * KC], bias_rows[:], ident[0:3 * KC, 0:3 * KC]))
        pe.wait_ge(wk_in, 16)
        pe.wait_ge(wq_in, 16)
        for c in range(KC):
            for k in range(KC):
                last = pe.matmul(banks[(MCH + c) % 8][:, :], wq_s[:, k, chunk(c)], wk_s[:, k, :],
                                 start=(k == 0), stop=(k == KC - 1))
            product(MCH + c, last)
        pe.wait_ge(pro_evac, BCOL + 1)
        for k in range(KC):
            last = pe.matmul(banks[UROW % 8][0:1, :], bias_col[:, k:k + 1], wk_s[:, k, :],
                             start=(k == 0), stop=(k == KC - 1))
        product(UROW, last)
        for k in range(KC):
            last = pe.matmul(banks[V4 % 8][0:NBATCH, :], bk_cols[:, k, :], wq_s[:, k, :],
                             start=(k == 0), stop=(k == KC - 1))
        product(V4, last)
        pe.wait_ge(pro_evac, UROW + 1)
        bank_free(UCOL)
        for k in range(KC):
            last = pe.transpose(banks[UCOL % 8][:, k:k + 1], u_row[:, chunk(k)], ident[0:1, 0:1])
        product(UCOL, last)
        for m in range(6):
            bank_free(MODS + m)
            pe.wait_ge(wm_in[m % 2], 16 * (m // 2 + 1))
            for k in range(KC):
                last = pe.matmul(banks[(MODS + m) % 8][0:NBATCH, :], sc_t[:, k, :], wm_s[m % 2][:, k, :],
                                 start=(k == 0), stop=(k == KC - 1))
            product(MODS + m, last)
        pe.wait_ge(mod_fixed, 1)
        bank_free(MCOL)
        for i, row in enumerate((SA, CA)):
            for k in range(KC):
                at_col = (i * KC + k) * NBATCH
                last = pe.transpose(banks[MCOL % 8][:, at_col:at_col + NBATCH], modr[:, row, chunk(k)],
                                    ident[0:NBATCH, 0:NBATCH])
        product(MCOL, last)
        pe.wait_ge(wo_in, 16)
        for c in range(KC):
            bank_free(WOT + c)
            for k in range(KC):
                last = pe.transpose(banks[(WOT + c) % 8][:, chunk(k)], wo_s[:, k, chunk(c)], ident[:])
            product(WOT + c, last)
        pe.wait_ge(wv_in, 16)
        pe.wait_ge(pro_evac, WOT + KC)
        for c in range(KC):
            bank_free(VCH + c)
            for k in range(KC):
                last = pe.matmul(banks[(VCH + c) % 8][:, :], wv_s[:, k, chunk(c)], wo_t[:, k, :],
                                 start=(k == 0), stop=(k == KC - 1))
            product(VCH + c, last)

        def transpose_xn(g, first):
            pe.wait_ge(xn_done, 4 * g.n + 4)
            for k in range(KC):
                if not first:
                    pe.wait_ge(u_split, 4 * g.n - 4 + k + 1)
                for s in range(GS):
                    last = pe.transpose(big[k][:, chunk(s)], xa[g.par][:, s, chunk(k)], ident[:])
                last.then_inc(t1_full, 1)

        pe.wait_ge(pro_evac, WOT + KC)
        transpose_xn(Group(0, 0), True)
        pe.wait_ge(ht_full, KC)
        for k in range(KC):
            last = pe.matmul(banks[BROW % 8][0:1, :], bias_col[:, 2 * KC + k:2 * KC + k + 1], wo_t[:, k, :],
                             start=(k == 0), stop=(k == KC - 1))
        product(BROW, last)
        pe.wait_ge(gsum_xn, 1)
        bank_free(HGT)
        for k in range(KC):
            last = pe.transpose(banks[HGT % 8][:, k * NSEG:(k + 1) * NSEG], g_a[:, chunk(k)], ident[0:NSEG, 0:NSEG])
        product(HGT, last)
        pe.wait_ge(pro_evac, HGT + 1)
        for k in range(KC):
            last = pe.matmul(banks[GROW % 8][0:NSEG, :], hg_t[:, k, :], m_f[:, k, :],
                             start=(k == 0), stop=(k == KC - 1))
        product(GROW, last)
        pe.wait_ge(pro_evac, GROW + 1)
        for k in range(KC):
            last = pe.transpose(banks[GGT % 8][:, k * NSEG:(k + 1) * NSEG], g_x[:, chunk(k)], ident[0:NSEG, 0:NSEG])
        product(GGT, last)
        pe.wait_ge(pro_evac, GGT + 1)
        for k in range(KC):
            last = pe.matmul(banks[SG % 8][0:NSEG, 0:NSEG], gg_t[:, k, :], hg_t[:, k, :],
                             start=(k == 0), stop=(k == KC - 1))
        product(SG, last)
        for k in range(KC):
            last = pe.matmul(banks[UG % 8][0:NSEG, :], hg_t[:, k, :], vo_f[:, k, :],
                             start=(k == 0), stop=(k == KC - 1))
        product(UG, last)
        pe.wait_ge(gsum_prob, 1)
        product(PGT, pe.transpose(banks[PGT % 8][:, 0:NSEG], pg[:], ident[0:NSEG, 0:NSEG]))
        pe.wait_ge(pro_evac, PGT + 1)
        pe.wait_ge(brow_ready, 1)
        pe.matmul(banks[TG % 8][0:NSEG, :], pg_t[:], g_b[:], start=True, stop=False)
        product(TG, pe.matmul(banks[TG % 8][0:NSEG, :], one_row[:], brow[:], start=False, stop=True))
        pe.wait_ge(b1_in, 16)
        for t in range(2):
            last = pe.transpose(banks[B1T % 8][:, chunk(t)], b1_rows[:, t, :], ident[:])
        product(B1T, last)
        pe.wait_ge(pro_evac, PRO_END)
        pe.wait_ge(m_split, KC)
        pe.wait_ge(v_split, KC)
        pe.wait_ge(wg_in, 16)
        pe.wait_ge(made, POOL_MADE)

        def g_tile(g, j):
            for k in range(KC):
                last = split3(pe, big[j][:, :], m_hi[:, k, chunk(j)], m_lo[:, k, chunk(j)], ht_hi[:, k, :],
                              ht_lo[:, k, :], k == 0, k == KC - 1)
            last.then_inc(gt_full, 1)

        def iteration(i, cur, prev, prev2, nxt):
            n = i.n
            p1, p2 = i.plus(-1), i.plus(-2)
            if cur:
                pe.wait_ge(ht_split, 4 * n + 4)
                g_tile(i, 0)
                g_tile(i, 1)
            if prev2:
                pe.wait_ge(h2_ready, 4 * p2.n + 4)
                if not cur:
                    pe.wait_ge(u_split, 4 * NG)
                for k in range(KC):
                    if cur and k >= 2:
                        pe.wait_ge(gt_done, 4 * n + k - 1)
                    for s in range(GS):
                        last = pe.transpose(big[(k + 2) % 4][:, chunk(s)], h2[p2.par][:, s, chunk(k)], ident[:])
                    last.then_inc(h2t_full, 1)
            if cur:
                if prev2:
                    pe.wait_ge(h2t_done, 4 * p2.n + 1)
                g_tile(i, 2)
            if prev:
                pe.wait_ge(prob_ready, p1.n + 1)
                for s in range(GS):
                    last = pe.transpose(pt_bank[:, chunk(s)], prob[:, s, :], ident[:])
                last.then_inc(pt_full, 1)
            if cur:
                if prev2:
                    pe.wait_ge(h2t_done, 4 * p2.n + 2)
                g_tile(i, 3)
            if prev:
                pe.wait_ge(u_split, 4 * p1.n + 4)
                pe.wait_ge(pt_split, p1.n + 1)
                pe.wait_ge(grows_in[p1.par], 16 * (p1.half + 1))
                if prev2:
                    pe.wait_ge(h2t_done, 4 * p2.n + 4)
                for s in range(GS):
                    if cur:
                        pe.wait_ge(gt_done, 4 * n + s + 1)
                    split3(pe, big[s][:, :], pt_hi[:, s, :], pt_lo[:, s, :], u_hi[:, s, :], u_lo[:, s, :], True, False)
                    pe.matmul(big[s][:, :], seg_sel[:, s, :], grows[p1.par][:], start=False, stop=True) \
                        .then_inc(av_full, 1)
            if cur:
                for s in range(GS):
                    if prev:
                        pe.wait_ge(av_taken, 4 * p1.n + s + 1)
                    else:
                        pe.wait_ge(gt_done, 4 * n + s + 1)
                    for k in range(KC):
                        last = split3(pe, big[s][:, :], ht_hi[:, k, chunk(s)], ht_lo[:, k, chunk(s)], v_hi[:, k, :],
                                      v_lo[:, k, :], k == 0, k == KC - 1)
                    last.then_inc(u_full, 1)
            if nxt:
                transpose_xn(i.plus(1), False)
            if prev2:
                pe.wait_ge(h2t_done, 4 * p2.n + 4)
                wait_past(pe, route, RT * p2.n - RT + 1)
                for s in range(GS):
                    for k in range(KC):
                        last = pe.matmul(lg_bank[:, chunk(s)], h2t[:, k, chunk(s)], wg_pad[:, k, :],
                                         start=(k == 0), stop=(k == KC - 1))
                last.then_inc(lg_full, 1)
            if cur:
                pe.wait_ge(gt_done, 4 * n + 4)
                for s in range(GS):
                    for k in range(KC):
                        last = pe.matmul(s_bank[:, chunk(s)], gt[:, k, chunk(s)], ht[i.par][:, k, chunk(s)],
                                         start=(k == 0), stop=(k == KC - 1))
                last.then_inc(s_full, 1)
            if prev2:
                pe.wait_ge(route, RT * p2.n + 6)
                flat = onehot[:].rearrange("p s e -> p (s e)")
                pe.matmul(pos_bank[:, 0:GS * E], tri[:], flat, start=True, stop=False)
                pe.matmul(pos_bank[:, 0:GS * E].rearrange("p (s e) -> p s e", e=E), ones[:],
                          count[:].unsqueeze(1).to_broadcast([P, GS, E]), start=False, stop=False)
                for s in range(GS - 1):
                    last = pe.matmul(pos_bank[:, (s + 1) * E:GS * E].rearrange("p (s e) -> p s e", e=E), ones[:],
                                     onehot[:, s:s + 1, :].to_broadcast([P, GS - 1 - s, E]),
                                     start=False, stop=(s == GS - 2))
                last.then_inc(pos_full, 1)

        iteration(Group(0, 0), True, False, False, True)
        iteration(Group(0, 1), True, True, False, True)
        iteration(Group(1, 0), True, True, True, True)
        iteration(Group(1, 1), True, True, True, True)
        with pe.Fori(2, NG // 2 - 1) as half:
            for par in range(2):
                iteration(Group(half, par), True, True, True, True)
        iteration(Group(NG // 2 - 1, 0), True, True, True, True)
        iteration(Group(NG // 2 - 1, 1), True, True, True, False)
        iteration(Group(NG // 2, 0), False, True, True, False)
        iteration(Group(NG // 2, 1), False, False, True, False)

        def gathered_transpose(e):
            pe.wait_ge(xh_in, 16 * GS * (e + 1))
            wait_past(pe, relu_done, 4 * NB * e)
            for k in range(KC):
                for j in range(GS):
                    last = pe.transpose(h_bank[k][:, chunk(j)], xh[:, j, chunk(k)], ident[:])
                last.then_inc(bt_full, 1)

        def hidden(e, b):
            n = NB * e + b
            if b == 0:
                pe.wait_ge(bt_split, 4 * e + 4)
            pe.wait_ge(w1_split, n + 1)
            for j in range(HC):
                if b > 0:
                    pe.wait_ge(relu_done, 4 * n + j - 3)
                for k in range(KC):
                    last = split3(pe, h_bank[j][:, :], w1_hi[b % 2][:, k, chunk(j)], w1_lo[b % 2][:, k, chunk(j)],
                                  bt_hi[:, k, :], bt_lo[:, k, :], k == 0, k == KC - 1)
                last.then_inc(h1_full, 1)

        def results(e, b):
            n = NB * e + b
            pe.wait_ge(h1_split, 4 * n + 4)
            pe.wait_ge(w2_split, n + 1)
            if b == 0:
                wait_past(pe, y_taken, 4 * e)
            for j in range(GS):
                for c in range(HC):
                    last = split3(pe, y_bank[j][:, :], h1_hi[b % 2][:, c, chunk(j)], h1_lo[b % 2][:, c, chunk(j)],
                                  w2_hi[b % 2][:, c, :], w2_lo[b % 2][:, c, :], b == 0 and c == 0,
                                  b == NB - 1 and c == HC - 1)
                if b == NB - 1:
                    last.then_inc(y_full, 1)
            if b < NB - 1:
                last.then_inc(g2_done, 1)

        def expert(e, first, last):
            for b in range(NB):
                hidden(e, b)
                if b == NB - 1 and not last:
                    gathered_transpose(e + 1)
                if b > 0:
                    results(e, b - 1)
                elif not first:
                    results(e - 1, NB - 1)

        pe.wait_ge(pos_full, NG)
        pe.wait_ge(route, RT * NG)
        gathered_transpose(0)
        expert(0, True, False)
        with pe.Fori(1, E - 1) as e:
            expert(e, False, False)
        expert(E - 1, False, True)
        results(E - 1, NB - 1)

    @block.scalar
    def _(act):
        def copy_out(q, dst, src, scale=1.0):
            act.wait_ge(pro_full, q + 1)
            act.activation(dst, src, ACT.Copy, scale=scale).then_inc(pro_evac, 1)

        act.wait_ge(cond_in, 16)
        act.activation(sc_tmp[:], sc_rows[:], ACT.Exp, scale=-1.0).then_inc(sc_exp, 1)
        copy_out(SCT, sc_t[:].rearrange("p k b -> p (k b)"), banks[SCT % 8][:, 0:KC * NBATCH])
        act.wait_ge(pro_full, BCOL + 1)
        act.activation(bias_col[:], banks[BCOL % 8][:, 0:3 * KC], ACT.Copy)
        act.activation(bk_cols[:], banks[BCOL % 8][:, KC:2 * KC].unsqueeze(2).to_broadcast([P, KC, NBATCH]),
                       ACT.Copy).then_inc(pro_evac, 1)
        for c in range(KC):
            copy_out(MCH + c, m_f[:, c, :], banks[(MCH + c) % 8][:, :])
        copy_out(UROW, u_row[:], banks[UROW % 8][0:1, :])
        copy_out(V4, modr[:, VC, :], banks[V4 % 8][0:NBATCH, :])
        copy_out(UCOL, u_col[:], banks[UCOL % 8][:, 0:KC])
        for m in range(6):
            copy_out(MODS + m, modr[:, m, :], banks[(MODS + m) % 8][0:NBATCH, :])
        copy_out(MCOL, mod_col[:].rearrange("p i k b -> p (i k b)"), banks[MCOL % 8][:, 0:2 * KC * NBATCH])
        for c in range(KC):
            copy_out(WOT + c, wo_t[:, c, :], banks[(WOT + c) % 8][:, :])
        act.wait_ge(gsum_rstd, 2)
        act.activation(g_a[:], g_x[:], ACT.Identity, bias=NR2[0:NSEG, 0:1], scale=RS2[0:NSEG, 0:1]).then_inc(gsum_xn, 1)
        for c in range(KC):
            copy_out(VCH + c, vo_f[:, c, :], banks[(VCH + c) % 8][:, :])

        def modulate(g):
            for k in range(KC):
                act.wait_ge(t1_full, 4 * g.n + k + 1)
                act.wait_ge(pro_evac, MCOL + 1)
                act.activation(ht[g.par][:, k, :], big[k][:, :], ACT.Identity,
                               bias=mod_col[:, 0, k, bass.ds(batch_of(g), 1)],
                               scale=mod_col[:, 1, k, bass.ds(batch_of(g), 1)]).then_inc(ht_full, 1)

        modulate(Group(0, 0))
        copy_out(BROW, brow[:], banks[BROW % 8][0:1, :], scale=2.0)
        act.wait_ge(pro_full, HGT + 1)
        for k in range(KC):
            for b in range(NBATCH):
                seg = slice(b * (NSEG // NBATCH), (b + 1) * (NSEG // NBATCH))
                ins = act.activation(hg_t[:, k, seg], banks[HGT % 8][:, k * NSEG + seg.start:k * NSEG + seg.stop],
                                     ACT.Identity, bias=mod_col[:, 0, k, b:b + 1], scale=mod_col[:, 1, k, b:b + 1])
        ins.then_inc(pro_evac, 1)
        copy_out(GROW, g_x[:], banks[GROW % 8][0:NSEG, :])
        act.wait_ge(pro_full, GGT + 1)
        for k in range(KC):
            ins = act.activation(gg_t[:, k, :], banks[GGT % 8][:, k * NSEG:(k + 1) * NSEG], ACT.Identity,
                                 bias=u_col[:, k:k + 1])
        ins.then_inc(pro_evac, 1)
        copy_out(SG, sg[:], banks[SG % 8][0:NSEG, 0:NSEG])
        act.wait_ge(gsum_step, 4)
        copy_out(UG, g_b[:], banks[UG % 8][0:NSEG, :])
        act.wait_ge(gsum_negb, 1)
        act.activation(pg[:, 0:NSEG], sg[:], ACT.Exp, bias=NEGB[0:NSEG, 0:1], scale=SCALE,
                       accum_out=PSUMS[0:NSEG, 0:1]).then_inc(gsum_exp, 1)
        copy_out(PGT, pg_t[:], banks[PGT % 8][0:NSEG, 0:NSEG])
        copy_out(TG, g_a[:], banks[TG % 8][0:NSEG, :])
        copy_out(B1T, b1_col[:], banks[B1T % 8][:, 0:2 * P])

        def iteration(i, cur, prev, prev2, nxt):
            n = i.n
            p1, p2 = i.plus(-1), i.plus(-2)

            def add_u(j):
                act.wait_ge(gt_full, 4 * n + j + 1)
                act.activation(gt[:, j, :], big[j][:, :], ACT.Identity, bias=u_col[:, j:j + 1]).then_inc(gt_done, 1)

            def empty_u(s):
                act.wait_ge(u_full, 4 * n + s + 1)
                act.activation(u_hi[:, s, :], big[s][:, :], ACT.Copy).then_inc(u_hi_done, 1)

            def normalise2(s):
                act.activation(h2[p1.par][:, s, :], xr[p1.par][:, s, :], ACT.Identity, bias=NR2[:, s:s + 1],
                               scale=RS2[:, s:s + 1]).then_inc(xn2_done, 1)

            if prev:
                act.wait_ge(negb_ready, p1.n + 1)
                for s in range(GS):
                    act.activation(prob[:, s, :], s_bank[:, chunk(s)], ACT.Exp, bias=NEGB[:, s:s + 1], scale=SCALE,
                                   accum_out=PSUMS[:, s:s + 1]).then_inc(exp_done, 1)
            if cur:
                add_u(0)
                add_u(1)
            if prev2:
                for k in range(KC):
                    act.wait_ge(h2t_full, 4 * p2.n + k + 1)
                    act.activation(h2t[:, k, :], big[(k + 2) % 4][:, :], ACT.Copy).then_inc(h2t_done, 1)
            if cur:
                add_u(2)
            if prev:
                act.wait_ge(pt_full, p1.n + 1)
                act.activation(pt_hi[:].rearrange("p s t -> p (s t)"), pt_bank[:, :], ACT.Copy).then_inc(pt_hi_done, 1)
            if cur:
                add_u(3)
                empty_u(0)
                empty_u(1)
            if prev:
                act.wait_ge(ln2_rstd, 2 * p1.n + 2)
                normalise2(0)
            if cur:
                empty_u(2)
            if prev:
                normalise2(1)
            if cur:
                empty_u(3)
            if prev:
                normalise2(2)
            if nxt:
                modulate(i.plus(1))
            if prev:
                normalise2(3)
            if prev2:
                act.wait_ge(route, RT * p2.n + 3)
                act.activation(lg_e[:], lg_d[:], ACT.Exp).then_inc(route_exp, 1)

        iteration(Group(0, 0), True, False, False, True)
        iteration(Group(0, 1), True, True, False, True)
        with act.Fori(1, NG // 2 - 1) as half:
            for par in range(2):
                iteration(Group(half, par), True, True, True, True)
        iteration(Group(NG // 2 - 1, 0), True, True, True, True)
        iteration(Group(NG // 2 - 1, 1), True, True, True, False)
        iteration(Group(NG // 2, 0), False, True, True, False)
        iteration(Group(NG // 2, 1), False, False, True, False)

        def w1_high(n, e, b):
            act.wait_ge(w1_in[b % 2], 16 * (NB // 2 * e + b // 2 + 1))
            wait_past(act, h1_full, 4 * n - 4)
            act.activation(w1_hi[b % 2][:], raw[2 * (b % 2)][:], ACT.Copy).then_inc(w1_hi_done, 1)

        def w2_high(n, e, b):
            act.wait_ge(w2_in[b % 2], 16 * (NB // 2 * e + b // 2 + 1))
            results_done(act, e, b)
            act.activation(w2_hi[b % 2][:], raw[2 * (b % 2) + 1][:], ACT.Copy).then_inc(w2_hi_done, 1)

        def relu(e, b, j):
            n = NB * e + b
            act.wait_ge(h1_full, 4 * n + j + 1)
            wait_past(act, h1_split, 4 * n + j - 3)
            act.wait_ge(pro_evac, PRO_END)
            act.activation(h1_f[:, j, :], h_bank[j][:, :], ACT.Relu,
                           bias=b1_col[:, bass.ds(e * (H // P) + b * HC + j, 1)]).then_inc(relu_done, 1)

        def rows_high(e):
            for k in range(KC):
                act.wait_ge(bt_full, 4 * e + k + 1)
                act.activation(bt_hi[:, k, :], h_bank[k][:, :], ACT.Copy).then_inc(bt_hi_done, 1)

        act.wait_ge(s_full, NG)
        w1_high(0, 0, 0)
        rows_high(0)

        def expert(e, last):
            for b in range(NB):
                n = NB * e + b
                relu(e, b, 0)
                if b + 1 < NB:
                    w1_high(n + 1, e, b + 1)
                elif not last:
                    w1_high(n + 1, e + 1, 0)
                relu(e, b, 1)
                w2_high(n, e, b)
                relu(e, b, 2)
                relu(e, b, 3)
            if not last:
                rows_high(e + 1)

        expert(0, False)
        with act.Fori(1, E - 1) as e:
            expert(e, False)
        expert(E - 1, True)

    @block.vector
    def _(dve):
        dve.memset(table_init[:, :, 0:1], NO_TOKEN).then_inc(init_made, 1)
        dve.memset(table_init[:, :, 1:2], 0).then_inc(init_made, 1)
        dve.memset(wg_pad[:], 0.0).then_inc(init_made, 1)
        dve.memset(count[:], 0.0).then_inc(init_made, 1)
        dve.memset(grows[0][:], 0.0).then_inc(init_made, 1)
        dve.memset(grows[1][:], 0.0).then_inc(init_made, 1)
        dve.memset(pg[:], 0.0).then_inc(init_made, 1)
        dve.memset(half_neg[:], -0.5).then_inc(init_made, 1)
        dve.memset(one_row[:], 1.0).then_inc(init_made, 1)
        dve.wait_ge(init_made, DVE_MADE)
        dve.wait_ge(sc_exp, 1)
        dve.tensor_scalar(sc_tmp[:], sc_tmp[:], 1.0, None, ALU.add).then_inc(sc_step, 1)
        dve.wait_ge(sc_step, 1)
        dve.reciprocal(sc_tmp[:], sc_tmp[:]).then_inc(sc_step, 1)
        dve.wait_ge(sc_step, 2)
        dve.tensor_tensor(sc_rows[:], sc_rows[:], sc_tmp[:], ALU.mult).then_inc(sc_ready, 1)

        def layer_stats(g, rows, step, ready, per_step, st, mvt, ve, mn, used, parts=P, segs=GS):
            used()
            for s in range(segs):
                dve.bn_stats(st[0:parts, s, :], rows[:, s, :]).then_inc(step, 1)
            dve.wait_ge(step, per_step * g + segs)
            stand_alone(dve, dve_passed)
            for s in range(segs):
                dve.bn_aggr(mvt[0:parts, s, :], st[0:parts, s, :]).then_inc(step, 1)
            dve.wait_ge(step, per_step * g + 2 * segs)
            dve.tensor_scalar(ve[0:parts, 0:segs], mvt[0:parts, 0:segs, 1], EPS, None, ALU.add).then_inc(ready, 1)
            dve.tensor_scalar(mn[0:parts, 0:segs], mvt[0:parts, 0:segs, 0], -1.0, None, ALU.mult).then_inc(ready, 1)

        def stats1(g):
            dve.wait_ge(x_in[g.par], 16 * (g.half + 1))
            layer_stats(g.n, xa[g.par], ln1_step, ln1_ready, 8, stats[0], mv[0], VE1, MN1,
                        lambda: wait_past(dve, xn_done, 4 * g.n))

        def split_weights(q, src, hi, lo, done, step):
            for c in range(KC):
                dve.wait_ge(pro_evac, q + c + 1)
                dve.tensor_copy(hi[:, c, :], src[:, c, :]).then_inc(step, 1)
                dve.wait_ge(step, c + 1)
                dve.tensor_tensor(lo[:, c, :], src[:, c, :], hi[:, c, :].bitcast(F32), ALU.subtract).then_inc(done, 1)

        stats1(Group(0, 0))
        split_weights(MCH, m_f, m_hi, m_lo, m_split, m_step)
        fix = [0]

        def link(ins):
            fix[0] += 1
            ins.then_inc(fix_step, 1)
            dve.wait_ge(fix_step, fix[0])

        dve.wait_ge(pro_evac, V4 + 1)
        dve.wait_ge(bqk_in, 32)
        link(dve.scalar_tensor_tensor(out=sc_tmp[:], in0=bqk[:, 0, :], scalar=1.0, in1=bqk[:, 1, :], op0=ALU.mult,
                                      op1=ALU.mult, accum_out=q_const[0:NBATCH, 1:2]))
        dve.wait_ge(pro_evac, MODS + 2)
        link(dve.scalar_tensor_tensor(out=sc_tmp[:], in0=modr[:, VC, :], scalar=1.0, in1=modr[:, SA, :], op0=ALU.mult,
                                      op1=ALU.mult, accum_out=q_const[0:NBATCH, 2:3]))
        link(dve.tensor_tensor(q_const[0:NBATCH, 0:1], q_const[0:NBATCH, 1:2], q_const[0:NBATCH, 2:3], ALU.add))
        link(dve.tensor_scalar(modr[:, CA, :], modr[:, CA, :], 1.0, None, ALU.add))
        link(dve.tensor_tensor(modr[:, VC, :], modr[:, VC, :], modr[:, CA, :], ALU.mult))
        for row in (GA, GB):
            dve.wait_ge(pro_evac, MODS + row + 1)
            link(dve.tensor_scalar(sc_tmp[:], modr[:, row, :], 0.0, 2.0, ALU.is_ge, ALU.mult))
            link(dve.tensor_scalar(sc_tmp[:], sc_tmp[:], -1.0, None, ALU.add))
            link(dve.tensor_tensor(modr[:, row, :], modr[:, row, :], sc_tmp[:], ALU.mult))
            link(dve.scalar_tensor_tensor(out=modr[:, row, :], in0=modr[:, row, :], scalar=GATE_FLOOR, in1=sc_tmp[:],
                                          op0=ALU.max, op1=ALU.mult))
        dve.tensor_scalar(modr[:, CB, :], modr[:, CB, :], 1.0, None, ALU.add).then_inc(mod_fixed, 1)
        dve.wait_ge(summ_in, 16)
        layer_stats(0, g_x[:].unsqueeze(1), gsum_step, gsum_stats, 0, stats[1], mv[1], VE2, MN2, lambda: None, NSEG, 1)
        dve.wait_ge(gsum_xn, 1)
        dve.wait_ge(vcg_in, 16 * NBATCH)
        dve.scalar_tensor_tensor(out=g_c[:], in0=g_a[:], scalar=1.0, in1=g_b[:], op0=ALU.mult, op1=ALU.mult,
                                 accum_out=q_const[0:NSEG, 3:4]).then_inc(gsum_step, 1)
        dve.wait_ge(gsum_step, 3)
        dve.wait_ge(qcg_in, 16 * NBATCH)
        dve.tensor_scalar(q_const[0:NSEG, 3:4], q_const[0:NSEG, 3:4], q_const_g[:, 0:1], SCALE, ALU.add, ALU.mult) \
            .then_inc(gsum_step, 1)
        split_weights(VCH, vo_f, v_hi, v_lo, v_split, v_step)

        def split_rows(g):
            for k in range(KC):
                dve.wait_ge(ht_full, 4 * g.n + k + 1)
                dve.tensor_copy(ht_hi[:, k, :], ht[g.par][:, k, :]).then_inc(ht_hi_done, 1)
                dve.wait_ge(ht_hi_done, 4 * g.n + k + 1)
                dve.tensor_tensor(ht_lo[:, k, :], ht[g.par][:, k, :], ht_hi[:, k, :].bitcast(F32), ALU.subtract) \
                    .then_inc(ht_split, 1)

        split_rows(Group(0, 0))
        dve.wait_ge(pro_evac, BROW + 1)
        dve.wait_ge(bo_in, 16)
        dve.tensor_tensor(brow[:], brow[:], bo_row[:], ALU.add).then_inc(brow_ready, 1)
        dve.wait_ge(gsum_masked, 2)
        dve.reduce_max(MX[0:NSEG, 0:1], sg[:], AX_X).then_inc(gsum_step, 1)
        dve.wait_ge(gsum_step, 5)
        dve.scalar_tensor_tensor(out=MXC[0:NSEG, 0:1], in0=MX[0:NSEG, 0:1], scalar=SCALE, in1=q_const[0:NSEG, 3:4],
                                 op0=ALU.mult, op1=ALU.add).then_inc(gsum_step, 1)
        dve.wait_ge(gsum_step, 6)
        dve.tensor_tensor(NEGB[0:NSEG, 0:1], q_const[0:NSEG, 3:4], MXC[0:NSEG, 0:1], ALU.subtract).then_inc(gsum_negb, 1)
        dve.wait_ge(gsum_exp, 1)
        dve.reciprocal(PREC[0:NSEG, 0:1], PSUMS[0:NSEG, 0:1]).then_inc(gsum_step, 1)
        dve.wait_ge(gsum_step, 7)
        dve.tensor_scalar(pg[:, 0:NSEG], pg[:, 0:NSEG], PREC[0:NSEG, 0:1], None, ALU.mult).then_inc(gsum_prob, 1)
        dve.wait_ge(pro_evac, TG + 1)
        dve.tensor_copy(g_split[:, 0, :], g_a[:]).then_inc(gsum_step, 1)
        dve.wait_ge(gsum_step, 8)
        dve.tensor_tensor(g_x[:], g_a[:], g_split[:, 0, :], ALU.subtract).then_inc(gsum_step, 1)
        dve.wait_ge(gsum_step, 9)
        dve.tensor_copy(g_split[:, 1, :], g_x[:]).then_inc(gsum_step, 1)
        dve.wait_ge(gsum_step, 10)
        dve.tensor_tensor(g_split[:, 2, :], g_x[:], g_split[:, 1, :], ALU.subtract).then_inc(g_split_done, 1)
        dve.wait_ge(pro_evac, PRO_END)
        dve.wait_ge(tab_in, 16)
        dve.wait_ge(qc_in, 16)
        dve.wait_ge(bg_in, 16)
        dve.wait_ge(made, POOL_MADE)

        def query_const(g):
            b = batch_of(g)
            for s in range(GS):
                if s > 0:
                    dve.wait_ge(qc_raw, 4 * g.n + s)
                dve.scalar_tensor_tensor(out=qc_junk, in0=xa[g.par][:, s, :], scalar=1.0,
                                         in1=vc_tab[:, bass.ds(b, 1), :].rearrange("p b d -> p (b d)"), op0=ALU.mult,
                                         op1=ALU.mult, accum_out=QRAW[:, s:s + 1]).then_inc(qc_raw, 1)
            dve.wait_ge(qc_raw, 4 * g.n + 4)
            dve.tensor_scalar(QCS2[g.par], QRAW, qc_bc[:, bass.ds(b, 1)], SCALE, ALU.add, ALU.mult) \
                .then_inc(qc_ready, 1)

        dve.wait_ge(g_split_done, 1)
        query_const(Group(0, 0))
        tok4 = [P, GS, E]

        def route_logits(g):
            r = RT * g.n
            dve.wait_ge(lg_full, g.n + 1)
            dve.tensor_tensor(lg[:], lg_bank[:, :].rearrange("p (s c) -> p s c", c=P)[:, :, 0:E],
                              bg_bc[:].unsqueeze(1).to_broadcast(tok4), ALU.add).then_inc(route, 1)
            dve.wait_ge(route, r + 1)
            dve.reduce_max(LG_MX, lg[:], AX_X).then_inc(route, 1)
            dve.wait_ge(route, r + 2)
            dve.tensor_tensor(lg_d[:], lg[:], LG_MX.unsqueeze(2).to_broadcast(tok4), ALU.subtract).then_inc(route, 1)
            dve.wait_ge(route, r + 3)
            dve.scalar_tensor_tensor(out=lg_v[:], in0=lg_d[:], scalar=0.0, in1=eidx[:], op0=ALU.is_ge,
                                     op1=ALU.mult).then_inc(route, 1)
            dve.wait_ge(route, r + 4)
            dve.tensor_reduce(V_MIN, lg_v[:], AX_X, ALU.min).then_inc(route, 1)
            dve.wait_ge(route, r + 5)
            dve.tensor_tensor(onehot[:], lg_v[:], V_MIN.unsqueeze(2).to_broadcast(tok4), ALU.is_equal) \
                .then_inc(route, 1)

        def route_slots(g):
            r = RT * g.n
            dve.wait_ge(pos_full, g.n + 1)
            dve.wait_ge(route, r + 6)
            dve.tensor_tensor(lg_r[:], pos_bank[:, 0:GS * E].rearrange("p (s e) -> p s e", e=E), onehot[:], ALU.mult) \
                .then_inc(route, 1)
            dve.wait_ge(route, r + 7)
            dve.reduce_sum(RANK, lg_r[:], AX_X).then_inc(route, 1)
            dve.wait_ge(route, r + 8)
            dve.tensor_scalar(OVER, RANK, float(CAP), float(NO_TOKEN), ALU.is_ge, ALU.mult).then_inc(route, 1)
            dve.scalar_tensor_tensor(out=SLOT_A, in0=V_MIN, scalar=float(CAP), in1=RANK, op0=ALU.mult, op1=ALU.add) \
                .then_inc(route, 1)
            dve.wait_ge(route, r + 10)
            dve.tensor_tensor(SLOT_B, SLOT_A, OVER, ALU.add).then_inc(route, 1)
            dve.wait_ge(route, r + 11)
            wait_past(dve, scattered[g.par], 16 * GS * g.half)
            dve.tensor_scalar(slot_i[g.par][:], SLOT_B, float(E * CAP), None, ALU.add).then_inc(route, 1)
            dve.tensor_reduce(osum[:], onehot[:].rearrange("p s e -> p e s"), AX_X, ALU.add).then_inc(route, 1)
            dve.wait_ge(route, r + 13)
            dve.tensor_tensor(count[:], count[:], osum[:], ALU.add).then_inc(route, 1)
            dve.wait_ge(route_exp, g.n + 1)
            dve.reduce_sum(LG_SUM, lg_e[:], AX_X).then_inc(route, 1)
            dve.wait_ge(route, r + 15)
            dve.reciprocal(pay[g.par][:, :, 1].bitcast(F32), LG_SUM).then_inc(route, 1)
            dve.tensor_copy(pay[g.par][:, :, 0], tokids[:, bass.ds(g.n * GS, GS)]).then_inc(route, 1)

        def iteration(i, cur, prev, prev2, nxt, prev3):
            n = i.n
            p1, p2, p3 = i.plus(-1), i.plus(-2), i.plus(-3)
            if prev:
                dve.wait_ge(s_full, p1.n + 1)
                dve.reduce_max(MX, s_bank[:, :].rearrange("p (s t) -> p s t", t=P), AX_X).then_inc(mx_step, 1)
                dve.wait_ge(mx_step, 2 * p1.n + 1)
                dve.wait_ge(qc_ready, p1.n + 1)
                dve.scalar_tensor_tensor(out=MXC, in0=MX, scalar=SCALE, in1=QCS2[p1.par], op0=ALU.mult, op1=ALU.add) \
                    .then_inc(mx_step, 1)
                dve.wait_ge(mx_step, 2 * p1.n + 2)
                dve.tensor_tensor(NEGB, QCS2[p1.par], MXC, ALU.subtract).then_inc(negb_ready, 1)
            if prev3:
                route_slots(p3)
            if prev:
                dve.wait_ge(exp_done, 4 * p1.n + 4)
                dve.reciprocal(PREC, PSUMS).then_inc(prec_ready, 1)
                dve.wait_ge(prec_ready, p1.n + 1)
                dve.tensor_tensor(prob[:], prob[:], PREC.unsqueeze(2).to_broadcast([P, GS, P]), ALU.mult) \
                    .then_inc(prob_ready, 1)
            if nxt:
                stats1(i.plus(1))
            if prev:
                dve.wait_ge(pt_hi_done, p1.n + 1)
                dve.tensor_tensor(pt_lo[:].rearrange("p s t -> p (s t)"), pt_bank[:, :],
                                  pt_hi[:].rearrange("p s t -> p (s t)").bitcast(F32), ALU.subtract).then_inc(pt_split, 1)
                if isinstance(n, int) and n == 1:
                    dve.wait_ge(late_tab_in, 48)
                if not isinstance(n, int) or n >= 3:
                    dve.wait_ge(h2_stored[p1.par], 16 * p1.half)
                for s in range(GS):
                    dve.wait_ge(av_full, 4 * p1.n + s + 1)
                    dve.tensor_tensor(h2[p1.par][:, s, :], big[s][:, :],
                                      ga_tab[:, bass.ds(batch_of(p1), 1), :].rearrange("p b d -> p (b d)"), ALU.mult) \
                        .then_inc(av_taken, 1)
                dve.wait_ge(x2_ready, 4 * p1.n + 4)
                layer_stats(p1.n, xr[p1.par], ln2_step, ln2_ready, 8, stats[1], mv[1], VE2, MN2,
                            lambda: wait_past(dve, xn2_done, 4 * p1.n))
            if cur:
                for s in range(GS):
                    dve.wait_ge(u_hi_done, 4 * n + s + 1)
                    dve.tensor_tensor(u_lo[:, s, :], big[s][:, :], u_hi[:, s, :].bitcast(F32), ALU.subtract) \
                        .then_inc(u_split, 1)
            if nxt:
                split_rows(i.plus(1))
                query_const(i.plus(1))
            if prev2:
                route_logits(p2)

        iteration(Group(0, 0), True, False, False, True, False)
        iteration(Group(0, 1), True, True, False, True, False)
        iteration(Group(1, 0), True, True, True, True, False)
        iteration(Group(1, 1), True, True, True, True, True)
        iteration(Group(2, 0), True, True, True, True, True)
        iteration(Group(2, 1), True, True, True, True, True)
        with dve.Fori(3, NG // 2 - 1) as half:
            for par in range(2):
                iteration(Group(half, par), True, True, True, True, True)
        iteration(Group(NG // 2 - 1, 0), True, True, True, True, True)
        iteration(Group(NG // 2 - 1, 1), True, True, True, False, True)
        iteration(Group(NG // 2, 0), False, True, True, False, True)
        iteration(Group(NG // 2, 1), False, False, True, False, True)
        iteration(Group(NG // 2 + 1, 0), False, False, False, False, True)

        def w1_low(n, b):
            dve.wait_ge(w1_hi_done, n + 1)
            dve.tensor_tensor(w1_lo[b % 2][:], raw[2 * (b % 2)][:], w1_hi[b % 2][:].bitcast(F32), ALU.subtract) \
                .then_inc(w1_split, 1)

        def w2_low(n, b):
            dve.wait_ge(w2_hi_done, n + 1)
            dve.tensor_tensor(w2_lo[b % 2][:], raw[2 * (b % 2) + 1][:], w2_hi[b % 2][:].bitcast(F32), ALU.subtract) \
                .then_inc(w2_split, 1)

        def split_hidden(e, b, j):
            n = NB * e + b
            dve.wait_ge(relu_done, 4 * n + j + 1)
            if j == 0:
                results_done(dve, e, b)
            dve.tensor_copy(h1_hi[b % 2][:, j, :], h1_f[:, j, :]).then_inc(h1_hi_done, 1)
            dve.wait_ge(h1_hi_done, 4 * n + j + 1)
            dve.tensor_tensor(h1_lo[b % 2][:, j, :], h1_f[:, j, :], h1_hi[b % 2][:, j, :].bitcast(F32), ALU.subtract) \
                .then_inc(h1_split, 1)

        def rows_low(e):
            for k in range(KC):
                dve.wait_ge(bt_hi_done, 4 * e + k + 1)
                dve.tensor_tensor(bt_lo[:, k, :], h_bank[k][:, :], bt_hi[:, k, :].bitcast(F32), ALU.subtract) \
                    .then_inc(bt_split, 1)

        def result_rows(e):
            for j in range(GS):
                q = 4 * e + j
                wait_past(dve, y_scaled, q - 1)
                mix = gb_mix[j % 2]
                dve.tensor_scalar(mix[:], gb_tab[:, 0, :], coef[:, 0, bass.ds(q, 1)], None, ALU.mult) \
                    .then_inc(mix_step, 1)
                for b in range(1, NBATCH):
                    dve.wait_ge(mix_step, 4 * q + b)
                    dve.scalar_tensor_tensor(out=mix[:], in0=gb_tab[:, b, :], scalar=coef[:, b, bass.ds(q, 1)], in1=mix[:],
                                             op0=ALU.mult, op1=ALU.add).then_inc(mix_step, 1)
                if j == 0:
                    dve.wait_ge(b2_in, 16 * (e + 1))
                dve.wait_ge(y_full, q + 1)
                wait_past(dve, y_sent[j % 2], 16 * (2 * e + j // 2))
                dve.tensor_tensor(yo[j % 2][:], y_bank[j][:, :], b2_bc[:], ALU.add).then_inc(y_taken, 1)

        dve.memset(xh[:], 0.0).then_inc(xh_cleared, 1)
        dve.memset(xo[:], 0.0).then_inc(xh_cleared, 1)
        w1_low(0, 0)
        dve.wait_ge(table_in, 16)
        tok = table[:].rearrange("p e j c -> p (e j) c")
        dve.tensor_copy(tok_h[:], tok[:, 0:GS, 0]).then_inc(tok_h_ready, 1)
        dve.tensor_copy(tok_x[:], tok[:, 0:GS, 0]).then_inc(tok_x_ready, 1)
        dve.tensor_copy(tok_f[:], tok[:, :, 0]).then_inc(coef_step, 1)
        dve.wait_ge(coef_step, 1)
        gates = tok[:, :, 1].bitcast(F32)
        for b in range(NBATCH):
            dve.tensor_scalar(coef_t[:, 0, :], tok_f[:], float(L * b), None, ALU.is_ge).then_inc(coef_step, 1)
            dve.wait_ge(coef_step, 3 * b + 2)
            dve.scalar_tensor_tensor(out=coef_t[:, 1, :], in0=tok_f[:], scalar=float(L * (b + 1)), in1=coef_t[:, 0, :],
                                     op0=ALU.is_lt, op1=ALU.mult).then_inc(coef_step, 1)
            dve.wait_ge(coef_step, 3 * b + 3)
            dve.tensor_tensor(coef[:, b, :], coef_t[:, 1, :], gates, ALU.mult).then_inc(coef_step, 1)
            dve.wait_ge(coef_step, 3 * b + 4)
        dve.wait_ge(gb_in, 16)
        rows_low(0)

        def expert(e, first, last):
            for b in range(NB):
                n = NB * e + b
                if not (last and b == NB - 1):
                    w1_low(n + 1, (b + 1) % 2)
                for j in range(HC):
                    split_hidden(e, b, j)
                w2_low(n, b)
                if b == 0 and not first:
                    result_rows(e - 1)
                if b == 1:
                    if not last:
                        dve.wait_ge(xh_in, 16 * GS * (e + 1))
                        dve.wait_ge(table_in, 16)
                        dve.tensor_copy(tok_h[:], tok[:, bass.ds(GS * (e + 1), GS), 0]).then_inc(tok_h_ready, 1)
                    if not first:
                        for par in range(2):
                            dve.wait_ge(y_sent[par], 32 * e)
                        dve.wait_ge(table_in, 16)
                        dve.tensor_copy(tok_x[:], tok[:, bass.ds(GS * e, GS), 0]).then_inc(tok_x_ready, 1)
            if not last:
                rows_low(e + 1)

        expert(0, True, False)
        expert(1, False, False)
        with dve.Fori(2, E - 1) as e:
            expert(e, False, False)
        expert(E - 1, False, True)
        result_rows(E - 1)

    @block.gpsimd
    def _(pool):
        pool.memset(ident[:], 0.0).then_inc(ident_made, 1)
        pool.wait_ge(ident_made, 1)
        pool.affine_select(out=ident[:], in_=ident[:], compare_op=ALU.not_equal, fill=1.0, base=0, pattern=[[-1, P]],
                           channel_multiplier=1).then_inc(ident_made, 1)
        pool.memset(tri[:], 1.0).then_inc(made, 1)
        pool.memset(ones[:], 1.0).then_inc(made, 1)
        pool.memset(seg_sel[:], 1.0).then_inc(made, 1)
        pool.wait_ge(made, 3)
        pool.affine_select(out=tri[:], in_=tri[:], compare_op=ALU.is_gt, fill=0.0, base=0, pattern=[[1, P]],
                           channel_multiplier=-1).then_inc(made, 1)
        pool.affine_select(out=seg_sel[:], in_=seg_sel[:], compare_op=ALU.is_ge, fill=0.0, base=0,
                           pattern=[[-3, GS], [0, P]], channel_multiplier=1).then_inc(made, 1)
        pool.wait_ge(made, 5)
        pool.affine_select(out=seg_sel[:], in_=seg_sel[:], compare_op=ALU.is_ge, fill=0.0, base=2,
                           pattern=[[3, GS], [0, P]], channel_multiplier=-1).then_inc(made, 1)
        pool.iota(tokids[:], pattern=[[P, NSEG]], base=0, channel_multiplier=1).then_inc(made, 1)
        pool.iota(eidx[:], pattern=[[0, GS], [1, E]], base=-E, channel_multiplier=0,
                  allow_small_or_imprecise_dtypes=True).then_inc(made, 1)
        pool.wait_ge(made, POOL_MADE)
        pool.wait_ge(init_made, DVE_MADE)

        def inverse_root(g, ready, step, ve, mn, rs, nr, parts=P, segs=GS):
            pool.wait_ge(ready, 2 * g + 2)
            pool.tensor_tensor(rs[0:parts, 0:segs], ve[0:parts, 0:segs], half_neg[0:parts, 0:segs], ALU.pow) \
                .then_inc(step, 1)
            pool.wait_ge(step, 2 * g + 1)
            pool.tensor_tensor(nr[0:parts, 0:segs], mn[0:parts, 0:segs], rs[0:parts, 0:segs], ALU.mult).then_inc(step, 1)

        def normalise1(g):
            inverse_root(g.n, ln1_ready, ln1_rstd, VE1, MN1, RS1, NR1)
            pool.wait_ge(ln1_rstd, 2 * g.n + 2)
            stand_alone(pool, pool_passed)
            for s in range(GS):
                pool.tensor_scalar(xa[g.par][:, s, :], xa[g.par][:, s, :], RS1[:, s:s + 1], NR1[:, s:s + 1], ALU.mult,
                                   ALU.add).then_inc(xn_done, 1)

        normalise1(Group(0, 0))
        pool.wait_ge(table_cleared, 16)
        inverse_root(0, gsum_stats, gsum_rstd, VE2, MN2, RS2, NR2, NSEG, 1)
        pool.wait_ge(pro_evac, SG + 1)
        blocks = sg[:].rearrange("p (b r) -> p b r", b=NBATCH)
        pool.affine_select(out=blocks, in_=blocks, compare_op=ALU.is_ge, fill=FAR_BELOW, base=0,
                           pattern=[[-(NSEG // NBATCH), NBATCH], [0, NSEG // NBATCH]], channel_multiplier=1) \
            .then_inc(gsum_masked, 1)
        pool.wait_ge(gsum_masked, 1)
        pool.affine_select(out=blocks, in_=blocks, compare_op=ALU.is_ge, fill=FAR_BELOW, base=NSEG // NBATCH - 1,
                           pattern=[[NSEG // NBATCH, NBATCH], [0, NSEG // NBATCH]], channel_multiplier=-1) \
            .then_inc(gsum_masked, 1)

        def scatter(g):
            pool.wait_ge(route, RT * g.n + RT)
            stand_alone(pool, pool_passed)
            for s in range(GS):
                pool.indirect_dma_start(out=table_dram, out_offset=bass.IndirectOffsetOnAxis(slot_i[g.par][:, s:s + 1], 0),
                                        in_=pay[g.par][:, s, :], in_offset=None, bounds_check=E * CAP - 1,
                                        oob_is_err=False).then_inc(scattered[g.par], 16)

        def iteration(i, prev, nxt, prev3):
            p1 = i.plus(-1)
            b = batch_of(p1)
            if nxt:
                normalise1(i.plus(1))
            if prev3:
                scatter(i.plus(-3))
            if prev:
                pool.wait_ge(xr_in[p1.par], 16 * (p1.half + 1))
                for s in range(GS):
                    pool.wait_ge(av_taken, 4 * p1.n + s + 1)
                    pool.tensor_tensor(xr[p1.par][:, s, :], xr[p1.par][:, s, :], h2[p1.par][:, s, :], ALU.add) \
                        .then_inc(x2_ready, 1)
                inverse_root(p1.n, ln2_ready, ln2_rstd, VE2, MN2, RS2, NR2)
                if isinstance(i.n, int) and i.n == 1:
                    pool.wait_ge(late_tab_in, 48)
                for s in range(GS):
                    rows = h2[p1.par][:, s, :]
                    pool.wait_ge(xn2_done, 4 * p1.n + s + 1)
                    stand_alone(pool, pool_passed)
                    pool.tensor_tensor(rows, rows, cb_tab[:, bass.ds(b, 1), :].rearrange("p b d -> p (b d)"), ALU.mult) \
                        .then_inc(h2_scaled, 1)
                    pool.wait_ge(h2_scaled, 4 * p1.n + s + 1)
                    stand_alone(pool, pool_passed)
                    pool.tensor_tensor(rows, rows, sb_tab[:, bass.ds(b, 1), :].rearrange("p b d -> p (b d)"), ALU.add) \
                        .then_inc(h2_ready, 1)

        iteration(Group(0, 0), False, True, False)
        iteration(Group(0, 1), True, True, False)
        iteration(Group(1, 0), True, True, False)
        iteration(Group(1, 1), True, True, True)
        with pool.Fori(2, NG // 2 - 1) as half:
            for par in range(2):
                iteration(Group(half, par), True, True, True)
        iteration(Group(NG // 2 - 1, 0), True, True, True)
        iteration(Group(NG // 2 - 1, 1), True, False, True)
        iteration(Group(NG // 2, 0), True, False, True)
        iteration(Group(NG // 2, 1), False, False, True)
        iteration(Group(NG // 2 + 1, 0), False, False, True)

        def gather(rows, source, tokens, done):
            for j in range(GS):
                pool.indirect_dma_start(out=rows[:, j, :], out_offset=None, in_=source,
                                        in_offset=bass.IndirectOffsetOnAxis(tokens[:, j:j + 1], 0), bounds_check=T - 1,
                                        oob_is_err=False).then_inc(done, 16)

        def gather_h(e):
            wait_past(pool, bt_full, 4 * e)
            pool.wait_ge(tok_h_ready, e + 1)
            stand_alone(pool, pool_passed)
            gather(xh, h2_dram, tok_h, xh_in)

        def gather_x(e):
            pool.wait_ge(tok_x_ready, e + 1)
            stand_alone(pool, pool_passed)
            gather(xo, out_rows, tok_x, xo_in)

        def finish_rows(e):
            pool.wait_ge(xo_in, 16 * GS * (e + 1))
            for j in range(GS):
                q = 4 * e + j
                pool.wait_ge(y_taken, q + 1)
                pool.tensor_tensor(yo[j % 2][:], yo[j % 2][:], gb_mix[j % 2][:], ALU.mult).then_inc(y_scaled, 1)
                pool.wait_ge(y_scaled, q + 1)
                pool.tensor_tensor(yo[j % 2][:], yo[j % 2][:], xo[:, j, :], ALU.add).then_inc(y_ready, 1)
                pool.wait_ge(y_ready, q + 1)
                stand_alone(pool, pool_passed)
                pool.indirect_dma_start(out=out_rows, out_offset=bass.IndirectOffsetOnAxis(tok_x[:, j:j + 1], 0),
                                        in_=yo[j % 2][:], in_offset=None, bounds_check=T - 1, oob_is_err=False) \
                    .then_inc(y_sent[j % 2], 16)

        for par in range(2):
            pool.wait_ge(h2_stored[par], 16 * (NG // 2))
            pool.wait_ge(x2_stored[par], 16 * (NG // 2))
        pool.wait_ge(xh_cleared, 2)
        gather_h(0)
        gather_x(0)
        gather_h(1)
        with pool.Fori(1, E - 1) as e:
            finish_rows(e - 1)
            gather_x(e)
            gather_h(e + 1)
        finish_rows(E - 2)
        gather_x(E - 1)
        finish_rows(E - 1)

    stack.close()


_INS = ["L0_attn_x", "L0_attn_Wq", "L0_attn_bq", "L0_attn_Wk", "L0_attn_bk", "L0_attn_Wv", "L0_attn_bv",
        "L0_attn_Wo", "L0_attn_bo", "L0_ffn_Wg", "L0_ffn_bg", "L0_ffn_W1", "L0_ffn_b1", "L0_ffn_W2", "L0_ffn_b2",
        "L0_c", "L0_wmod"]


def kernel(**inputs):
    import numpy as _np
    import concourse.bacc as _bacc
    from concourse import mybir as _mybir
    from concourse.bass_utils import run_bass_kernel_spmd as _run

    nc = _bacc.Bacc("TRN2", target_bir_lowering=False, num_devices=1)
    arrays, args = {}, []
    for name in _INS:
        a = _np.ascontiguousarray(inputs[name])
        arrays[f"in_{name}_dram"] = a
        args.append(nc.dram_tensor(f"in_{name}_dram", a.shape, _mybir.dt.from_np(a.dtype), kind="ExternalInput").ap())
    shape = inputs["L0_attn_x"].shape
    out = nc.dram_tensor("out_0_dram", shape, _mybir.dt.float32, kind="ExternalOutput").ap()
    build_block(nc, *args, out)
    r = _run(nc, [arrays], core_ids=[0])
    return r.results[0]["out_0_dram"]
```

```python
from contextlib import ExitStack

import concourse.bass as bass
from concourse import mybir

F32 = mybir.dt.float32
F32R = mybir.dt.float32r
BF16 = mybir.dt.bfloat16
I32 = mybir.dt.int32
ACT = mybir.ActivationFunctionType
ALU = mybir.AluOpType
AX_X = mybir.AxisListType.X

P = 128
GS = 4
ROWS = GS * P
HEAD_DIM = 32
SCALE = HEAD_DIM ** -0.5
EPS = 1e-5
GATE_FLOOR = 0.25
NO_TOKEN = 1 << 20
FAR_BELOW = -3.0e38
RT = 20

SA, CA, GA, SB, CB, GB, VC = range(7)


class Group:

    def __init__(self, half, par):
        self.half, self.par, self.n = half, par, half * 2 + par

    def plus(self, k):
        q = self.par + k
        return Group(self.half + q // 2, q % 2)


def build_block(nc, x, wq, bq, wk, bk, wv, bv, wo, bo, wg, bg, w1, b1, w2, b2, cond, wmod, out):
    NBATCH, L, D = x.shape
    T = NBATCH * L
    KC = D // P
    NG = T // ROWS
    GPB = L // ROWS
    NSEG = T // P
    E = wg.shape[1]
    H = w1.shape[2]
    CAP = -(-T // E)
    HB = 512
    NB = H // HB
    HC = HB // P
    assert D == 512 and ROWS == 512 and CAP == ROWS and KC == 4 and HC == 4 and NSEG == 64 and NB % 2 == 0

    x_rows = x.rearrange("b l d -> (b l) d")
    out_rows = out.rearrange("b l d -> (b l) d")

    mod_dram = nc.dram_tensor("mod_rows", (NBATCH, 7, D), F32, kind="Internal").ap()
    qc_dram = nc.dram_tensor("query_consts", (NBATCH, 1), F32, kind="Internal").ap()
    global_dram = nc.dram_tensor("global_rows", (NSEG * 3, D), BF16, kind="Internal").ap()
    h2_dram = nc.dram_tensor("h2_rows", (T, D), F32, kind="Internal").ap()
    table_dram = nc.dram_tensor("slot_table", (E * CAP, 2), I32, kind="Internal").ap()

    KB = 1024
    base = nc.sbuf_base + (-nc.sbuf_base) % 64
    limit = nc.sbuf_usable_end
    sizes = {F32: 4, F32R: 4, BF16: 2, I32: 4}
    cursor = [base]

    def at(name, shape, dt, offset):
        n = sizes[dt]
        for k in shape[1:]:
            n *= k
        assert offset + n <= limit, (name, offset + n - limit)
        return nc.alloc_sbuf_tensor_at(name, shape, dt, offset=offset), offset + n

    def keep(name, shape, dt):
        t, end = at(name, shape, dt, cursor[0])
        cursor[0] = end + (-end) % 32
        return t

    def region(kilobytes):
        start = cursor[0]
        cursor[0] += kilobytes * KB
        assert cursor[0] <= limit
        return start

    def over(start, *tensors):
        made = []
        for name, shape, dt in tensors:
            t, start = at(name, shape, dt, start)
            made.append(t)
        return made

    ident = keep("ident", [P, P], F32)
    tri = keep("tri", [P, P], BF16)
    ones = keep("ones", [P, P], BF16)
    seg_sel = keep("seg_sel", [P, GS, P], BF16)
    grows = [keep(f"grows{i}", [P, D], BF16) for i in range(2)]
    wg_pad = keep("wg_pad", [P, KC, P], F32)
    b1_col = keep("b1_col", [P, E * H // P], F32)
    tokids = keep("tokids", [P, NSEG], I32)
    eidx = keep("eidx", [P, GS, E], F32)
    bg_bc = keep("bg_bc", [P, E], F32)
    mod_col = keep("mod_col", [P, 2, KC, NBATCH], F32)
    u_col = keep("u_col", [P, KC], F32)
    bias_col = keep("bias_col", [P, 3 * KC], F32)
    qc_bc = keep("qc_bc", [P, NBATCH], F32)
    half_neg = keep("half_neg", [P, GS], F32)
    count = keep("count", [P, E], BF16)
    over_tile = keep("over_tile", [P, GS, GS - 1], F32)
    tile_ends = keep("tile_ends", [P, GS, GS - 1], F32)
    expert_rows = keep("expert_rows", [1, E], I32)
    onehot = keep("onehot", [P, GS, E], BF16)
    lg, lg_d, lg_v, lg_e, lg_r = (keep(f"lg{i}", [P, GS, E], F32) for i in range(5))
    osum = keep("osum", [P, E], F32)
    per_tok = keep("per_tok", [P, 24, GS], F32)
    (LG_MX, V_MIN, RANK, OVER, SLOT_A, SLOT_B, TILE, LG_SUM, MX, MXC, NEGB, PSUMS, PREC, VE1, MN1, RS1, NR1,
     VE2, MN2, RS2, NR2, QC, QCS, QRAW) = (per_tok[:, i, :] for i in range(24))
    stats = [keep(f"stats{i}", [P, GS, 6], F32) for i in range(2)]
    mv = [keep(f"mv{i}", [P, GS, 2], F32) for i in range(2)]
    slot_i = [keep(f"slot_i{i}", [P, GS], I32) for i in range(2)]
    pay = [keep(f"pay{i}", [P, GS, 2], I32) for i in range(2)]
    bias_rows = keep("bias_rows", [3 * KC, P], F32)
    sc_t = keep("sc_t", [P, KC, NBATCH], F32)
    bk_cols = keep("bk_cols", [P, KC, NBATCH], F32)
    q_const = keep("q_const", [P, 4], F32)
    q_const_g = keep("q_const_g", [NSEG, 1], F32)
    one_row = keep("one_row", [1, NSEG], F32)
    tok_h = keep("tok_h", [P, GS], I32)
    tok_x = keep("tok_x", [P, GS], I32)
    tok_g = keep("tok_g", [P, GS], I32)
    gate_x = keep("gate_x", [P, GS], F32)

    r_m, r_v, r_xa, r_ht, r_split, r_xr = (region(16) for _ in range(6))
    r_gt, r_u, r_h2, r_h2t, r_p = region(8), region(16), region(16), region(8), region(6)
    r_tab, r_raw0 = region(32), region(8)

    full = [P, KC, D]
    m_hi, m_lo = over(r_m, ("m_hi", full, F32R), ("m_lo", full, F32R))
    v_hi, v_lo = over(r_v, ("v_hi", full, F32R), ("v_lo", full, F32R))
    xa = over(r_xa, ("xa0", full, F32), ("xa1", full, F32))
    ht = over(r_ht, ("ht0", full, F32), ("ht1", full, F32))
    ht_hi, ht_lo = over(r_split, ("ht_hi", full, F32R), ("ht_lo", full, F32R))
    xr = over(r_xr, ("xr0", full, F32), ("xr1", full, F32))
    gt, = over(r_gt, ("gt", full, F32))
    u_hi, u_lo = over(r_u, ("u_hi", full, F32R), ("u_lo", full, F32R))
    h2 = over(r_h2, ("h2_0", full, F32), ("h2_1", full, F32))
    h2t, = over(r_h2t, ("h2t", full, F32))
    seg_sq = [P, GS, P]
    prob, pt_hi, pt_lo = over(r_p, ("prob", seg_sq, F32), ("pt_hi", seg_sq, F32R), ("pt_lo", seg_sq, F32R))
    batch_rows = [P, NBATCH, D]
    ga_tab, cb_tab, sb_tab, vc_tab = over(r_tab, *((f"{k}_tab", batch_rows, F32) for k in ("ga", "cb", "sb", "vc")))

    wq_s, wk_s = over(r_xr, ("wq_s", full, F32), ("wk_s", full, F32))
    wv_s, wo_s = over(r_u, ("wv_s", full, F32), ("wo_s", full, F32))
    m_f, = over(r_gt, ("m_f", full, F32))
    wo_t, = over(r_h2t, ("wo_t", full, F32))
    vo_f, = over(r_raw0, ("vo_f", full, F32))
    wm_s = over(r_xa + 8 * KB, ("wm_s0", full, F32)) + over(r_ht + 8 * KB, ("wm_s1", full, F32))
    modr, sc_rows = over(r_h2, ("modr", [NBATCH, 7, D], F32), ("sc_rows", [NBATCH, D], F32))
    g_x, g_a, g_b = over(r_p, ("g_x", [NSEG, D], F32), ("g_a", [NSEG, D], F32), ("g_b", [NSEG, D], F32))
    b1_rows, bo_row, bqk, hg_t = over(r_tab, ("b1_rows", [P, 2, P], F32), ("bo_row", [1, D], F32),
                                      ("bqk", [NBATCH, 2, D], F32), ("hg_t", [P, KC, NSEG], F32))
    g_split, brow, u_row, gg_t = over(r_tab + 8 * KB, ("g_split", [NSEG, 3, D], BF16), ("brow", [1, D], F32),
                                      ("u_row", [1, D], F32), ("gg_t", [P, KC, NSEG], F32))

    sg, pg, pg_t, table_init = over(r_tab + 16 * KB, ("sg", [NSEG, NSEG], F32), ("pg", [NSEG, P], F32),
                                    ("pg_t", [NSEG, NSEG], F32), ("table_init", [P, E * CAP // P, 2], I32))
    sc_tmp, = over(r_raw0, ("sc_tmp", [NBATCH, D], F32))
    g_c, = over(r_split, ("g_c", [NSEG, D], F32))
    qc_junk = prob[:].rearrange("p s t -> p (s t)")
    QCS2 = [QC, QCS]

    raw = over(r_raw0, ("raw0", full, F32)) + over(r_xa, ("raw1", full, F32), ("raw2", full, F32)) \
        + over(r_ht, ("raw3", full, F32))
    w1_hi, w1_lo, w2_hi, w2_lo = [None] * 2, [None] * 2, [None] * 2, [None] * 2
    w1_hi[0], w1_lo[0] = over(r_m, ("w1_hi0", full, F32R), ("w1_lo0", full, F32R))
    w1_hi[1], w1_lo[1] = over(r_v, ("w1_hi1", full, F32R), ("w1_lo1", full, F32R))
    w2_hi[0], w2_lo[0] = over(r_split, ("w2_hi0", full, F32R), ("w2_lo0", full, F32R))
    w2_hi[1], w2_lo[1] = over(r_xr, ("w2_hi1", full, F32R), ("w2_lo1", full, F32R))
    h1_f, = over(r_ht + 8 * KB, ("h1_f", full, F32))
    xh, = over(r_gt, ("xh", full, F32))
    bt_hi, bt_lo = over(r_u, ("bt_hi", full, F32R), ("bt_lo", full, F32R))
    h1_hi, h1_lo = [None] * 2, [None] * 2
    h1_hi[0], h1_lo[0] = over(r_h2, ("h1_hi0", full, F32R), ("h1_lo0", full, F32R))
    xo, = over(r_h2t, ("xo", full, F32))
    b2_bc, table, tok_f, batch_f, gb_index = over(
        r_p, ("b2_bc", [P, D], F32), ("table", [P, E, GS, 2], I32), ("tok_f", [P, E * GS], F32),
        ("batch_f", [P, 4, E * GS], F32), ("gb_index", [P, E * GS], I32))
    h1_hi[1], h1_lo[1], gb_rows, yo0, yo1 = over(
        r_tab, ("h1_hi1", full, F32R), ("h1_lo1", full, F32R), ("gb_rows", full, F32),
        ("yo0", [P, D], F32), ("yo1", [P, D], F32))
    yo = [yo0, yo1]

    stack = ExitStack()
    banks = [stack.enter_context(nc.psum_tensor(f"bank{i}", [P, 512], F32)) for i in range(8)]
    big, (s_bank, pt_bank, lg_bank, pos_bank) = banks[:4], banks[4:]
    y_bank, h_bank = banks[:4], banks[4:]

    def sem(name):
        return stack.enter_context(nc.semaphore(name))

    made = sem("made")
    ident_made = sem("ident_made")
    init_made = sem("init_made")
    cond_in, bias_in, wq_in, wk_in, wv_in, wo_in, summ_in = (sem(f"{k}_in") for k in (
        "cond", "bias", "wq", "wk", "wv", "wo", "summ"))
    wm_in = [sem(f"wm_in{i}") for i in range(2)]
    wg_in, bg_in, bo_in, bqk_in, b1_in = (sem(f"{k}_in") for k in ("wg", "bg", "bo", "bqk", "b1"))
    pro_full, pro_evac = sem("pro_full"), sem("pro_evac")
    sc_step, sc_exp, sc_ready = sem("sc_step"), sem("sc_exp"), sem("sc_ready")
    m_step, v_step, m_split, v_split = sem("m_step"), sem("v_step"), sem("m_split"), sem("v_split")
    fix_step, mod_fixed, mod_stored = sem("fix_step"), sem("mod_fixed"), sem("mod_stored")
    brow_ready = sem("brow_ready")
    vcg_in, qcg_in = sem("vcg_in"), sem("qcg_in")
    tab_in, qc_in, late_tab_in = sem("tab_in"), sem("qc_in"), sem("late_tab_in")
    gsum_stats, gsum_rstd, gsum_xn, gsum_step = (sem(f"gsum_{k}") for k in ("stats", "rstd", "xn", "step"))
    gsum_masked, gsum_negb, gsum_exp, gsum_prob = (sem(f"gsum_{k}") for k in ("masked", "negb", "exp", "prob"))
    g_split_done, g_stored, table_cleared = sem("g_split_done"), sem("g_stored"), sem("table_cleared")

    x_in = [sem(f"x_in{i}") for i in range(2)]
    xr_in = [sem(f"xr_in{i}") for i in range(2)]
    grows_in = [sem(f"grows_in{i}") for i in range(2)]
    ln1_step, ln1_ready, ln1_rstd, xn_done = (sem(k) for k in ("ln1_step", "ln1_ready", "ln1_rstd", "xn_done"))
    t1_full, ht_full, ht_hi_done, ht_split, qc_raw, qc_ready = (sem(k) for k in (
        "t1_full", "ht_full", "ht_hi_done", "ht_split", "qc_raw", "qc_ready"))
    gt_full, gt_done, u_full, u_hi_done, u_split = (sem(k) for k in (
        "gt_full", "gt_done", "u_full", "u_hi_done", "u_split"))
    s_full, mx_step, negb_ready, exp_done, prec_ready, prob_ready = (sem(k) for k in (
        "s_full", "mx_step", "negb_ready", "exp_done", "prec_ready", "prob_ready"))
    pt_full, pt_hi_done, pt_split, av_full, av_taken = (sem(k) for k in (
        "pt_full", "pt_hi_done", "pt_split", "av_full", "av_taken"))
    x2_ready, ln2_step, ln2_ready, ln2_rstd, xn2_done, h2_scaled, h2_ready = (sem(k) for k in (
        "x2_ready", "ln2_step", "ln2_ready", "ln2_rstd", "xn2_done", "h2_scaled", "h2_ready"))
    x2_stored = [sem(f"x2_stored{i}") for i in range(2)]
    h2_stored = [sem(f"h2_stored{i}") for i in range(2)]
    h2t_full, h2t_done, lg_full, route, route_exp, pos_full = (sem(k) for k in (
        "h2t_full", "h2t_done", "lg_full", "route", "route_exp", "pos_full"))
    scattered = [sem(f"scattered{i}") for i in range(2)]

    count_full, rows_counted = sem("count_full"), sem("rows_counted")
    table_in, index_step, tok_h_ready, tok_x_ready, gate_ready, gb_in, gb_gated = (sem(k) for k in (
        "table_in", "index_step", "tok_h_ready", "tok_x_ready", "gate_ready", "gb_in", "gb_gated"))
    w1_in = [sem(f"w1_in{i}") for i in range(2)]
    w2_in = [sem(f"w2_in{i}") for i in range(2)]
    w1_hi_done, w1_split, w2_hi_done, w2_split = (sem(k) for k in (
        "w1_hi_done", "w1_split", "w2_hi_done", "w2_split"))
    rows_cleared, xh_in, xo_in, b2_in = sem("rows_cleared"), sem("xh_in"), sem("xo_in"), sem("b2_in")
    bt_full, bt_hi_done, bt_split = sem("bt_full"), sem("bt_hi_done"), sem("bt_split")
    h1_full, relu_done, h1_split, g2_done = (sem(k) for k in ("h1_full", "relu_done", "h1_split", "g2_done"))
    y_full, y_taken, y_scaled, y_ready = (sem(k) for k in ("y_full", "y_taken", "y_scaled", "y_ready"))
    y_sent = [sem(f"y_sent{i}") for i in range(2)]

    sp_passed, act_passed, dve_passed, pool_passed = (sem(f"{k}_passed") for k in ("sp", "act", "dve", "pool"))

    def wait_past(eng, s, n):
        if not isinstance(n, int) or n > 0:
            eng.wait_ge(s, n)

    def stand_alone(eng, passed):
        eng.sem_inc(passed, 1)

    def chunk(k):
        return slice(k * P, (k + 1) * P)

    def batch_of(g):
        return g.n // GPB

    def split3(pe, o, a_hi, a_lo, b_hi, b_lo, start, stop):
        pe.matmul(o, a_hi, b_hi, start=start, stop=False)
        pe.matmul(o, a_hi, b_lo, start=False, stop=False)
        return pe.matmul(o, a_lo, b_hi, start=False, stop=stop)

    (SCT, BCOL, MCH, UROW, V4, UCOL, MODS, MCOL, WOT, VCH, BROW, HGT, GROW, GGT, SG, UG, PGT, TG, B1T,
     PRO_END) = (0, 1, 2, 6, 7, 8, 9, 15, 16, 20, 24, 25, 26, 27, 28, 29, 30, 31, 32, 33)
    POOL_MADE = 9
    DVE_MADE = 9

    def results_done(eng, e, b):
        if b == 0:
            wait_past(eng, g2_done, (NB - 1) * e)
        elif b == 1:
            wait_past(eng, y_full, GS * e)
        else:
            eng.wait_ge(g2_done, (NB - 1) * e + b - 1)

    block = stack.enter_context(nc.Block())

    @block.sync
    def _(sp):
        def w_rows(w):
            return w.rearrange("(c p) n -> p c n", p=P)

        def group_rows(rows, g):
            return rows[bass.ds(g.n * ROWS, ROWS), :].rearrange("(s p) d -> p s d", p=P)

        def load_x(g):
            sp.dma_start(xa[g.par][:], group_rows(x_rows, g)).then_inc(x_in[g.par], 16)

        sp.dma_start(sc_rows[:], cond).then_inc(cond_in, 16)
        for i, b in enumerate((bq, bk, bv)):
            sp.dma_start(bias_rows[KC * i:KC * (i + 1), :], b.rearrange("(c p) -> c p", p=P)).then_inc(bias_in, 16)
        sp.dma_start(wk_s[:], w_rows(wk)).then_inc(wk_in, 16)
        sp.dma_start(wq_s[:], w_rows(wq)).then_inc(wq_in, 16)
        load_x(Group(0, 0))

        def load_wmod(m):
            if m >= 2:
                sp.wait_ge(pro_full, MODS + m - 1)
            sp.dma_start(wm_s[m % 2][:], wmod[:, m * D:(m + 1) * D].rearrange("(c p) n -> p c n", p=P)) \
                .then_inc(wm_in[m % 2], 16)

        load_wmod(0)
        load_wmod(1)
        for i, b in enumerate((bq, bk)):
            sp.dma_start(bqk[:, i, :], b.rearrange("(a d) -> a d", a=1).to_broadcast([NBATCH, D])).then_inc(bqk_in, 16)
        sp.dma_start(wo_s[:], w_rows(wo)).then_inc(wo_in, 16)
        sp.dma_start(wv_s[:], w_rows(wv)).then_inc(wv_in, 16)
        sp.dma_start(g_x[:], x_rows.rearrange("(n p) d -> n p d", p=P)[:, 0, :]).then_inc(summ_in, 16)
        sp.dma_start(bo_row[:], bo.rearrange("(a d) -> a d", a=1)).then_inc(bo_in, 16)
        sp.dma_start(bg_bc[:], bg.rearrange("(a d) -> a d", a=1).to_broadcast([P, E])).then_inc(bg_in, 16)
        sp.dma_start(b1_rows[:], b1.rearrange("e (c p) -> (e c) p", p=P).rearrange("(t r) p -> r t p", r=P)) \
            .then_inc(b1_in, 16)
        sp.wait_ge(init_made, 6)
        sp.dma_start(wg_pad[:, :, 0:E], wg.rearrange("(c p) e -> p c e", p=P)).then_inc(wg_in, 16)
        sp.dma_start(table_dram.rearrange("(p a) c -> p a c", p=P), table_init[:]).then_inc(table_cleared, 16)
        for m in range(2, 6):
            load_wmod(m)
        sp.wait_ge(mod_fixed, 1)
        sp.dma_start(mod_dram, modr[:]).then_inc(mod_stored, 16)
        sp.dma_start(qc_dram, q_const[0:NBATCH, 0:1]).then_inc(mod_stored, 16)
        sp.wait_ge(mod_stored, 32)

        def spread(row, n):
            return mod_dram[:, row, :].unsqueeze(0).to_broadcast([n, NBATCH, D])

        for b in range(NBATCH):
            seg = slice(b * (NSEG // NBATCH), (b + 1) * (NSEG // NBATCH))
            sp.dma_start(g_b[seg, :], mod_dram[b:b + 1, VC, :].to_broadcast([NSEG // NBATCH, D])).then_inc(vcg_in, 16)
            sp.dma_start(q_const_g[seg, :], qc_dram[b:b + 1, :].to_broadcast([NSEG // NBATCH, 1])).then_inc(qcg_in, 16)
        sp.dma_start(vc_tab[:], spread(VC, P)).then_inc(tab_in, 16)
        sp.dma_start(qc_bc[:], qc_dram.rearrange("b a -> a b").to_broadcast([P, NBATCH])).then_inc(qc_in, 16)
        sp.wait_ge(g_split_done, 1)
        sp.dma_start(global_dram.rearrange("(n t) d -> n t d", t=3), g_split[:]).then_inc(g_stored, 16)
        sp.wait_ge(pro_evac, PRO_END)
        load_x(Group(0, 1))
        sp.dma_start(ga_tab[:], spread(GA, P)).then_inc(late_tab_in, 16)
        sp.wait_ge(g_stored, 16)
        sp.dma_start(cb_tab[:], spread(CB, P)).then_inc(late_tab_in, 16)
        sp.wait_ge(table_cleared, 16)
        sp.dma_start(sb_tab[:], spread(SB, P)).then_inc(late_tab_in, 16)

        def iteration(i, cur, prev, load2):
            if load2:
                sp.wait_ge(t1_full, 4 * i.n + 4)
                sp.wait_ge(qc_raw, 4 * i.n + 4)
                load_x(i.plus(2))
            if cur:
                wait_past(sp, av_full, 4 * i.n - 4)
                sp.dma_start(grows[i.par][0:3 * GS, :], global_dram[bass.ds(i.n * 3 * GS, 3 * GS), :]) \
                    .then_inc(grows_in[i.par], 16)
                if not isinstance(i.n, int) or i.n >= 2:
                    sp.wait_ge(xn2_done, 4 * i.n - 4)
                    stand_alone(sp, sp_passed)
                    sp.wait_ge(x2_stored[i.par], 16 * i.half)
                sp.dma_start(xr[i.par][:], group_rows(x_rows, i)).then_inc(xr_in[i.par], 16)
            if prev:
                g = i.plus(-1)
                sp.wait_ge(x2_ready, 4 * g.n + 4)
                sp.dma_start(group_rows(out_rows, g), xr[g.par][:]).then_inc(x2_stored[g.par], 16)
                sp.wait_ge(h2_ready, 4 * g.n + 4)
                sp.dma_start(group_rows(h2_dram, g), h2[g.par][:]).then_inc(h2_stored[g.par], 16)

        iteration(Group(0, 0), True, False, True)
        iteration(Group(0, 1), True, True, True)
        with sp.Fori(1, NG // 2 - 1) as half:
            for par in range(2):
                iteration(Group(half, par), True, True, True)
        for n in range(NG - 2, NG):
            iteration(Group(n // 2, n % 2), True, True, False)
        iteration(Group(NG // 2, 0), False, True, False)

        def load_w1(n, par):
            sp.dma_start(raw[2 * par][:], w1_block(n)).then_inc(w1_in[par], 16)

        def load_w2(n, par):
            sp.dma_start(raw[2 * par + 1][:], w2_block(n)).then_inc(w2_in[par], 16)

        w1_flat = w1.rearrange("e d h -> (e d) h")
        w2_flat = w2.rearrange("e h d -> (e h) d")

        def w1_block(n):
            e, b = n
            return w1_flat[bass.ds(e * D, D), b * HB:(b + 1) * HB].rearrange("(c p) h -> p c h", p=P)

        def w2_block(n):
            e, b = n
            return w2_flat[bass.ds(e * H + b * HB, HB), :].rearrange("(c p) d -> p c d", p=P)

        sp.wait_ge(s_full, NG)
        sp.wait_ge(qc_raw, 4 * NG)
        load_w1((0, 0), 0)
        load_w2((0, 0), 0)
        load_w1((0, 1), 1)
        load_w2((0, 1), 1)
        sp.wait_ge(h2_ready, 4 * NG)
        for par in range(2):
            sp.wait_ge(scattered[par], 16 * GS * (NG // 2))
        sp.dma_start(table[:], table_dram.rearrange("(e p j) c -> p e j c", p=P, j=GS)).then_inc(table_in, 16)
        sp.dma_start(b2_bc[:], b2[0:1, :].to_broadcast([P, D])).then_inc(b2_in, 16)

        def expert(e, first, last):
            for b in range(NB):
                n = e * NB + b
                ahead = (e, b + 2) if b + 2 < NB else (e + 1, b + 2 - NB)
                if not (last and b + 2 >= NB):
                    sp.wait_ge(w1_split, n + 1)
                    load_w1(ahead, b % 2)
                    sp.wait_ge(w2_split, n + 1)
                    load_w2(ahead, b % 2)
                if b == 1 and not first:
                    sp.wait_ge(y_taken, 4 * e)
                    stand_alone(sp, sp_passed)
                    sp.dma_start(b2_bc[:], b2[bass.ds(e, 1), :].to_broadcast([P, D])).then_inc(b2_in, 16)

        expert(0, True, False)
        with sp.Fori(1, E - 1) as e:
            expert(e, False, False)
        expert(E - 1, False, True)
        for par in range(2):
            sp.wait_ge(x2_stored[par], 16 * (NG // 2))
            sp.wait_ge(y_sent[par], 16 * 2 * E)

    @block.tensor
    def _(pe):
        def product(q, last):
            last.then_inc(pro_full, 1)

        def bank_free(q):
            wait_past(pe, pro_evac, q - 7)

        pe.wait_ge(ident_made, 2)
        pe.wait_ge(sc_ready, 1)
        for k in range(KC):
            last = pe.transpose(banks[SCT % 8][:, k * NBATCH:(k + 1) * NBATCH], sc_rows[:, chunk(k)],
                                ident[0:NBATCH, 0:NBATCH])
        product(SCT, last)
        pe.wait_ge(bias_in, 48)
        product(BCOL, pe.transpose(banks[BCOL % 8][:, 0:3 * KC], bias_rows[:], ident[0:3 * KC, 0:3 * KC]))
        pe.wait_ge(wk_in, 16)
        pe.wait_ge(wq_in, 16)
        for c in range(KC):
            for k in range(KC):
                last = pe.matmul(banks[(MCH + c) % 8][:, :], wq_s[:, k, chunk(c)], wk_s[:, k, :],
                                 start=(k == 0), stop=(k == KC - 1))
            product(MCH + c, last)
        pe.wait_ge(pro_evac, BCOL + 1)
        for k in range(KC):
            last = pe.matmul(banks[UROW % 8][0:1, :], bias_col[:, k:k + 1], wk_s[:, k, :],
                             start=(k == 0), stop=(k == KC - 1))
        product(UROW, last)
        for k in range(KC):
            last = pe.matmul(banks[V4 % 8][0:NBATCH, :], bk_cols[:, k, :], wq_s[:, k, :],
                             start=(k == 0), stop=(k == KC - 1))
        product(V4, last)
        pe.wait_ge(pro_evac, UROW + 1)
        bank_free(UCOL)
        for k in range(KC):
            last = pe.transpose(banks[UCOL % 8][:, k:k + 1], u_row[:, chunk(k)], ident[0:1, 0:1])
        product(UCOL, last)
        for m in range(6):
            bank_free(MODS + m)
            pe.wait_ge(wm_in[m % 2], 16 * (m // 2 + 1))
            for k in range(KC):
                last = pe.matmul(banks[(MODS + m) % 8][0:NBATCH, :], sc_t[:, k, :], wm_s[m % 2][:, k, :],
                                 start=(k == 0), stop=(k == KC - 1))
            product(MODS + m, last)
        pe.wait_ge(mod_fixed, 1)
        bank_free(MCOL)
        for i, row in enumerate((SA, CA)):
            for k in range(KC):
                at_col = (i * KC + k) * NBATCH
                last = pe.transpose(banks[MCOL % 8][:, at_col:at_col + NBATCH], modr[:, row, chunk(k)],
                                    ident[0:NBATCH, 0:NBATCH])
        product(MCOL, last)
        pe.wait_ge(wo_in, 16)
        for c in range(KC):
            bank_free(WOT + c)
            for k in range(KC):
                last = pe.transpose(banks[(WOT + c) % 8][:, chunk(k)], wo_s[:, k, chunk(c)], ident[:])
            product(WOT + c, last)
        pe.wait_ge(wv_in, 16)
        pe.wait_ge(pro_evac, WOT + KC)
        for c in range(KC):
            bank_free(VCH + c)
            for k in range(KC):
                last = pe.matmul(banks[(VCH + c) % 8][:, :], wv_s[:, k, chunk(c)], wo_t[:, k, :],
                                 start=(k == 0), stop=(k == KC - 1))
            product(VCH + c, last)

        def transpose_xn(g, first):
            pe.wait_ge(xn_done, 4 * g.n + 4)
            for k in range(KC):
                if not first:
                    pe.wait_ge(u_split, 4 * g.n - 4 + k + 1)
                for s in range(GS):
                    last = pe.transpose(big[k][:, chunk(s)], xa[g.par][:, s, chunk(k)], ident[:])
                last.then_inc(t1_full, 1)

        pe.wait_ge(pro_evac, WOT + KC)
        transpose_xn(Group(0, 0), True)
        pe.wait_ge(ht_full, KC)
        for k in range(KC):
            last = pe.matmul(banks[BROW % 8][0:1, :], bias_col[:, 2 * KC + k:2 * KC + k + 1], wo_t[:, k, :],
                             start=(k == 0), stop=(k == KC - 1))
        product(BROW, last)
        pe.wait_ge(gsum_xn, 1)
        bank_free(HGT)
        for k in range(KC):
            last = pe.transpose(banks[HGT % 8][:, k * NSEG:(k + 1) * NSEG], g_a[:, chunk(k)], ident[0:NSEG, 0:NSEG])
        product(HGT, last)
        pe.wait_ge(pro_evac, HGT + 1)
        for k in range(KC):
            last = pe.matmul(banks[GROW % 8][0:NSEG, :], hg_t[:, k, :], m_f[:, k, :],
                             start=(k == 0), stop=(k == KC - 1))
        product(GROW, last)
        pe.wait_ge(pro_evac, GROW + 1)
        for k in range(KC):
            last = pe.transpose(banks[GGT % 8][:, k * NSEG:(k + 1) * NSEG], g_x[:, chunk(k)], ident[0:NSEG, 0:NSEG])
        product(GGT, last)
        pe.wait_ge(pro_evac, GGT + 1)
        for k in range(KC):
            last = pe.matmul(banks[SG % 8][0:NSEG, 0:NSEG], gg_t[:, k, :], hg_t[:, k, :],
                             start=(k == 0), stop=(k == KC - 1))
        product(SG, last)
        for k in range(KC):
            last = pe.matmul(banks[UG % 8][0:NSEG, :], hg_t[:, k, :], vo_f[:, k, :],
                             start=(k == 0), stop=(k == KC - 1))
        product(UG, last)
        pe.wait_ge(gsum_prob, 1)
        product(PGT, pe.transpose(banks[PGT % 8][:, 0:NSEG], pg[:], ident[0:NSEG, 0:NSEG]))
        pe.wait_ge(pro_evac, PGT + 1)
        pe.wait_ge(brow_ready, 1)
        pe.matmul(banks[TG % 8][0:NSEG, :], pg_t[:], g_b[:], start=True, stop=False)
        product(TG, pe.matmul(banks[TG % 8][0:NSEG, :], one_row[:], brow[:], start=False, stop=True))
        pe.wait_ge(b1_in, 16)
        for t in range(2):
            last = pe.transpose(banks[B1T % 8][:, chunk(t)], b1_rows[:, t, :], ident[:])
        product(B1T, last)
        pe.wait_ge(pro_evac, PRO_END)
        pe.wait_ge(m_split, KC)
        pe.wait_ge(v_split, KC)
        pe.wait_ge(wg_in, 16)
        pe.wait_ge(made, POOL_MADE)

        def g_tile(g, j):
            for k in range(KC):
                if j == 0:
                    pe.wait_ge(ht_split, 4 * g.n + k + 1)
                last = split3(pe, big[j][:, :], m_hi[:, k, chunk(j)], m_lo[:, k, chunk(j)], ht_hi[:, k, :],
                              ht_lo[:, k, :], k == 0, k == KC - 1)
            last.then_inc(gt_full, 1)

        def ranks(g):
            pe.wait_ge(route, RT * g.n + 6)
            flat = onehot[:].rearrange("p s e -> p (s e)")
            pe.matmul(pos_bank[:, 0:GS * E], tri[:], flat, start=True, stop=False)
            pe.matmul(pos_bank[:, 0:GS * E].rearrange("p (s e) -> p s e", e=E), ones[:],
                      count[:].unsqueeze(1).to_broadcast([P, GS, E]), start=False, stop=False)
            for s in range(GS - 1):
                last = pe.matmul(pos_bank[:, (s + 1) * E:GS * E].rearrange("p (s e) -> p s e", e=E), ones[:],
                                 onehot[:, s:s + 1, :].to_broadcast([P, GS - 1 - s, E]),
                                 start=False, stop=(s == GS - 2))
            last.then_inc(pos_full, 1)

        def iteration(i, cur, prev, prev2, nxt, prev3):
            n = i.n
            p1, p2 = i.plus(-1), i.plus(-2)
            if cur:
                g_tile(i, 0)
                g_tile(i, 1)
            if prev2:
                pe.wait_ge(h2_ready, 4 * p2.n + 4)
                if not cur:
                    pe.wait_ge(u_split, 4 * NG)
                for k in range(KC):
                    if cur and k >= 2:
                        pe.wait_ge(gt_done, 4 * n + k - 1)
                    for s in range(GS):
                        last = pe.transpose(big[(k + 2) % 4][:, chunk(s)], h2[p2.par][:, s, chunk(k)], ident[:])
                    last.then_inc(h2t_full, 1)
            if prev3:
                ranks(i.plus(-3))
            if cur:
                if prev2:
                    pe.wait_ge(h2t_done, 4 * p2.n + 1)
                g_tile(i, 2)
            if prev:
                pe.wait_ge(prob_ready, p1.n + 1)
                for s in range(GS):
                    last = pe.transpose(pt_bank[:, chunk(s)], prob[:, s, :], ident[:])
                last.then_inc(pt_full, 1)
            if cur:
                if prev2:
                    pe.wait_ge(h2t_done, 4 * p2.n + 2)
                g_tile(i, 3)
            if prev:
                pe.wait_ge(u_split, 4 * p1.n + 4)
                pe.wait_ge(pt_split, p1.n + 1)
                pe.wait_ge(grows_in[p1.par], 16 * (p1.half + 1))
                if prev2:
                    pe.wait_ge(h2t_done, 4 * p2.n + 4)
                for s in range(GS):
                    if cur:
                        pe.wait_ge(gt_done, 4 * n + s + 1)
                    split3(pe, big[s][:, :], pt_hi[:, s, :], pt_lo[:, s, :], u_hi[:, s, :], u_lo[:, s, :], True, False)
                    pe.matmul(big[s][:, :], seg_sel[:, s, :], grows[p1.par][:], start=False, stop=True) \
                        .then_inc(av_full, 1)
            if cur:
                for s in range(GS):
                    if prev:
                        pe.wait_ge(av_taken, 4 * p1.n + s + 1)
                    else:
                        pe.wait_ge(gt_done, 4 * n + s + 1)
                    for k in range(KC):
                        last = split3(pe, big[s][:, :], ht_hi[:, k, chunk(s)], ht_lo[:, k, chunk(s)], v_hi[:, k, :],
                                      v_lo[:, k, :], k == 0, k == KC - 1)
                    last.then_inc(u_full, 1)
            if prev2:
                pe.wait_ge(h2t_done, 4 * p2.n + 4)
                wait_past(pe, route, RT * p2.n - RT + 1)
                for s in range(GS):
                    for k in range(KC):
                        last = pe.matmul(lg_bank[:, chunk(s)], h2t[:, k, chunk(s)], wg_pad[:, k, :],
                                         start=(k == 0), stop=(k == KC - 1))
                last.then_inc(lg_full, 1)
            if nxt:
                transpose_xn(i.plus(1), False)
            if cur:
                pe.wait_ge(gt_done, 4 * n + 4)
                for s in range(GS):
                    for k in range(KC):
                        last = pe.matmul(s_bank[:, chunk(s)], gt[:, k, chunk(s)], ht[i.par][:, k, chunk(s)],
                                         start=(k == 0), stop=(k == KC - 1))
                last.then_inc(s_full, 1)

        iteration(Group(0, 0), True, False, False, True, False)
        iteration(Group(0, 1), True, True, False, True, False)
        iteration(Group(1, 0), True, True, True, True, False)
        iteration(Group(1, 1), True, True, True, True, True)
        with pe.Fori(2, NG // 2 - 1) as half:
            for par in range(2):
                iteration(Group(half, par), True, True, True, True, True)
        iteration(Group(NG // 2 - 1, 0), True, True, True, True, True)
        iteration(Group(NG // 2 - 1, 1), True, True, True, False, True)
        iteration(Group(NG // 2, 0), False, True, True, False, True)
        iteration(Group(NG // 2, 1), False, False, True, False, True)
        ranks(Group(NG // 2 - 1, 1))

        def rows_of(e):
            return pe.value_load(expert_rows[0:1, bass.ds(e, 1)], min_val=0, max_val=T)

        def filled_tiles(rows, tile, passed_over=lambda: None):
            for j in range(GS - 1, 0, -1):
                with pe.If(rows > j * P):
                    tile(j)
                with pe.Else():
                    passed_over()
            tile(0)

        def gathered_transpose(e, rows):
            pe.wait_ge(xh_in, 16 * GS * (e + 1))
            wait_past(pe, relu_done, 4 * NB * e)

            def tile(j):
                for k in range(KC):
                    last = pe.transpose(h_bank[k][:, chunk(j)], xh[:, j, chunk(k)], ident[:])
                    if j == 0:
                        last.then_inc(bt_full, 1)

            filled_tiles(rows, tile)

        def hidden(e, b, rows):
            n = NB * e + b
            if b == 0:
                pe.wait_ge(bt_split, 4 * e + 4)
            pe.wait_ge(w1_split, n + 1)

            def product(slots):
                for j in range(HC):
                    if b > 0:
                        pe.wait_ge(relu_done, 4 * n + j - 3)
                    for k in range(KC):
                        last = split3(pe, h_bank[j][:, 0:slots], w1_hi[b % 2][:, k, chunk(j)],
                                      w1_lo[b % 2][:, k, chunk(j)], bt_hi[:, k, 0:slots], bt_lo[:, k, 0:slots],
                                      k == 0, k == KC - 1)
                    last.then_inc(h1_full, 1)

            with pe.If(rows > 3 * P):
                product(4 * P)
            with pe.Else():
                with pe.If(rows > 2 * P):
                    product(3 * P)
                with pe.Else():
                    product(2 * P)

        def results(e, b, rows):
            n = NB * e + b
            pe.wait_ge(h1_split, 4 * n + 4)
            pe.wait_ge(w2_split, n + 1)
            if b == 0:
                wait_past(pe, y_taken, 4 * e)

            def tile(j):
                for c in range(HC):
                    last = split3(pe, y_bank[j][:, :], h1_hi[b % 2][:, c, chunk(j)], h1_lo[b % 2][:, c, chunk(j)],
                                  w2_hi[b % 2][:, c, :], w2_lo[b % 2][:, c, :], b == 0 and c == 0,
                                  b == NB - 1 and c == HC - 1)
                if b == NB - 1:
                    last.then_inc(y_full, 1)
                elif j == 0:
                    last.then_inc(g2_done, 1)

            def passed_over():
                if b == NB - 1:
                    pe.sem_inc(y_full, 1)

            filled_tiles(rows, tile, passed_over)

        def expert(e, first, last):
            rows = rows_of(e)
            for b in range(NB):
                hidden(e, b, rows)
                if b == NB - 1 and not last:
                    gathered_transpose(e + 1, rows_of(e + 1))
                if b > 0:
                    results(e, b - 1, rows)
                elif not first:
                    results(e - 1, NB - 1, rows_of(e - 1))

        pe.wait_ge(pos_full, NG)
        pe.wait_ge(route, RT * NG)
        pe.matmul(pos_bank[0:1, 0:E], ones[:, 0:1], count[:], start=True, stop=True).then_inc(count_full, 1)
        pe.wait_ge(rows_counted, 1)
        gathered_transpose(0, rows_of(0))
        expert(0, True, False)
        with pe.Fori(1, E - 1) as e:
            expert(e, False, False)
        expert(E - 1, False, True)
        results(E - 1, NB - 1, rows_of(E - 1))

    @block.scalar
    def _(act):
        def copy_out(q, dst, src, scale=1.0):
            act.wait_ge(pro_full, q + 1)
            act.activation(dst, src, ACT.Copy, scale=scale).then_inc(pro_evac, 1)

        act.wait_ge(cond_in, 16)
        act.activation(sc_tmp[:], sc_rows[:], ACT.Exp, scale=-1.0).then_inc(sc_exp, 1)
        copy_out(SCT, sc_t[:].rearrange("p k b -> p (k b)"), banks[SCT % 8][:, 0:KC * NBATCH])
        act.wait_ge(pro_full, BCOL + 1)
        act.activation(bias_col[:], banks[BCOL % 8][:, 0:3 * KC], ACT.Copy)
        act.activation(bk_cols[:], banks[BCOL % 8][:, KC:2 * KC].unsqueeze(2).to_broadcast([P, KC, NBATCH]),
                       ACT.Copy).then_inc(pro_evac, 1)
        for c in range(KC):
            copy_out(MCH + c, m_f[:, c, :], banks[(MCH + c) % 8][:, :])
        copy_out(UROW, u_row[:], banks[UROW % 8][0:1, :])
        copy_out(V4, modr[:, VC, :], banks[V4 % 8][0:NBATCH, :])
        copy_out(UCOL, u_col[:], banks[UCOL % 8][:, 0:KC])
        for m in range(6):
            copy_out(MODS + m, modr[:, m, :], banks[(MODS + m) % 8][0:NBATCH, :])
        copy_out(MCOL, mod_col[:].rearrange("p i k b -> p (i k b)"), banks[MCOL % 8][:, 0:2 * KC * NBATCH])
        for c in range(KC):
            copy_out(WOT + c, wo_t[:, c, :], banks[(WOT + c) % 8][:, :])
        act.wait_ge(gsum_rstd, 2)
        act.activation(g_a[:], g_x[:], ACT.Identity, bias=NR2[0:NSEG, 0:1], scale=RS2[0:NSEG, 0:1]).then_inc(gsum_xn, 1)
        for c in range(KC):
            copy_out(VCH + c, vo_f[:, c, :], banks[(VCH + c) % 8][:, :])

        def modulate(g):
            for k in range(KC):
                act.wait_ge(t1_full, 4 * g.n + k + 1)
                act.wait_ge(pro_evac, MCOL + 1)
                act.activation(ht[g.par][:, k, :], big[k][:, :], ACT.Identity,
                               bias=mod_col[:, 0, k, bass.ds(batch_of(g), 1)],
                               scale=mod_col[:, 1, k, bass.ds(batch_of(g), 1)]).then_inc(ht_full, 1)

        modulate(Group(0, 0))
        copy_out(BROW, brow[:], banks[BROW % 8][0:1, :], scale=2.0)
        act.wait_ge(pro_full, HGT + 1)
        for k in range(KC):
            for b in range(NBATCH):
                seg = slice(b * (NSEG // NBATCH), (b + 1) * (NSEG // NBATCH))
                ins = act.activation(hg_t[:, k, seg], banks[HGT % 8][:, k * NSEG + seg.start:k * NSEG + seg.stop],
                                     ACT.Identity, bias=mod_col[:, 0, k, b:b + 1], scale=mod_col[:, 1, k, b:b + 1])
        ins.then_inc(pro_evac, 1)
        copy_out(GROW, g_x[:], banks[GROW % 8][0:NSEG, :])
        act.wait_ge(pro_full, GGT + 1)
        for k in range(KC):
            ins = act.activation(gg_t[:, k, :], banks[GGT % 8][:, k * NSEG:(k + 1) * NSEG], ACT.Identity,
                                 bias=u_col[:, k:k + 1])
        ins.then_inc(pro_evac, 1)
        copy_out(SG, sg[:], banks[SG % 8][0:NSEG, 0:NSEG])
        act.wait_ge(gsum_step, 4)
        copy_out(UG, g_b[:], banks[UG % 8][0:NSEG, :])
        act.wait_ge(gsum_negb, 1)
        act.activation(pg[:, 0:NSEG], sg[:], ACT.Exp, bias=NEGB[0:NSEG, 0:1], scale=SCALE,
                       accum_out=PSUMS[0:NSEG, 0:1]).then_inc(gsum_exp, 1)
        copy_out(PGT, pg_t[:], banks[PGT % 8][0:NSEG, 0:NSEG])
        copy_out(TG, g_a[:], banks[TG % 8][0:NSEG, :])
        copy_out(B1T, b1_col[:], banks[B1T % 8][:, 0:2 * P])

        def iteration(i, cur, prev, prev2, nxt, prev3):
            n = i.n
            p1, p2 = i.plus(-1), i.plus(-2)

            def add_u(j):
                act.wait_ge(gt_full, 4 * n + j + 1)
                act.activation(gt[:, j, :], big[j][:, :], ACT.Identity, bias=u_col[:, j:j + 1]).then_inc(gt_done, 1)

            def empty_u(s):
                act.wait_ge(u_full, 4 * n + s + 1)
                act.activation(u_hi[:, s, :], big[s][:, :], ACT.Copy).then_inc(u_hi_done, 1)

            def normalise2(s):
                act.activation(h2[p1.par][:, s, :], xr[p1.par][:, s, :], ACT.Identity, bias=NR2[:, s:s + 1],
                               scale=RS2[:, s:s + 1]).then_inc(xn2_done, 1)

            if prev:
                act.wait_ge(negb_ready, p1.n + 1)
                for s in range(GS):
                    act.activation(prob[:, s, :], s_bank[:, chunk(s)], ACT.Exp, bias=NEGB[:, s:s + 1], scale=SCALE,
                                   accum_out=PSUMS[:, s:s + 1]).then_inc(exp_done, 1)
            if prev3:
                p3 = i.plus(-3)
                act.wait_ge(route, RT * p3.n + 3)
                act.activation(lg_e[:], lg_d[:], ACT.Exp).then_inc(route_exp, 1)
            if cur:
                add_u(0)
                add_u(1)
            if prev2:
                for k in range(KC):
                    act.wait_ge(h2t_full, 4 * p2.n + k + 1)
                    act.activation(h2t[:, k, :], big[(k + 2) % 4][:, :], ACT.Copy).then_inc(h2t_done, 1)
            if cur:
                add_u(2)
            if prev:
                act.wait_ge(pt_full, p1.n + 1)
                act.activation(pt_hi[:].rearrange("p s t -> p (s t)"), pt_bank[:, :], ACT.Copy).then_inc(pt_hi_done, 1)
            if cur:
                add_u(3)
                empty_u(0)
                empty_u(1)
                empty_u(2)
            if prev:
                act.wait_ge(ln2_rstd, 2 * p1.n + 2)
                normalise2(0)
                normalise2(1)
                normalise2(2)
            if cur:
                empty_u(3)
            if prev:
                normalise2(3)
            if nxt:
                modulate(i.plus(1))

        iteration(Group(0, 0), True, False, False, True, False)
        iteration(Group(0, 1), True, True, False, True, False)
        iteration(Group(1, 0), True, True, True, True, False)
        iteration(Group(1, 1), True, True, True, True, True)
        with act.Fori(2, NG // 2 - 1) as half:
            for par in range(2):
                iteration(Group(half, par), True, True, True, True, True)
        iteration(Group(NG // 2 - 1, 0), True, True, True, True, True)
        iteration(Group(NG // 2 - 1, 1), True, True, True, False, True)
        iteration(Group(NG // 2, 0), False, True, True, False, True)
        iteration(Group(NG // 2, 1), False, False, True, False, True)
        iteration(Group(NG // 2 + 1, 0), False, False, False, False, True)

        def w2_high(n, e, b):
            act.wait_ge(w2_in[b % 2], 16 * (NB // 2 * e + b // 2 + 1))
            results_done(act, e, b)
            act.activation(w2_hi[b % 2][:], raw[2 * (b % 2) + 1][:], ACT.Copy).then_inc(w2_hi_done, 1)

        def relu(e, b, j):
            n = NB * e + b
            act.wait_ge(h1_full, 4 * n + j + 1)
            if j == 0:
                results_done(act, e, b)
            wait_past(act, h1_split, 4 * n + j - 3)
            stand_alone(act, act_passed)
            bias = b1_col[:, bass.ds(e * (H // P) + b * HC + j, 1)]
            act.activation(h1_hi[b % 2][:, j, :], h_bank[j][:, :], ACT.Relu, bias=bias)
            act.activation(h1_f[:, j, :], h_bank[j][:, :], ACT.Relu, bias=bias).then_inc(relu_done, 1)

        def gate_rows(e):
            act.wait_ge(gate_ready, e + 1)
            act.wait_ge(gb_in, 16 * GS * (e + 1))
            for j in range(GS):
                act.activation(gb_rows[:, j, :], gb_rows[:, j, :], ACT.Copy, scale=gate_x[:, j:j + 1]) \
                    .then_inc(gb_gated, 1)

        def rows_high(e):
            for k in range(KC):
                act.wait_ge(bt_full, 4 * e + k + 1)
                act.activation(bt_hi[:, k, :], h_bank[k][:, :], ACT.Copy).then_inc(bt_hi_done, 1)

        rows_high(0)

        def expert(e, first, last):
            for b in range(NB):
                n = NB * e + b
                relu(e, b, 0)
                relu(e, b, 1)
                relu(e, b, 2)
                relu(e, b, 3)
                w2_high(n, e, b)
                if b == 0 and not first:
                    gate_rows(e - 1)
            if not last:
                rows_high(e + 1)

        expert(0, True, False)
        with act.Fori(1, E - 1) as e:
            expert(e, False, False)
        expert(E - 1, False, True)
        gate_rows(E - 1)

    @block.vector
    def _(dve):
        dve.memset(table_init[:, :, 0:1], NO_TOKEN).then_inc(init_made, 1)
        dve.memset(table_init[:, :, 1:2], 0).then_inc(init_made, 1)
        dve.memset(wg_pad[:], 0.0).then_inc(init_made, 1)
        dve.memset(count[:], 0.0).then_inc(init_made, 1)
        dve.memset(grows[0][:], 0.0).then_inc(init_made, 1)
        dve.memset(grows[1][:], 0.0).then_inc(init_made, 1)
        dve.memset(pg[:], 0.0).then_inc(init_made, 1)
        dve.memset(half_neg[:], -0.5).then_inc(init_made, 1)
        dve.memset(one_row[:], 1.0).then_inc(init_made, 1)
        dve.wait_ge(init_made, DVE_MADE)
        dve.wait_ge(sc_exp, 1)
        dve.tensor_scalar(sc_tmp[:], sc_tmp[:], 1.0, None, ALU.add).then_inc(sc_step, 1)
        dve.wait_ge(sc_step, 1)
        dve.reciprocal(sc_tmp[:], sc_tmp[:]).then_inc(sc_step, 1)
        dve.wait_ge(sc_step, 2)
        dve.tensor_tensor(sc_rows[:], sc_rows[:], sc_tmp[:], ALU.mult).then_inc(sc_ready, 1)

        def layer_stats(g, rows, step, ready, per_step, st, mvt, ve, mn, used, parts=P, segs=GS):
            used()
            for s in range(segs):
                dve.bn_stats(st[0:parts, s, :], rows[:, s, :]).then_inc(step, 1)
            dve.wait_ge(step, per_step * g + segs)
            stand_alone(dve, dve_passed)
            for s in range(segs):
                dve.bn_aggr(mvt[0:parts, s, :], st[0:parts, s, :]).then_inc(step, 1)
            dve.wait_ge(step, per_step * g + 2 * segs)
            dve.tensor_scalar(ve[0:parts, 0:segs], mvt[0:parts, 0:segs, 1], EPS, None, ALU.add).then_inc(ready, 1)
            dve.tensor_scalar(mn[0:parts, 0:segs], mvt[0:parts, 0:segs, 0], -1.0, None, ALU.mult).then_inc(ready, 1)

        def stats1(g):
            dve.wait_ge(x_in[g.par], 16 * (g.half + 1))
            layer_stats(g.n, xa[g.par], ln1_step, ln1_ready, 8, stats[0], mv[0], VE1, MN1,
                        lambda: wait_past(dve, xn_done, 4 * g.n))

        def split_weights(q, src, hi, lo, done, step):
            for c in range(KC):
                dve.wait_ge(pro_evac, q + c + 1)
                dve.tensor_copy(hi[:, c, :], src[:, c, :]).then_inc(step, 1)
                dve.wait_ge(step, c + 1)
                dve.tensor_tensor(lo[:, c, :], src[:, c, :], hi[:, c, :].bitcast(F32), ALU.subtract).then_inc(done, 1)

        stats1(Group(0, 0))
        split_weights(MCH, m_f, m_hi, m_lo, m_split, m_step)
        fix = [0]

        def link(ins):
            fix[0] += 1
            ins.then_inc(fix_step, 1)
            dve.wait_ge(fix_step, fix[0])

        dve.wait_ge(pro_evac, V4 + 1)
        dve.wait_ge(bqk_in, 32)
        link(dve.scalar_tensor_tensor(out=sc_tmp[:], in0=bqk[:, 0, :], scalar=1.0, in1=bqk[:, 1, :], op0=ALU.mult,
                                      op1=ALU.mult, accum_out=q_const[0:NBATCH, 1:2]))
        dve.wait_ge(pro_evac, MODS + 2)
        link(dve.scalar_tensor_tensor(out=sc_tmp[:], in0=modr[:, VC, :], scalar=1.0, in1=modr[:, SA, :], op0=ALU.mult,
                                      op1=ALU.mult, accum_out=q_const[0:NBATCH, 2:3]))
        link(dve.tensor_tensor(q_const[0:NBATCH, 0:1], q_const[0:NBATCH, 1:2], q_const[0:NBATCH, 2:3], ALU.add))
        link(dve.tensor_scalar(modr[:, CA, :], modr[:, CA, :], 1.0, None, ALU.add))
        link(dve.tensor_tensor(modr[:, VC, :], modr[:, VC, :], modr[:, CA, :], ALU.mult))
        for row in (GA, GB):
            dve.wait_ge(pro_evac, MODS + row + 1)
            link(dve.tensor_scalar(sc_tmp[:], modr[:, row, :], 0.0, 2.0, ALU.is_ge, ALU.mult))
            link(dve.tensor_scalar(sc_tmp[:], sc_tmp[:], -1.0, None, ALU.add))
            link(dve.tensor_tensor(modr[:, row, :], modr[:, row, :], sc_tmp[:], ALU.mult))
            link(dve.scalar_tensor_tensor(out=modr[:, row, :], in0=modr[:, row, :], scalar=GATE_FLOOR, in1=sc_tmp[:],
                                          op0=ALU.max, op1=ALU.mult))
        dve.tensor_scalar(modr[:, CB, :], modr[:, CB, :], 1.0, None, ALU.add).then_inc(mod_fixed, 1)
        dve.wait_ge(summ_in, 16)
        layer_stats(0, g_x[:].unsqueeze(1), gsum_step, gsum_stats, 0, stats[1], mv[1], VE2, MN2, lambda: None, NSEG, 1)
        dve.wait_ge(gsum_xn, 1)
        dve.wait_ge(vcg_in, 16 * NBATCH)
        dve.scalar_tensor_tensor(out=g_c[:], in0=g_a[:], scalar=1.0, in1=g_b[:], op0=ALU.mult, op1=ALU.mult,
                                 accum_out=q_const[0:NSEG, 3:4]).then_inc(gsum_step, 1)
        dve.wait_ge(gsum_step, 3)
        dve.wait_ge(qcg_in, 16 * NBATCH)
        dve.tensor_scalar(q_const[0:NSEG, 3:4], q_const[0:NSEG, 3:4], q_const_g[:, 0:1], SCALE, ALU.add, ALU.mult) \
            .then_inc(gsum_step, 1)
        split_weights(VCH, vo_f, v_hi, v_lo, v_split, v_step)

        def split_rows(g):
            for k in range(KC):
                dve.wait_ge(ht_full, 4 * g.n + k + 1)
                dve.tensor_copy(ht_hi[:, k, :], ht[g.par][:, k, :]).then_inc(ht_hi_done, 1)
                dve.wait_ge(ht_hi_done, 4 * g.n + k + 1)
                dve.tensor_tensor(ht_lo[:, k, :], ht[g.par][:, k, :], ht_hi[:, k, :].bitcast(F32), ALU.subtract) \
                    .then_inc(ht_split, 1)

        split_rows(Group(0, 0))
        dve.wait_ge(pro_evac, BROW + 1)
        dve.wait_ge(bo_in, 16)
        dve.tensor_tensor(brow[:], brow[:], bo_row[:], ALU.add).then_inc(brow_ready, 1)
        dve.wait_ge(gsum_masked, 2)
        dve.reduce_max(MX[0:NSEG, 0:1], sg[:], AX_X).then_inc(gsum_step, 1)
        dve.wait_ge(gsum_step, 5)
        dve.scalar_tensor_tensor(out=MXC[0:NSEG, 0:1], in0=MX[0:NSEG, 0:1], scalar=SCALE, in1=q_const[0:NSEG, 3:4],
                                 op0=ALU.mult, op1=ALU.add).then_inc(gsum_step, 1)
        dve.wait_ge(gsum_step, 6)
        dve.tensor_tensor(NEGB[0:NSEG, 0:1], q_const[0:NSEG, 3:4], MXC[0:NSEG, 0:1], ALU.subtract).then_inc(gsum_negb, 1)
        dve.wait_ge(gsum_exp, 1)
        dve.reciprocal(PREC[0:NSEG, 0:1], PSUMS[0:NSEG, 0:1]).then_inc(gsum_step, 1)
        dve.wait_ge(gsum_step, 7)
        dve.tensor_scalar(pg[:, 0:NSEG], pg[:, 0:NSEG], PREC[0:NSEG, 0:1], None, ALU.mult).then_inc(gsum_prob, 1)
        dve.wait_ge(pro_evac, TG + 1)
        dve.tensor_copy(g_split[:, 0, :], g_a[:]).then_inc(gsum_step, 1)
        dve.wait_ge(gsum_step, 8)
        dve.tensor_tensor(g_x[:], g_a[:], g_split[:, 0, :], ALU.subtract).then_inc(gsum_step, 1)
        dve.wait_ge(gsum_step, 9)
        dve.tensor_copy(g_split[:, 1, :], g_x[:]).then_inc(gsum_step, 1)
        dve.wait_ge(gsum_step, 10)
        dve.tensor_tensor(g_split[:, 2, :], g_x[:], g_split[:, 1, :], ALU.subtract).then_inc(g_split_done, 1)
        dve.wait_ge(pro_evac, PRO_END)
        dve.wait_ge(tab_in, 16)
        dve.wait_ge(qc_in, 16)
        dve.wait_ge(bg_in, 16)
        dve.wait_ge(made, POOL_MADE)

        def query_const(g):
            b = batch_of(g)
            for s in range(GS):
                if s > 0:
                    dve.wait_ge(qc_raw, 4 * g.n + s)
                dve.scalar_tensor_tensor(out=qc_junk, in0=xa[g.par][:, s, :], scalar=1.0,
                                         in1=vc_tab[:, bass.ds(b, 1), :].rearrange("p b d -> p (b d)"), op0=ALU.mult,
                                         op1=ALU.mult, accum_out=QRAW[:, s:s + 1]).then_inc(qc_raw, 1)
            dve.wait_ge(qc_raw, 4 * g.n + 4)
            dve.tensor_scalar(QCS2[g.par], QRAW, qc_bc[:, bass.ds(b, 1)], SCALE, ALU.add, ALU.mult) \
                .then_inc(qc_ready, 1)

        dve.wait_ge(g_split_done, 1)
        tok4 = [P, GS, E]

        def route_logits(g):
            r = RT * g.n
            dve.wait_ge(lg_full, g.n + 1)
            dve.tensor_tensor(lg[:], lg_bank[:, :].rearrange("p (s c) -> p s c", c=P)[:, :, 0:E],
                              bg_bc[:].unsqueeze(1).to_broadcast(tok4), ALU.add).then_inc(route, 1)
            dve.wait_ge(route, r + 1)
            dve.reduce_max(LG_MX, lg[:], AX_X).then_inc(route, 1)
            dve.wait_ge(route, r + 2)
            dve.tensor_tensor(lg_d[:], lg[:], LG_MX.unsqueeze(2).to_broadcast(tok4), ALU.subtract).then_inc(route, 1)
            dve.wait_ge(route, r + 3)
            dve.scalar_tensor_tensor(out=lg_v[:], in0=lg_d[:], scalar=0.0, in1=eidx[:], op0=ALU.is_ge,
                                     op1=ALU.mult).then_inc(route, 1)
            dve.wait_ge(route, r + 4)
            dve.tensor_reduce(V_MIN, lg_v[:], AX_X, ALU.min).then_inc(route, 1)
            dve.wait_ge(route, r + 5)
            dve.tensor_tensor(onehot[:], lg_v[:], V_MIN.unsqueeze(2).to_broadcast(tok4), ALU.is_equal) \
                .then_inc(route, 1)

        def route_slots(g):
            r = RT * g.n
            dve.wait_ge(pos_full, g.n + 1)
            dve.wait_ge(route, r + 6)
            dve.tensor_tensor(lg_r[:], pos_bank[:, 0:GS * E].rearrange("p (s e) -> p s e", e=E), onehot[:], ALU.mult) \
                .then_inc(route, 1)
            dve.wait_ge(route, r + 7)
            dve.reduce_sum(RANK, lg_r[:], AX_X).then_inc(route, 1)
            dve.wait_ge(route, r + 8)
            dve.tensor_scalar(OVER, RANK, float(CAP), float(NO_TOKEN), ALU.is_ge, ALU.mult).then_inc(route, 1)
            dve.tensor_tensor(over_tile[:], RANK.unsqueeze(2).to_broadcast([P, GS, GS - 1]), tile_ends[:], ALU.is_ge) \
                .then_inc(route, 1)
            dve.wait_ge(route, r + 9)
            dve.scalar_tensor_tensor(out=SLOT_A, in0=RANK, scalar=float(GS), in1=OVER, op0=ALU.mult, op1=ALU.add) \
                .then_inc(route, 1)
            dve.wait_ge(route, r + 10)
            dve.reduce_sum(TILE, over_tile[:], AX_X).then_inc(route, 1)
            dve.wait_ge(route, r + 11)
            dve.scalar_tensor_tensor(out=SLOT_B, in0=V_MIN, scalar=float(CAP), in1=SLOT_A, op0=ALU.mult, op1=ALU.add) \
                .then_inc(route, 1)
            dve.wait_ge(route, r + 13)
            dve.scalar_tensor_tensor(out=SLOT_A, in0=TILE, scalar=1.0 - GS * P, in1=SLOT_B, op0=ALU.mult, op1=ALU.add) \
                .then_inc(route, 1)
            dve.wait_ge(route, r + 14)
            wait_past(dve, scattered[g.par], 16 * GS * g.half)
            dve.tensor_scalar(slot_i[g.par][:], SLOT_A, float(E * CAP), None, ALU.add).then_inc(route, 1)
            dve.tensor_reduce(osum[:], onehot[:].rearrange("p s e -> p e s"), AX_X, ALU.add).then_inc(route, 1)
            dve.wait_ge(route, r + 16)
            dve.tensor_tensor(count[:], count[:], osum[:], ALU.add).then_inc(route, 1)
            dve.wait_ge(route_exp, g.n + 1)
            dve.reduce_sum(LG_SUM, lg_e[:], AX_X).then_inc(route, 1)
            dve.wait_ge(route, r + 18)
            dve.reciprocal(pay[g.par][:, :, 1].bitcast(F32), LG_SUM).then_inc(route, 1)
            dve.tensor_copy(pay[g.par][:, :, 0], tokids[:, bass.ds(g.n * GS, GS)]).then_inc(route, 1)

        def iteration(i, cur, prev, prev2, nxt, prev3):
            n = i.n
            p1, p2, p3 = i.plus(-1), i.plus(-2), i.plus(-3)
            if prev:
                dve.wait_ge(s_full, p1.n + 1)
                dve.reduce_max(MX, s_bank[:, :].rearrange("p (s t) -> p s t", t=P), AX_X).then_inc(mx_step, 1)
                dve.wait_ge(mx_step, 2 * p1.n + 1)
                dve.wait_ge(qc_ready, p1.n + 1)
                dve.scalar_tensor_tensor(out=MXC, in0=MX, scalar=SCALE, in1=QCS2[p1.par], op0=ALU.mult, op1=ALU.add) \
                    .then_inc(mx_step, 1)
                dve.wait_ge(mx_step, 2 * p1.n + 2)
                dve.tensor_tensor(NEGB, QCS2[p1.par], MXC, ALU.subtract).then_inc(negb_ready, 1)
            if prev3:
                route_logits(p3)
            if prev:
                dve.wait_ge(exp_done, 4 * p1.n + 4)
                dve.reciprocal(PREC, PSUMS).then_inc(prec_ready, 1)
                dve.wait_ge(prec_ready, p1.n + 1)
                dve.tensor_tensor(prob[:], prob[:], PREC.unsqueeze(2).to_broadcast([P, GS, P]), ALU.mult) \
                    .then_inc(prob_ready, 1)
            if nxt:
                stats1(i.plus(1))
            if prev3:
                route_slots(p3)
            if prev:
                dve.wait_ge(pt_hi_done, p1.n + 1)
                dve.tensor_tensor(pt_lo[:].rearrange("p s t -> p (s t)"), pt_bank[:, :],
                                  pt_hi[:].rearrange("p s t -> p (s t)").bitcast(F32), ALU.subtract).then_inc(pt_split, 1)
                if isinstance(n, int) and n == 1:
                    dve.wait_ge(late_tab_in, 48)
                if not isinstance(n, int) or n >= 3:
                    dve.wait_ge(h2_stored[p1.par], 16 * p1.half)
                dve.wait_ge(xr_in[p1.par], 16 * (p1.half + 1))
                for s in range(GS):
                    dve.wait_ge(av_full, 4 * p1.n + s + 1)
                    dve.tensor_tensor(h2[p1.par][:, s, :], big[s][:, :],
                                      ga_tab[:, bass.ds(batch_of(p1), 1), :].rearrange("p b d -> p (b d)"), ALU.mult) \
                        .then_inc(av_taken, 1)
                    dve.wait_ge(av_taken, 4 * p1.n + s + 1)
                    dve.tensor_tensor(xr[p1.par][:, s, :], xr[p1.par][:, s, :], h2[p1.par][:, s, :], ALU.add) \
                        .then_inc(x2_ready, 1)
                dve.wait_ge(x2_ready, 4 * p1.n + 4)
                layer_stats(p1.n, xr[p1.par], ln2_step, ln2_ready, 8, stats[1], mv[1], VE2, MN2,
                            lambda: wait_past(dve, xn2_done, 4 * p1.n))
            if cur:
                for s in range(GS):
                    if s == 2:
                        query_const(i)
                    dve.wait_ge(u_hi_done, 4 * n + s + 1)
                    dve.tensor_tensor(u_lo[:, s, :], big[s][:, :], u_hi[:, s, :].bitcast(F32), ALU.subtract) \
                        .then_inc(u_split, 1)
            if nxt:
                split_rows(i.plus(1))

        iteration(Group(0, 0), True, False, False, True, False)
        iteration(Group(0, 1), True, True, False, True, False)
        iteration(Group(1, 0), True, True, True, True, False)
        iteration(Group(1, 1), True, True, True, True, True)
        iteration(Group(2, 0), True, True, True, True, True)
        iteration(Group(2, 1), True, True, True, True, True)
        with dve.Fori(3, NG // 2 - 1) as half:
            for par in range(2):
                iteration(Group(half, par), True, True, True, True, True)
        iteration(Group(NG // 2 - 1, 0), True, True, True, True, True)
        iteration(Group(NG // 2 - 1, 1), True, True, True, False, True)
        iteration(Group(NG // 2, 0), False, True, True, False, True)
        iteration(Group(NG // 2, 1), False, False, True, False, True)
        iteration(Group(NG // 2 + 1, 0), False, False, False, False, True)

        def split_w1(n, e, b):
            dve.wait_ge(w1_in[b % 2], 16 * (NB // 2 * e + b // 2 + 1))
            wait_past(dve, h1_full, 4 * n - 4)
            dve.tensor_copy(w1_hi[b % 2][:], raw[2 * (b % 2)][:]).then_inc(w1_hi_done, 1)
            dve.wait_ge(w1_hi_done, n + 1)
            dve.tensor_tensor(w1_lo[b % 2][:], raw[2 * (b % 2)][:], w1_hi[b % 2][:].bitcast(F32), ALU.subtract) \
                .then_inc(w1_split, 1)

        def w2_low(n, b):
            dve.wait_ge(w2_hi_done, n + 1)
            dve.tensor_tensor(w2_lo[b % 2][:], raw[2 * (b % 2) + 1][:], w2_hi[b % 2][:].bitcast(F32), ALU.subtract) \
                .then_inc(w2_split, 1)

        def split_hidden(e, b, j):
            n = NB * e + b
            dve.wait_ge(relu_done, 4 * n + j + 1)
            if j == 0:
                results_done(dve, e, b)
            dve.tensor_tensor(h1_lo[b % 2][:, j, :], h1_f[:, j, :], h1_hi[b % 2][:, j, :].bitcast(F32), ALU.subtract) \
                .then_inc(h1_split, 1)

        def rows_low(e):
            for k in range(KC):
                dve.wait_ge(bt_hi_done, 4 * e + k + 1)
                dve.tensor_tensor(bt_lo[:, k, :], h_bank[k][:, :], bt_hi[:, k, :].bitcast(F32), ALU.subtract) \
                    .then_inc(bt_split, 1)

        def result_rows(e):
            for i in range(GS):
                q, j = 4 * e + i, GS - 1 - i
                if i == 0:
                    dve.wait_ge(b2_in, 16 * (e + 1))
                dve.wait_ge(y_full, q + 1)
                wait_past(dve, y_sent[i % 2], 16 * (2 * e + i // 2))
                dve.tensor_tensor(yo[i % 2][:], y_bank[j][:, :], b2_bc[:], ALU.add).then_inc(y_taken, 1)

        dve.wait_ge(count_full, 1)
        dve.tensor_copy(expert_rows[:], pos_bank[0:1, 0:E]).then_inc(rows_counted, 1)
        dve.memset(xh[:], 0.0).then_inc(rows_cleared, 1)
        dve.memset(xo[:], 0.0).then_inc(rows_cleared, 1)
        dve.memset(gb_rows[:], 0.0).then_inc(rows_cleared, 1)
        split_w1(0, 0, 0)
        dve.wait_ge(table_in, 16)
        tok = table[:].rearrange("p e j c -> p (e j) c")
        dve.tensor_copy(tok_h[:], tok[:, 0:GS, 0]).then_inc(tok_h_ready, 1)
        dve.tensor_copy(tok_f[:], tok[:, :, 0]).then_inc(index_step, 1)
        dve.wait_ge(index_step, 1)
        dve.tensor_scalar(batch_f[:, 0, :], tok_f[:], float(L), None, ALU.is_ge).then_inc(index_step, 1)
        for b in range(2, NBATCH + 1):
            dve.wait_ge(index_step, b)
            dve.scalar_tensor_tensor(out=batch_f[:, b - 1, :], in0=tok_f[:], scalar=float(L * b),
                                     in1=batch_f[:, b - 2, :], op0=ALU.is_ge, op1=ALU.add).then_inc(index_step, 1)
        dve.wait_ge(index_step, NBATCH + 1)
        dve.tensor_scalar(gb_index[:], batch_f[:, NBATCH - 1, :], 7.0, float(GB), ALU.mult, ALU.add) \
            .then_inc(index_step, 1)
        dve.wait_ge(index_step, NBATCH + 2)
        rows_low(0)

        def expert(e, first, last):
            for b in range(NB):
                n = NB * e + b
                if b == 0 and not last:
                    dve.wait_ge(xh_in, 16 * GS * (e + 1))
                    stand_alone(dve, dve_passed)
                    dve.tensor_copy(tok_h[:], tok[:, bass.ds(GS * (e + 1), GS), 0]).then_inc(tok_h_ready, 1)
                split_hidden(e, b, 0)
                if b + 1 < NB:
                    split_w1(n + 1, e, b + 1)
                elif not last:
                    split_w1(n + 1, e + 1, 0)
                for j in range(1, HC):
                    split_hidden(e, b, j)
                w2_low(n, b)
                if b == 0 and not first:
                    result_rows(e - 1)
                if b == 2:
                    if not first:
                        for par in range(2):
                            dve.wait_ge(y_sent[par], 32 * e)
                        dve.wait_ge(gb_gated, 4 * e)
                        stand_alone(dve, dve_passed)
                    dve.tensor_copy(tok_x[:], tok[:, bass.ds(GS * e, GS), 0]).then_inc(tok_x_ready, 1)
                    dve.tensor_copy(tok_g[:], gb_index[:, bass.ds(GS * e, GS)]).then_inc(tok_x_ready, 1)
                    dve.tensor_copy(gate_x[:], tok[:, bass.ds(GS * e, GS), 1].bitcast(F32)).then_inc(gate_ready, 1)
            if not last:
                rows_low(e + 1)

        expert(0, True, False)
        expert(1, False, False)
        with dve.Fori(2, E - 1) as e:
            expert(e, False, False)
        expert(E - 1, False, True)
        result_rows(E - 1)

    @block.gpsimd
    def _(pool):
        pool.memset(ident[:], 0.0).then_inc(ident_made, 1)
        pool.wait_ge(ident_made, 1)
        pool.affine_select(out=ident[:], in_=ident[:], compare_op=ALU.not_equal, fill=1.0, base=0, pattern=[[-1, P]],
                           channel_multiplier=1).then_inc(ident_made, 1)
        pool.memset(tri[:], 1.0).then_inc(made, 1)
        pool.memset(ones[:], 1.0).then_inc(made, 1)
        pool.memset(seg_sel[:], 1.0).then_inc(made, 1)
        pool.wait_ge(made, 3)
        pool.affine_select(out=tri[:], in_=tri[:], compare_op=ALU.is_gt, fill=0.0, base=0, pattern=[[1, P]],
                           channel_multiplier=-1).then_inc(made, 1)
        pool.affine_select(out=seg_sel[:], in_=seg_sel[:], compare_op=ALU.is_ge, fill=0.0, base=0,
                           pattern=[[-3, GS], [0, P]], channel_multiplier=1).then_inc(made, 1)
        pool.wait_ge(made, 5)
        pool.affine_select(out=seg_sel[:], in_=seg_sel[:], compare_op=ALU.is_ge, fill=0.0, base=2,
                           pattern=[[3, GS], [0, P]], channel_multiplier=-1).then_inc(made, 1)
        pool.iota(tokids[:], pattern=[[P, NSEG]], base=0, channel_multiplier=1).then_inc(made, 1)
        pool.iota(eidx[:], pattern=[[0, GS], [1, E]], base=-E, channel_multiplier=0,
                  allow_small_or_imprecise_dtypes=True).then_inc(made, 1)
        pool.iota(tile_ends[:], pattern=[[0, GS], [P, GS - 1]], base=P, channel_multiplier=0,
                  allow_small_or_imprecise_dtypes=True).then_inc(made, 1)
        pool.wait_ge(made, POOL_MADE)
        pool.wait_ge(init_made, DVE_MADE)

        def inverse_root(g, ready, step, ve, mn, rs, nr, parts=P, segs=GS):
            pool.wait_ge(ready, 2 * g + 2)
            pool.tensor_tensor(rs[0:parts, 0:segs], ve[0:parts, 0:segs], half_neg[0:parts, 0:segs], ALU.pow) \
                .then_inc(step, 1)
            pool.wait_ge(step, 2 * g + 1)
            pool.tensor_tensor(nr[0:parts, 0:segs], mn[0:parts, 0:segs], rs[0:parts, 0:segs], ALU.mult).then_inc(step, 1)

        def normalise1(g):
            inverse_root(g.n, ln1_ready, ln1_rstd, VE1, MN1, RS1, NR1)
            pool.wait_ge(ln1_rstd, 2 * g.n + 2)
            stand_alone(pool, pool_passed)
            for s in range(GS):
                pool.tensor_scalar(xa[g.par][:, s, :], xa[g.par][:, s, :], RS1[:, s:s + 1], NR1[:, s:s + 1], ALU.mult,
                                   ALU.add).then_inc(xn_done, 1)

        normalise1(Group(0, 0))
        pool.wait_ge(table_cleared, 16)
        inverse_root(0, gsum_stats, gsum_rstd, VE2, MN2, RS2, NR2, NSEG, 1)
        pool.wait_ge(pro_evac, SG + 1)
        blocks = sg[:].rearrange("p (b r) -> p b r", b=NBATCH)
        pool.affine_select(out=blocks, in_=blocks, compare_op=ALU.is_ge, fill=FAR_BELOW, base=0,
                           pattern=[[-(NSEG // NBATCH), NBATCH], [0, NSEG // NBATCH]], channel_multiplier=1) \
            .then_inc(gsum_masked, 1)
        pool.wait_ge(gsum_masked, 1)
        pool.affine_select(out=blocks, in_=blocks, compare_op=ALU.is_ge, fill=FAR_BELOW, base=NSEG // NBATCH - 1,
                           pattern=[[NSEG // NBATCH, NBATCH], [0, NSEG // NBATCH]], channel_multiplier=-1) \
            .then_inc(gsum_masked, 1)

        def scatter(g):
            pool.wait_ge(route, RT * g.n + RT)
            stand_alone(pool, pool_passed)
            for s in range(GS):
                pool.indirect_dma_start(out=table_dram, out_offset=bass.IndirectOffsetOnAxis(slot_i[g.par][:, s:s + 1], 0),
                                        in_=pay[g.par][:, s, :], in_offset=None, bounds_check=E * CAP - 1,
                                        oob_is_err=False).then_inc(scattered[g.par], 16)

        def iteration(i, prev, nxt, prev3):
            p1 = i.plus(-1)
            b = batch_of(p1)
            if nxt:
                normalise1(i.plus(1))
            if prev3:
                scatter(i.plus(-3))
            if prev:
                inverse_root(p1.n, ln2_ready, ln2_rstd, VE2, MN2, RS2, NR2)
                if isinstance(i.n, int) and i.n == 1:
                    pool.wait_ge(late_tab_in, 48)
                for s in range(GS):
                    rows = h2[p1.par][:, s, :]
                    pool.wait_ge(xn2_done, 4 * p1.n + s + 1)
                    stand_alone(pool, pool_passed)
                    pool.tensor_tensor(rows, rows, cb_tab[:, bass.ds(b, 1), :].rearrange("p b d -> p (b d)"), ALU.mult) \
                        .then_inc(h2_scaled, 1)
                    pool.wait_ge(h2_scaled, 4 * p1.n + s + 1)
                    stand_alone(pool, pool_passed)
                    pool.tensor_tensor(rows, rows, sb_tab[:, bass.ds(b, 1), :].rearrange("p b d -> p (b d)"), ALU.add) \
                        .then_inc(h2_ready, 1)

        iteration(Group(0, 0), False, True, False)
        iteration(Group(0, 1), True, True, False)
        iteration(Group(1, 0), True, True, False)
        iteration(Group(1, 1), True, True, True)
        with pool.Fori(2, NG // 2 - 1) as half:
            for par in range(2):
                iteration(Group(half, par), True, True, True)
        iteration(Group(NG // 2 - 1, 0), True, True, True)
        iteration(Group(NG // 2 - 1, 1), True, False, True)
        iteration(Group(NG // 2, 0), True, False, True)
        iteration(Group(NG // 2, 1), False, False, True)
        iteration(Group(NG // 2 + 1, 0), False, False, True)

        def gather(rows, source, tokens, done, n=T):
            for j in range(GS):
                pool.indirect_dma_start(out=rows[:, j, :], out_offset=None, in_=source,
                                        in_offset=bass.IndirectOffsetOnAxis(tokens[:, j:j + 1], 0), bounds_check=n - 1,
                                        oob_is_err=False).then_inc(done, 16)

        def gather_h(e):
            wait_past(pool, bt_full, 4 * e)
            pool.wait_ge(tok_h_ready, e + 1)
            stand_alone(pool, pool_passed)
            gather(xh, h2_dram, tok_h, xh_in)

        def gather_x(e):
            pool.wait_ge(tok_x_ready, 2 * e + 2)
            wait_past(pool, y_scaled, 4 * e)
            stand_alone(pool, pool_passed)
            gather(gb_rows, mod_dram.rearrange("b r d -> (b r) d"), tok_g, gb_in, NBATCH * 7)
            gather(xo, out_rows, tok_x, xo_in)

        def finish_rows(e):
            pool.wait_ge(xo_in, 16 * GS * (e + 1))
            for i in range(GS):
                q, j = 4 * e + i, GS - 1 - i
                pool.wait_ge(gb_gated, 4 * e + j + 1)
                pool.wait_ge(y_taken, q + 1)
                pool.tensor_tensor(yo[i % 2][:], yo[i % 2][:], gb_rows[:, j, :], ALU.mult).then_inc(y_scaled, 1)
                pool.wait_ge(y_scaled, q + 1)
                pool.tensor_tensor(yo[i % 2][:], yo[i % 2][:], xo[:, j, :], ALU.add).then_inc(y_ready, 1)
                pool.wait_ge(y_ready, q + 1)
                stand_alone(pool, pool_passed)
                pool.indirect_dma_start(out=out_rows, out_offset=bass.IndirectOffsetOnAxis(tok_x[:, j:j + 1], 0),
                                        in_=yo[i % 2][:], in_offset=None, bounds_check=T - 1, oob_is_err=False) \
                    .then_inc(y_sent[i % 2], 16)

        for par in range(2):
            pool.wait_ge(h2_stored[par], 16 * (NG // 2))
            pool.wait_ge(x2_stored[par], 16 * (NG // 2))
        pool.wait_ge(rows_cleared, 3)
        gather_h(0)
        gather_h(1)
        gather_x(0)
        with pool.Fori(1, E - 1) as e:
            gather_h(e + 1)
            finish_rows(e - 1)
            gather_x(e)
        finish_rows(E - 2)
        gather_x(E - 1)
        finish_rows(E - 1)

    stack.close()


_INS = ["L0_attn_x", "L0_attn_Wq", "L0_attn_bq", "L0_attn_Wk", "L0_attn_bk", "L0_attn_Wv", "L0_attn_bv",
        "L0_attn_Wo", "L0_attn_bo", "L0_ffn_Wg", "L0_ffn_bg", "L0_ffn_W1", "L0_ffn_b1", "L0_ffn_W2", "L0_ffn_b2",
        "L0_c", "L0_wmod"]


def kernel(**inputs):
    import numpy as _np
    import concourse.bacc as _bacc
    from concourse import mybir as _mybir
    from concourse.bass_utils import run_bass_kernel_spmd as _run

    nc = _bacc.Bacc("TRN2", target_bir_lowering=False, num_devices=1)
    arrays, args = {}, []
    for name in _INS:
        a = _np.ascontiguousarray(inputs[name])
        arrays[f"in_{name}_dram"] = a
        args.append(nc.dram_tensor(f"in_{name}_dram", a.shape, _mybir.dt.from_np(a.dtype), kind="ExternalInput").ap())
    shape = inputs["L0_attn_x"].shape
    out = nc.dram_tensor("out_0_dram", shape, _mybir.dt.float32, kind="ExternalOutput").ap()
    build_block(nc, *args, out)
    r = _run(nc, [arrays], core_ids=[0])
    return r.results[0]["out_0_dram"]
```

```python
from contextlib import ExitStack

import concourse.bass as bass
from concourse import mybir

F32 = mybir.dt.float32
F32R = mybir.dt.float32r
BF16 = mybir.dt.bfloat16
I32 = mybir.dt.int32
ACT = mybir.ActivationFunctionType
ALU = mybir.AluOpType
AX_X = mybir.AxisListType.X

P = 128
GS = 4
ROWS = GS * P
HEAD_DIM = 32
SCALE = HEAD_DIM ** -0.5
EPS = 1e-5
GATE_FLOOR = 0.25
NO_TOKEN = 1 << 20
FAR_BELOW = -3.0e38
RT = 20

SA, CA, GA, SB, CB, GB, VC = range(7)


class Group:

    def __init__(self, half, par):
        self.half, self.par, self.n = half, par, half * 2 + par

    def plus(self, k):
        q = self.par + k
        return Group(self.half + q // 2, q % 2)


def build_block(nc, x, wq, bq, wk, bk, wv, bv, wo, bo, wg, bg, w1, b1, w2, b2, cond, wmod, out):
    NBATCH, L, D = x.shape
    T = NBATCH * L
    KC = D // P
    NG = T // ROWS
    GPB = L // ROWS
    NSEG = T // P
    E = wg.shape[1]
    H = w1.shape[2]
    CAP = -(-T // E)
    HB = 512
    NB = H // HB
    HC = HB // P
    assert D == 512 and ROWS == 512 and CAP == ROWS and KC == 4 and HC == 4 and NSEG == 64 and NB % 2 == 0

    x_rows = x.rearrange("b l d -> (b l) d")
    out_rows = out.rearrange("b l d -> (b l) d")

    mod_dram = nc.dram_tensor("mod_rows", (NBATCH, 7, D), F32, kind="Internal").ap()
    qc_dram = nc.dram_tensor("query_consts", (NBATCH, 1), F32, kind="Internal").ap()
    global_dram = nc.dram_tensor("global_rows", (NSEG * 3, D), BF16, kind="Internal").ap()
    h2_dram = nc.dram_tensor("h2_rows", (T, D), F32, kind="Internal").ap()
    table_dram = nc.dram_tensor("slot_table", (E * CAP, 2), I32, kind="Internal").ap()

    KB = 1024
    base = nc.sbuf_base + (-nc.sbuf_base) % 64
    limit = nc.sbuf_usable_end
    sizes = {F32: 4, F32R: 4, BF16: 2, I32: 4}
    cursor = [base]

    def at(name, shape, dt, offset):
        n = sizes[dt]
        for k in shape[1:]:
            n *= k
        assert offset + n <= limit, (name, offset + n - limit)
        return nc.alloc_sbuf_tensor_at(name, shape, dt, offset=offset), offset + n

    def keep(name, shape, dt):
        t, end = at(name, shape, dt, cursor[0])
        cursor[0] = end + (-end) % 32
        return t

    def region(kilobytes):
        start = cursor[0]
        cursor[0] += kilobytes * KB
        assert cursor[0] <= limit
        return start

    def over(start, *tensors):
        made = []
        for name, shape, dt in tensors:
            t, start = at(name, shape, dt, start)
            made.append(t)
        return made

    ident = keep("ident", [P, P], F32)
    tri = keep("tri", [P, P], BF16)
    ones = keep("ones", [P, P], BF16)
    seg_sel = keep("seg_sel", [P, GS, P], BF16)
    grows = [keep(f"grows{i}", [P, D], BF16) for i in range(2)]
    wg_s = keep("wg_s", [P, KC, E], F32)
    wg_split = keep("wg_split", [P, KC, 2 * E], F32R)
    b1_col = keep("b1_col", [P, E * H // P], F32)
    tokids = keep("tokids", [P, NSEG], I32)
    eidx = keep("eidx", [P, GS, E], F32)
    bg_bc = keep("bg_bc", [P, E], F32)
    mod_col = keep("mod_col", [P, 2, KC, NBATCH], F32)
    u_col = keep("u_col", [P, KC], F32)
    bias_col = keep("bias_col", [P, 3 * KC], F32)
    qc_bc = keep("qc_bc", [P, NBATCH], F32)
    half_neg = keep("half_neg", [P, GS], F32)
    count = keep("count", [P, E], BF16)
    over_tile = keep("over_tile", [P, GS, GS - 1], F32)
    tile_ends = keep("tile_ends", [P, GS, GS - 1], F32)
    expert_rows = keep("expert_rows", [1, E], I32)
    onehot = keep("onehot", [P, GS, E], BF16)
    lg, lg_d, lg_v, lg_e, lg_r = (keep(f"lg{i}", [P, GS, E], F32) for i in range(5))
    osum = keep("osum", [P, E], F32)
    per_tok = keep("per_tok", [P, 24, GS], F32)
    (LG_MX, V_MIN, RANK, OVER, SLOT_A, SLOT_B, TILE, LG_SUM, MX, MXC, NEGB, PSUMS, PREC, VE1, MN1, RS1, NR1,
     VE2, MN2, RS2, NR2, QC, QCS, QRAW) = (per_tok[:, i, :] for i in range(24))
    stats = [keep(f"stats{i}", [P, GS, 6], F32) for i in range(2)]
    mv = [keep(f"mv{i}", [P, GS, 2], F32) for i in range(2)]
    slot_i = [keep(f"slot_i{i}", [P, GS], I32) for i in range(2)]
    pay = [keep(f"pay{i}", [P, GS, 2], I32) for i in range(2)]
    sc_t = keep("sc_t", [P, KC, NBATCH], F32)
    bk_cols = keep("bk_cols", [P, KC, NBATCH], F32)
    q_const = keep("q_const", [P, 4], F32)
    q_const_g = keep("q_const_g", [NSEG, 1], F32)
    one_row = keep("one_row", [1, NSEG], F32)
    tok_h = keep("tok_h", [P, GS], I32)
    tok_x = keep("tok_x", [P, GS], I32)
    tok_g = keep("tok_g", [P, GS], I32)
    gate_x = keep("gate_x", [P, GS], F32)

    r_m, r_v, r_xa, r_ht, r_split, r_xr = (region(16) for _ in range(6))
    r_gt, r_u, r_h2, r_h2t, r_p = region(8), region(16), region(16), region(8), region(6)
    r_tab, r_raw0 = region(32), region(8)

    full = [P, KC, D]
    m_hi, m_lo = over(r_m, ("m_hi", full, F32R), ("m_lo", full, F32R))
    v_hi, v_lo = over(r_v, ("v_hi", full, F32R), ("v_lo", full, F32R))
    xa = over(r_xa, ("xa0", full, F32), ("xa1", full, F32))
    ht = over(r_ht, ("ht0", full, F32), ("ht1", full, F32))
    ht_hi, ht_lo = over(r_split, ("ht_hi", full, F32R), ("ht_lo", full, F32R))
    xr = over(r_xr, ("xr0", full, F32), ("xr1", full, F32))
    gt, = over(r_gt, ("gt", full, F32))
    u_hi, u_lo = over(r_u, ("u_hi", full, F32R), ("u_lo", full, F32R))
    h2 = over(r_h2, ("h2_0", full, F32), ("h2_1", full, F32))
    h2t_hi, = over(r_h2t, ("h2t_hi", full, F32R))
    h2t_lo, = over(cursor[0], ("h2t_lo", full, F32R))
    seg_sq = [P, GS, P]
    prob, pt_hi, pt_lo = over(r_p, ("prob", seg_sq, F32), ("pt_hi", seg_sq, F32R), ("pt_lo", seg_sq, F32R))
    logit_parts, = over(r_p + 4 * KB, ("logit_parts", [2 * E, ROWS], F32))
    batch_rows = [P, NBATCH, D]
    ga_tab, cb_tab, sb_tab, vc_tab = over(r_tab, *((f"{k}_tab", batch_rows, F32) for k in ("ga", "cb", "sb", "vc")))

    wq_s, wk_s = over(r_xr, ("wq_s", full, F32), ("wk_s", full, F32))
    wv_s, wo_s = over(r_u, ("wv_s", full, F32), ("wo_s", full, F32))
    m_f = over(cursor[0], *((f"m_f{c}", [P, D], F32) for c in range(KC - 1)))
    wo_t, = over(r_h2t, ("wo_t", full, F32))
    vo_f, = over(r_raw0, ("vo_f", full, F32))
    wm_a, = over(r_xa + 8 * KB, ("wm_a", full, F32))
    wm_b, = over(r_ht + 8 * KB, ("wm_b", full, F32))
    wm_c, wm_d = over(r_xr, ("wm_c", full, F32), ("wm_d", full, F32))
    wm_s = [wm_a, wm_b, wm_d, wm_c, wm_b, wm_d]
    modr, sc_rows = over(r_h2, ("modr", [NBATCH, 7, D], F32), ("sc_rows", [NBATCH, D], F32))
    g_x, g_a, g_b = over(r_p, ("g_x", [NSEG, D], F32), ("g_a", [NSEG, D], F32), ("g_b", [NSEG, D], F32))
    b1_rows, bo_row, bqk, hg_t = over(r_tab, ("b1_rows", [P, 2, P], F32), ("bo_row", [1, D], F32),
                                      ("bqk", [NBATCH, 2, D], F32), ("hg_t", [P, KC, NSEG], F32))
    g_split, brow, u_row, gg_t = over(r_tab + 8 * KB, ("g_split", [NSEG, 3, D], BF16), ("brow", [1, D], F32),
                                      ("u_row", [1, D], F32), ("gg_t", [P, KC, NSEG], F32))

    sg, pg, pg_t, table_init, sc_tmp, bias_rows, g_c, m_f3 = over(
        r_tab + 16 * KB, ("sg", [NSEG, NSEG], F32), ("pg", [NSEG, P], F32),
        ("pg_t", [NSEG, NSEG], F32), ("table_init", [P, E * CAP // P, 2], I32),
        ("sc_tmp", [NBATCH, D], F32), ("bias_rows", [3 * KC, P], F32),
        ("g_c", [NSEG, D], F32), ("m_f3", [P, D], F32))
    m_f.append(m_f3)
    qc_junk = prob[:].rearrange("p s t -> p (s t)")
    QCS2 = [QC, QCS]

    raw = over(r_raw0, ("raw0", full, F32)) + over(r_xa, ("raw1", full, F32), ("raw2", full, F32)) \
        + over(r_ht, ("raw3", full, F32))
    w1_hi, w1_lo, w2_hi, w2_lo = [None] * 2, [None] * 2, [None] * 2, [None] * 2
    w1_hi[0], w1_lo[0] = over(r_m, ("w1_hi0", full, F32R), ("w1_lo0", full, F32R))
    w1_hi[1], w1_lo[1] = over(r_v, ("w1_hi1", full, F32R), ("w1_lo1", full, F32R))
    w2_hi[0], w2_lo[0] = over(r_split, ("w2_hi0", full, F32R), ("w2_lo0", full, F32R))
    w2_hi[1], w2_lo[1] = over(r_xr, ("w2_hi1", full, F32R), ("w2_lo1", full, F32R))
    h1_f, = over(r_ht + 8 * KB, ("h1_f", full, F32))
    xh, = over(r_gt, ("xh", full, F32))
    bt_hi, bt_lo = over(r_u, ("bt_hi", full, F32R), ("bt_lo", full, F32R))
    h1_hi, h1_lo = [None] * 2, [None] * 2
    h1_hi[0], h1_lo[0] = over(r_h2, ("h1_hi0", full, F32R), ("h1_lo0", full, F32R))
    xo, = over(r_h2t, ("xo", full, F32))
    b2_bc, table, tok_f, batch_f, gb_index = over(
        r_p, ("b2_bc", [P, D], F32), ("table", [P, E, GS, 2], I32), ("tok_f", [P, E * GS], F32),
        ("batch_f", [P, 4, E * GS], F32), ("gb_index", [P, E * GS], I32))
    h1_hi[1], h1_lo[1], gb_rows, yo = over(
        r_tab, ("h1_hi1", full, F32R), ("h1_lo1", full, F32R), ("gb_rows", full, F32),
        ("yo", full, F32))

    stack = ExitStack()
    banks = [stack.enter_context(nc.psum_tensor(f"bank{i}", [P, 512], F32)) for i in range(8)]
    big, (s_bank, pt_bank, lg_bank, pos_bank) = banks[:4], banks[4:]
    y_bank, h_bank = banks[:4], banks[4:]

    def sem(name):
        return stack.enter_context(nc.semaphore(name))

    made = sem("made")
    ident_made = sem("ident_made")
    init_made = sem("init_made")
    cond_in, bias_in, wv_in, wo_in, summ_in = (sem(f"{k}_in") for k in ("cond", "bias", "wv", "wo", "summ"))
    wqk_in = [sem(f"wqk_in{k}") for k in range(KC)]
    wm_in = [sem(f"wm_in{i}") for i in range(6)]
    wg_ready = sem("wg_ready")
    wg_in, bg_in, bo_in, bqk_in, b1_in = (sem(f"{k}_in") for k in ("wg", "bg", "bo", "bqk", "b1"))
    pro_full, pro_evac = sem("pro_full"), sem("pro_evac")
    sc_step, sc_exp, sc_ready = sem("sc_step"), sem("sc_exp"), sem("sc_ready")
    m_step, v_step, m_split, v_split = sem("m_step"), sem("v_step"), sem("m_split"), sem("v_split")
    fix_step, mod_fixed = sem("fix_step"), sem("mod_fixed")
    vc_stored, mod_stored = sem("vc_stored"), sem("mod_stored")
    brow_ready = sem("brow_ready")
    vcg_in, qcg_in = sem("vcg_in"), sem("qcg_in")
    tab_in, qc_in, late_tab_in = sem("tab_in"), sem("qc_in"), sem("late_tab_in")
    gsum_stats, gsum_rstd, gsum_xn, gsum_step = (sem(f"gsum_{k}") for k in ("stats", "rstd", "xn", "step"))
    gsum_masked, gsum_negb, gsum_exp, gsum_prob = (sem(f"gsum_{k}") for k in ("masked", "negb", "exp", "prob"))
    g_split_done, g_stored, table_cleared = sem("g_split_done"), sem("g_stored"), sem("table_cleared")

    x_in = [sem(f"x_in{i}") for i in range(2)]
    xr_in = [sem(f"xr_in{i}") for i in range(2)]
    grows_in = [sem(f"grows_in{i}") for i in range(2)]
    ln1_step, ln1_ready, ln1_rstd, xn_done = (sem(k) for k in ("ln1_step", "ln1_ready", "ln1_rstd", "xn_done"))
    t1_full, ht_full, ht_hi_done, ht_split, qc_raw, qc_ready = (sem(k) for k in (
        "t1_full", "ht_full", "ht_hi_done", "ht_split", "qc_raw", "qc_ready"))
    gt_full, gt_done, u_full, u_hi_done, u_split = (sem(k) for k in (
        "gt_full", "gt_done", "u_full", "u_hi_done", "u_split"))
    s_full, mx_step, negb_ready, exp_done, prec_ready, prob_ready = (sem(k) for k in (
        "s_full", "mx_step", "negb_ready", "exp_done", "prec_ready", "prob_ready"))
    pt_full, pt_hi_done, pt_split, av_full, av_taken = (sem(k) for k in (
        "pt_full", "pt_hi_done", "pt_split", "av_full", "av_taken"))
    x2_ready, ln2_step, ln2_ready, ln2_rstd, xn2_done, h2_scaled, h2_ready = (sem(k) for k in (
        "x2_ready", "ln2_step", "ln2_ready", "ln2_rstd", "xn2_done", "h2_scaled", "h2_ready"))
    last_scaled = sem("last_scaled")
    x2_stored = [sem(f"x2_stored{i}") for i in range(2)]
    h2_stored = [sem(f"h2_stored{i}") for i in range(2)]
    h2t_full, h2t_hi_done, h2t_split, parts_full, parts_out, lg_full = (sem(k) for k in (
        "h2t_full", "h2t_hi_done", "h2t_split", "parts_full", "parts_out", "lg_full"))
    lg_step, route, route_exp, pos_full = (sem(k) for k in ("lg_step", "route", "route_exp", "pos_full"))
    scattered = [sem(f"scattered{i}") for i in range(2)]

    count_full, rows_counted = sem("count_full"), sem("rows_counted")
    table_in, index_step, tok_h_ready, tok_x_ready, gate_ready, gb_in, gb_gated = (sem(k) for k in (
        "table_in", "index_step", "tok_h_ready", "tok_x_ready", "gate_ready", "gb_in", "gb_gated"))
    w1_in = [sem(f"w1_in{i}") for i in range(2)]
    w2_in = [sem(f"w2_in{i}") for i in range(2)]
    w1_hi_done, w1_split, w2_hi_done, w2_split = (sem(k) for k in (
        "w1_hi_done", "w1_split", "w2_hi_done", "w2_split"))
    rows_cleared, xo_in, b2_in = sem("rows_cleared"), sem("xo_in"), sem("b2_in")
    xh_in = [sem(f"xh_in{j}") for j in range(GS)]
    bt_full, bt_hi_done, bt_split = sem("bt_full"), sem("bt_hi_done"), sem("bt_split")
    h1_full, relu_done, h1_split, g2_done = (sem(k) for k in ("h1_full", "relu_done", "h1_split", "g2_done"))
    y_full, y_taken, y_scaled, y_ready = (sem(k) for k in ("y_full", "y_taken", "y_scaled", "y_ready"))
    y_sent = [sem(f"y_sent{j}") for j in range(GS)]

    sp_passed, pe_passed, act_passed, dve_passed, pool_passed = (sem(f"{k}_passed") for k in (
        "sp", "pe", "act", "dve", "pool"))

    def wait_past(eng, s, n):
        if not isinstance(n, int) or n > 0:
            eng.wait_ge(s, n)

    def stand_alone(eng, passed):
        eng.sem_inc(passed, 1)

    def chunk(k):
        return slice(k * P, (k + 1) * P)

    def batch_of(g):
        return g.n // GPB

    def split3(pe, o, a_hi, a_lo, b_hi, b_lo, start, stop):
        pe.matmul(o, a_hi, b_hi, start=start, stop=False)
        pe.matmul(o, a_hi, b_lo, start=False, stop=False)
        return pe.matmul(o, a_lo, b_hi, start=False, stop=stop)

    (MCH, SCT, BCOL, UROW, V4, UCOL, WOT, MCOL, VCH, HGT, GROW, GGT, SG, UG, BROW, PGT, TG, B1T,
     PRO_END) = (0, 4, 5, 6, 7, 8, 11, 15, 16, 21, 22, 23, 25, 26, 27, 28, 30, 31, 33)
    MODS = (9, 10, 20, 24, 29, 32)

    def pro_bank(q):
        return banks[q % 8 if q < MODS[GA] else 4 + q % 4]

    LAST_POOL_SEG = GS - 1
    POOL_MADE = 9
    DVE_MADE = 8

    def results_done(eng, e, b):
        if b == 0:
            wait_past(eng, g2_done, (NB - 1) * e)
        elif b == 1:
            wait_past(eng, y_full, GS * e)
        else:
            eng.wait_ge(g2_done, (NB - 1) * e + b - 1)

    block = stack.enter_context(nc.Block())

    @block.sync
    def _(sp):
        def w_rows(w):
            return w.rearrange("(c p) n -> p c n", p=P)

        def group_rows(rows, g):
            return rows[bass.ds(g.n * ROWS, ROWS), :].rearrange("(s p) d -> p s d", p=P)

        def load_x(g):
            sp.dma_start(xa[g.par][:], group_rows(x_rows, g)).then_inc(x_in[g.par], 16)

        for k in range(KC):
            sp.dma_start(wk_s[:, k, :], wk[chunk(k), :]).then_inc(wqk_in[k], 16)
            sp.dma_start(wq_s[:, k, :], wq[chunk(k), :]).then_inc(wqk_in[k], 16)
        sp.dma_start(sc_rows[:], cond).then_inc(cond_in, 16)
        for i, b in enumerate((bq, bk, bv)):
            sp.dma_start(bias_rows[KC * i:KC * (i + 1), :], b.rearrange("(c p) -> c p", p=P)).then_inc(bias_in, 16)
        load_x(Group(0, 0))

        def load_wmod(m):
            sp.dma_start(wm_s[m][:], wmod[:, m * D:(m + 1) * D].rearrange("(c p) n -> p c n", p=P)) \
                .then_inc(wm_in[m], 16)

        load_wmod(0)
        load_wmod(1)
        for i, b in enumerate((bq, bk)):
            sp.dma_start(bqk[:, i, :], b.rearrange("(a d) -> a d", a=1).to_broadcast([NBATCH, D])).then_inc(bqk_in, 16)
        sp.dma_start(wo_s[:], w_rows(wo)).then_inc(wo_in, 16)
        sp.dma_start(wv_s[:], w_rows(wv)).then_inc(wv_in, 16)
        sp.dma_start(g_x[:], x_rows.rearrange("(n p) d -> n p d", p=P)[:, 0, :]).then_inc(summ_in, 16)
        sp.dma_start(bo_row[:], bo.rearrange("(a d) -> a d", a=1)).then_inc(bo_in, 16)
        sp.dma_start(bg_bc[:], bg.rearrange("(a d) -> a d", a=1).to_broadcast([P, E])).then_inc(bg_in, 16)
        sp.dma_start(b1_rows[:], b1.rearrange("e (c p) -> (e c) p", p=P).rearrange("(t r) p -> r t p", r=P)) \
            .then_inc(b1_in, 16)
        sp.dma_start(wg_s[:], wg.rearrange("(c p) e -> p c e", p=P)).then_inc(wg_in, 16)
        sp.wait_ge(init_made, 2)
        sp.dma_start(table_dram.rearrange("(p a) c -> p a c", p=P), table_init[:]).then_inc(table_cleared, 16)
        sp.wait_ge(pro_full, UROW + 1)
        load_wmod(GA)
        sp.wait_ge(pro_full, V4 + 1)
        load_wmod(SB)
        sp.wait_ge(pro_full, MODS[SA] + 1)
        load_x(Group(0, 1))
        sp.wait_ge(pro_full, MODS[CA] + 1)
        load_wmod(CB)
        sp.wait_ge(mod_fixed, 1)
        sp.dma_start(mod_dram[:, VC, :], modr[:, VC, :]).then_inc(vc_stored, 16)
        sp.dma_start(qc_dram, q_const[0:NBATCH, 0:1]).then_inc(vc_stored, 16)
        sp.wait_ge(vc_stored, 32)

        def spread(row, n):
            return mod_dram[:, row, :].unsqueeze(0).to_broadcast([n, NBATCH, D])

        for b in range(NBATCH):
            seg = slice(b * (NSEG // NBATCH), (b + 1) * (NSEG // NBATCH))
            sp.dma_start(g_b[seg, :], mod_dram[b:b + 1, VC, :].to_broadcast([NSEG // NBATCH, D])).then_inc(vcg_in, 16)
            sp.dma_start(q_const_g[seg, :], qc_dram[b:b + 1, :].to_broadcast([NSEG // NBATCH, 1])).then_inc(qcg_in, 16)
        sp.dma_start(vc_tab[:], spread(VC, P)).then_inc(tab_in, 16)
        sp.dma_start(qc_bc[:], qc_dram.rearrange("b a -> a b").to_broadcast([P, NBATCH])).then_inc(qc_in, 16)
        sp.wait_ge(pro_full, MODS[GA] + 1)
        load_wmod(GB)
        sp.wait_ge(g_split_done, 1)
        sp.dma_start(global_dram.rearrange("(n t) d -> n t d", t=3), g_split[:]).then_inc(g_stored, 16)
        sp.wait_ge(mod_fixed, 2)
        sp.dma_start(mod_dram[:, 0:VC, :], modr[:, 0:VC, :]).then_inc(mod_stored, 16)
        sp.wait_ge(mod_stored, 16)
        sp.wait_ge(pro_evac, PRO_END)
        sp.dma_start(ga_tab[:], spread(GA, P)).then_inc(late_tab_in, 16)
        sp.wait_ge(g_stored, 16)
        sp.dma_start(cb_tab[:], spread(CB, P)).then_inc(late_tab_in, 16)
        sp.wait_ge(table_cleared, 16)
        sp.dma_start(sb_tab[:], spread(SB, P)).then_inc(late_tab_in, 16)

        def iteration(i, cur, prev, load2):
            if load2:
                sp.wait_ge(t1_full, 4 * i.n + 4)
                sp.wait_ge(qc_raw, 4 * i.n + 4)
                load_x(i.plus(2))
            if cur:
                wait_past(sp, av_full, 4 * i.n - 4)
                sp.dma_start(grows[i.par][0:3 * GS, :], global_dram[bass.ds(i.n * 3 * GS, 3 * GS), :]) \
                    .then_inc(grows_in[i.par], 16)
                if not isinstance(i.n, int) or i.n >= 2:
                    sp.wait_ge(xn2_done, 4 * i.n - 4)
                    stand_alone(sp, sp_passed)
                    sp.wait_ge(x2_stored[i.par], 16 * i.half)
                sp.dma_start(xr[i.par][:], group_rows(x_rows, i)).then_inc(xr_in[i.par], 16)
            if prev:
                g = i.plus(-1)
                sp.wait_ge(x2_ready, 4 * g.n + 4)
                sp.dma_start(group_rows(out_rows, g), xr[g.par][:]).then_inc(x2_stored[g.par], 16)
                sp.wait_ge(h2_ready, 4 * g.n + 4)
                sp.dma_start(group_rows(h2_dram, g), h2[g.par][:]).then_inc(h2_stored[g.par], 16)

        iteration(Group(0, 0), True, False, True)
        iteration(Group(0, 1), True, True, True)
        with sp.Fori(1, NG // 2 - 1) as half:
            for par in range(2):
                iteration(Group(half, par), True, True, True)
        for n in range(NG - 2, NG):
            iteration(Group(n // 2, n % 2), True, True, False)

        def load_w1(n, par):
            sp.dma_start(raw[2 * par][:], w1_block(n)).then_inc(w1_in[par], 16)

        def load_w2(n, par):
            sp.dma_start(raw[2 * par + 1][:], w2_block(n)).then_inc(w2_in[par], 16)

        w1_flat = w1.rearrange("e d h -> (e d) h")
        w2_flat = w2.rearrange("e h d -> (e h) d")

        def w1_block(n):
            e, b = n
            return w1_flat[bass.ds(e * D, D), b * HB:(b + 1) * HB].rearrange("(c p) h -> p c h", p=P)

        def w2_block(n):
            e, b = n
            return w2_flat[bass.ds(e * H + b * HB, HB), :].rearrange("(c p) d -> p c d", p=P)

        sp.wait_ge(s_full, NG)
        sp.wait_ge(qc_raw, 4 * NG)
        load_w1((0, 0), 0)
        load_w2((0, 0), 0)
        load_w1((0, 1), 1)
        load_w2((0, 1), 1)
        iteration(Group(NG // 2, 0), False, True, False)
        sp.wait_ge(h2_ready, 4 * NG)
        for par in range(2):
            sp.wait_ge(scattered[par], 16 * GS * (NG // 2))
        sp.dma_start(table[:], table_dram.rearrange("(e p j) c -> p e j c", p=P, j=GS)).then_inc(table_in, 16)
        sp.dma_start(b2_bc[:], b2[0:1, :].to_broadcast([P, D])).then_inc(b2_in, 16)

        def expert(e, first, last):
            for b in range(NB):
                n = e * NB + b
                ahead = (e, b + 2) if b + 2 < NB else (e + 1, b + 2 - NB)
                if not (last and b + 2 >= NB):
                    sp.wait_ge(w1_split, n + 1)
                    load_w1(ahead, b % 2)
                    sp.wait_ge(w2_split, n + 1)
                    load_w2(ahead, b % 2)
                if b == 1 and not first:
                    sp.wait_ge(y_taken, 4 * e)
                    stand_alone(sp, sp_passed)
                    sp.dma_start(b2_bc[:], b2[bass.ds(e, 1), :].to_broadcast([P, D])).then_inc(b2_in, 16)

        expert(0, True, False)
        with sp.Fori(1, E - 1) as e:
            expert(e, False, False)
        expert(E - 1, False, True)
        for par in range(2):
            sp.wait_ge(x2_stored[par], 16 * (NG // 2))
        for j in range(GS):
            sp.wait_ge(y_sent[j], 16 * E)

    @block.tensor
    def _(pe):
        def product(q, last):
            last.then_inc(pro_full, 1)

        def bank_free(q):
            wait_past(pe, pro_evac, q - 7 if q < MODS[GA] else q - 3)

        for k in range(KC):
            pe.wait_ge(wqk_in[k], 32)
            for c in range(KC):
                last = pe.matmul(pro_bank(MCH + c)[:, :], wq_s[:, k, chunk(c)], wk_s[:, k, :],
                                 start=(k == 0), stop=(k == KC - 1))
                if k == KC - 1:
                    product(MCH + c, last)
        pe.wait_ge(ident_made, 2)
        pe.wait_ge(sc_ready, 1)
        for k in range(KC):
            last = pe.transpose(pro_bank(SCT)[:, k * NBATCH:(k + 1) * NBATCH], sc_rows[:, chunk(k)],
                                ident[0:NBATCH, 0:NBATCH])
        product(SCT, last)
        pe.wait_ge(bias_in, 48)
        product(BCOL, pe.transpose(pro_bank(BCOL)[:, 0:3 * KC], bias_rows[:], ident[0:3 * KC, 0:3 * KC]))
        pe.wait_ge(pro_evac, BCOL + 1)
        for k in range(KC):
            last = pe.matmul(pro_bank(UROW)[0:1, :], bias_col[:, k:k + 1], wk_s[:, k, :],
                             start=(k == 0), stop=(k == KC - 1))
        product(UROW, last)
        for k in range(KC):
            last = pe.matmul(pro_bank(V4)[0:NBATCH, :], bk_cols[:, k, :], wq_s[:, k, :],
                             start=(k == 0), stop=(k == KC - 1))
        product(V4, last)
        pe.wait_ge(pro_evac, UROW + 1)
        bank_free(UCOL)
        for k in range(KC):
            last = pe.transpose(pro_bank(UCOL)[:, k:k + 1], u_row[:, chunk(k)], ident[0:1, 0:1])
        product(UCOL, last)
        def modulation(m):
            bank_free(MODS[m])
            pe.wait_ge(wm_in[m], 16)
            for k in range(KC):
                last = pe.matmul(pro_bank(MODS[m])[0:NBATCH, :], sc_t[:, k, :], wm_s[m][:, k, :],
                                 start=(k == 0), stop=(k == KC - 1))
            product(MODS[m], last)

        modulation(SA)
        modulation(CA)
        pe.wait_ge(wo_in, 16)
        for c in range(KC):
            bank_free(WOT + c)
            for k in range(KC):
                last = pe.transpose(pro_bank(WOT + c)[:, chunk(k)], wo_s[:, k, chunk(c)], ident[:])
            product(WOT + c, last)
        pe.wait_ge(mod_fixed, 1)
        bank_free(MCOL)
        for i, row in enumerate((SA, CA)):
            for k in range(KC):
                at_col = (i * KC + k) * NBATCH
                last = pe.transpose(pro_bank(MCOL)[:, at_col:at_col + NBATCH], modr[:, row, chunk(k)],
                                    ident[0:NBATCH, 0:NBATCH])
        product(MCOL, last)
        pe.wait_ge(wv_in, 16)
        pe.wait_ge(pro_evac, WOT + KC)
        for c in range(KC):
            bank_free(VCH + c)
            for k in range(KC):
                last = pe.matmul(pro_bank(VCH + c)[:, :], wv_s[:, k, chunk(c)], wo_t[:, k, :],
                                 start=(k == 0), stop=(k == KC - 1))
            product(VCH + c, last)

        def transpose_xn(g, first):
            pe.wait_ge(xn_done, 4 * g.n + 4)
            for k in range(KC):
                if not first:
                    pe.wait_ge(u_split, 4 * g.n - 4 + k + 1)
                for s in range(GS):
                    last = pe.transpose(big[k][:, chunk(s)], xa[g.par][:, s, chunk(k)], ident[:])
                last.then_inc(t1_full, 1)

        def g_tile(g, j):
            for k in range(KC):
                if j == 0:
                    pe.wait_ge(ht_split, 4 * g.n + k + 1)
                last = split3(pe, big[j][:, :], m_hi[:, k, chunk(j)], m_lo[:, k, chunk(j)], ht_hi[:, k, :],
                              ht_lo[:, k, :], k == 0, k == KC - 1)
            last.then_inc(gt_full, 1)

        pe.wait_ge(pro_evac, VCH + KC)
        transpose_xn(Group(0, 0), True)
        modulation(GA)
        pe.wait_ge(gsum_xn, 1)
        bank_free(HGT)
        for k in range(KC):
            last = pe.transpose(pro_bank(HGT)[:, k * NSEG:(k + 1) * NSEG], g_a[:, chunk(k)], ident[0:NSEG, 0:NSEG])
        product(HGT, last)
        pe.wait_ge(m_split, KC)
        g_tile(Group(0, 0), 0)
        g_tile(Group(0, 0), 1)
        pe.wait_ge(pro_evac, HGT + 1)
        bank_free(GROW)
        for k in range(KC):
            last = pe.matmul(pro_bank(GROW)[0:NSEG, :], hg_t[:, k, :], m_f[k][:],
                             start=(k == 0), stop=(k == KC - 1))
        product(GROW, last)
        g_tile(Group(0, 0), 2)
        pe.wait_ge(pro_evac, GROW + 1)
        for k in range(KC):
            last = pe.transpose(pro_bank(GGT)[:, k * NSEG:(k + 1) * NSEG], g_x[:, chunk(k)], ident[0:NSEG, 0:NSEG])
        product(GGT, last)
        modulation(SB)
        pe.wait_ge(pro_evac, GGT + 1)
        bank_free(SG)
        for k in range(KC):
            last = pe.matmul(pro_bank(SG)[0:NSEG, 0:NSEG], gg_t[:, k, :], hg_t[:, k, :],
                             start=(k == 0), stop=(k == KC - 1))
        product(SG, last)
        bank_free(UG)
        for k in range(KC):
            last = pe.matmul(pro_bank(UG)[0:NSEG, :], hg_t[:, k, :], vo_f[:, k, :],
                             start=(k == 0), stop=(k == KC - 1))
        product(UG, last)
        bank_free(BROW)
        for k in range(KC):
            last = pe.matmul(pro_bank(BROW)[0:1, :], bias_col[:, 2 * KC + k:2 * KC + k + 1], wo_t[:, k, :],
                             start=(k == 0), stop=(k == KC - 1))
        product(BROW, last)
        g_tile(Group(0, 0), 3)
        pe.wait_ge(gsum_prob, 1)
        bank_free(PGT)
        product(PGT, pe.transpose(pro_bank(PGT)[:, 0:NSEG], pg[:], ident[0:NSEG, 0:NSEG]))
        modulation(CB)
        pe.wait_ge(brow_ready, 1)
        pe.wait_ge(pro_evac, PGT + 1)
        bank_free(TG)
        pe.matmul(pro_bank(TG)[0:NSEG, :], pg_t[:], g_b[:], start=True, stop=False)
        product(TG, pe.matmul(pro_bank(TG)[0:NSEG, :], one_row[:], brow[:], start=False, stop=True))
        pe.wait_ge(b1_in, 16)
        bank_free(B1T)
        for t in range(2):
            last = pe.transpose(pro_bank(B1T)[:, chunk(t)], b1_rows[:, t, :], ident[:])
        product(B1T, last)
        modulation(GB)
        pe.wait_ge(v_split, KC)
        pe.wait_ge(wg_ready, 2)
        pe.wait_ge(made, POOL_MADE)

        def ranks(g):
            pe.wait_ge(route, RT * g.n + 6)
            flat = onehot[:].rearrange("p s e -> p (s e)")
            pe.matmul(pos_bank[:, 0:GS * E], tri[:], flat, start=True, stop=False)
            pe.matmul(pos_bank[:, 0:GS * E].rearrange("p (s e) -> p s e", e=E), ones[:],
                      count[:].unsqueeze(1).to_broadcast([P, GS, E]), start=False, stop=False)
            for s in range(GS - 1):
                last = pe.matmul(pos_bank[:, (s + 1) * E:GS * E].rearrange("p (s e) -> p s e", e=E), ones[:],
                                 onehot[:, s:s + 1, :].to_broadcast([P, GS - 1 - s, E]),
                                 start=False, stop=(s == GS - 2))
            last.then_inc(pos_full, 1)

        def iteration(i, cur, prev, prev2, nxt, prev3):
            n = i.n
            p1, p2 = i.plus(-1), i.plus(-2)
            g_tiles = cur and not (isinstance(n, int) and n == 0)
            if g_tiles:
                g_tile(i, 0)
                g_tile(i, 1)
            if prev2:
                pe.wait_ge(h2_ready, 4 * p2.n + 4)
                if not cur:
                    pe.wait_ge(u_split, 4 * NG)
                for k in range(KC):
                    if cur and k >= 2:
                        pe.wait_ge(gt_done, 4 * n + k - 1)
                    for s in range(GS):
                        last = pe.transpose(big[(k + 2) % 4][:, chunk(s)], h2[p2.par][:, s, chunk(k)], ident[:])
                    last.then_inc(h2t_full, 1)
            if prev3:
                ranks(i.plus(-3))
            if g_tiles:
                if prev2:
                    pe.wait_ge(h2t_split, 4 * p2.n + 1)
                g_tile(i, 2)
            if prev:
                pe.wait_ge(prob_ready, p1.n + 1)
                for s in range(GS):
                    last = pe.transpose(pt_bank[:, chunk(s)], prob[:, s, :], ident[:])
                last.then_inc(pt_full, 1)
            if g_tiles:
                if prev2:
                    pe.wait_ge(h2t_split, 4 * p2.n + 2)
                g_tile(i, 3)
            if prev:
                pe.wait_ge(u_split, 4 * p1.n + 4)
                pe.wait_ge(pt_split, p1.n + 1)
                pe.wait_ge(grows_in[p1.par], 16 * (p1.half + 1))
                if prev2:
                    pe.wait_ge(h2t_split, 4 * p2.n + 4)
                for s in range(GS):
                    if cur:
                        pe.wait_ge(gt_done, 4 * n + s + 1)
                    split3(pe, big[s][:, :], pt_hi[:, s, :], pt_lo[:, s, :], u_hi[:, s, :], u_lo[:, s, :], True, False)
                    pe.matmul(big[s][:, :], seg_sel[:, s, :], grows[p1.par][:], start=False, stop=True) \
                        .then_inc(av_full, 1)
            if cur:
                for s in range(GS):
                    if prev:
                        pe.wait_ge(av_taken, 4 * p1.n + s + 1)
                    else:
                        pe.wait_ge(gt_done, 4 * n + s + 1)
                    for k in range(KC):
                        last = split3(pe, big[s][:, :], ht_hi[:, k, chunk(s)], ht_lo[:, k, chunk(s)], v_hi[:, k, :],
                                      v_lo[:, k, :], k == 0, k == KC - 1)
                    last.then_inc(u_full, 1)
            if prev2:
                pe.wait_ge(h2t_split, 4 * p2.n + 4)
                for k in range(KC):
                    pe.matmul(lg_bank[0:2 * E, :], wg_split[:, k, :], h2t_hi[:, k, :], start=(k == 0), stop=False)
                for k in range(KC):
                    last = pe.matmul(lg_bank[0:E, :], wg_split[:, k, 0:E], h2t_lo[:, k, :],
                                     start=False, stop=(k == KC - 1))
                last.then_inc(parts_full, 1)
            if nxt:
                transpose_xn(i.plus(1), False)
            if prev2:
                pe.wait_ge(parts_out, p2.n + 1)
                if prev:
                    pe.wait_ge(pt_split, p1.n + 1)
                stand_alone(pe, pe_passed)
                for s in range(GS):
                    last = pe.transpose(pt_bank[:, s * 2 * E:(s + 1) * 2 * E], logit_parts[:, chunk(s)],
                                        ident[0:2 * E, 0:2 * E])
                last.then_inc(lg_full, 1)
            if cur:
                if not g_tiles:
                    pe.wait_ge(pro_evac, PRO_END)
                pe.wait_ge(gt_done, 4 * n + 4)
                for s in range(GS):
                    for k in range(KC):
                        last = pe.matmul(s_bank[:, chunk(s)], gt[:, k, chunk(s)], ht[i.par][:, k, chunk(s)],
                                         start=(k == 0), stop=(k == KC - 1))
                last.then_inc(s_full, 1)

        iteration(Group(0, 0), True, False, False, True, False)
        iteration(Group(0, 1), True, True, False, True, False)
        iteration(Group(1, 0), True, True, True, True, False)
        iteration(Group(1, 1), True, True, True, True, True)
        with pe.Fori(2, NG // 2 - 1) as half:
            for par in range(2):
                iteration(Group(half, par), True, True, True, True, True)
        iteration(Group(NG // 2 - 1, 0), True, True, True, True, True)
        iteration(Group(NG // 2 - 1, 1), True, True, True, False, True)
        iteration(Group(NG // 2, 0), False, True, True, False, True)
        iteration(Group(NG // 2, 1), False, False, True, False, True)
        ranks(Group(NG // 2 - 1, 1))

        def rows_of(e):
            return pe.value_load(expert_rows[0:1, bass.ds(e, 1)], min_val=0, max_val=T)

        def filled_tiles(rows, tile, passed_over=lambda: None, between=lambda: None):
            for j in range(GS - 1, 0, -1):
                if rows is None:
                    tile(j)
                    continue
                with pe.If(rows > j * P):
                    tile(j)
                with pe.Else():
                    passed_over()
            between()
            tile(0)

        def gathered_transpose(e, rows):
            wait_past(pe, relu_done, 4 * NB * e)

            def tile(j):
                pe.wait_ge(xh_in[j], 16 * (e + 1))
                for k in range(KC):
                    last = pe.transpose(h_bank[k][:, chunk(j)], xh[:, j, chunk(k)], ident[:])
                    if j == 0:
                        last.then_inc(bt_full, 1)

            filled_tiles(rows, tile)

        def hidden(e, b, rows):
            n = NB * e + b
            pe.wait_ge(w1_split, n + 1)

            def product(slots):
                for j in range(HC):
                    if b > 0:
                        pe.wait_ge(relu_done, 4 * n + j - 3)
                    for k in range(KC):
                        if b == 0 and j == 0:
                            pe.wait_ge(bt_split, 4 * e + k + 1)
                        last = split3(pe, h_bank[j][:, 0:slots], w1_hi[b % 2][:, k, chunk(j)],
                                      w1_lo[b % 2][:, k, chunk(j)], bt_hi[:, k, 0:slots], bt_lo[:, k, 0:slots],
                                      k == 0, k == KC - 1)
                    last.then_inc(h1_full, 1)

            def narrowest(widths):
                if len(widths) == 1:
                    product(widths[0])
                    return
                middle = (len(widths) + 1) // 2
                with pe.If(rows > widths[middle - 1]):
                    narrowest(widths[middle:])
                with pe.Else():
                    narrowest(widths[:middle])

            narrowest(range(256, ROWS + 1, 64))

        def results(e, b, rows, between=lambda: None):
            n = NB * e + b
            pe.wait_ge(h1_split, 4 * n + 4)
            pe.wait_ge(w2_split, n + 1)
            if b == 0:
                wait_past(pe, y_taken, 4 * e)

            def tile(j):
                for c in range(HC):
                    last = split3(pe, y_bank[j][:, :], h1_hi[b % 2][:, c, chunk(j)], h1_lo[b % 2][:, c, chunk(j)],
                                  w2_hi[b % 2][:, c, :], w2_lo[b % 2][:, c, :], b == 0 and c == 0,
                                  b == NB - 1 and c == HC - 1)
                if b == NB - 1:
                    last.then_inc(y_full, 1)
                elif j == 0:
                    last.then_inc(g2_done, 1)

            def passed_over():
                if b == NB - 1:
                    pe.sem_inc(y_full, 1)

            filled_tiles(rows, tile, passed_over, between)

        def expert(e, first, last):
            rows = rows_of(e)
            for b in range(NB):
                hidden(e, b, rows)
                if b == NB - 1 and not last:
                    results(e, b - 1, rows, lambda: gathered_transpose(e + 1, rows_of(e + 1)))
                elif b > 0:
                    results(e, b - 1, rows)
                elif not first:
                    results(e - 1, NB - 1, rows_of(e - 1))

        pe.wait_ge(pos_full, NG)
        pe.wait_ge(route, RT * NG)
        pe.matmul(pos_bank[0:1, 0:E], ones[:, 0:1], count[:], start=True, stop=True).then_inc(count_full, 1)
        pe.wait_ge(rows_counted, 1)
        gathered_transpose(0, None)
        expert(0, True, False)
        with pe.Fori(1, E - 1) as e:
            expert(e, False, False)
        expert(E - 1, False, True)
        results(E - 1, NB - 1, rows_of(E - 1))

    @block.scalar
    def _(act):
        def copy_out(q, dst, src, scale=1.0):
            act.wait_ge(pro_full, q + 1)
            act.activation(dst, src, ACT.Copy, scale=scale).then_inc(pro_evac, 1)

        act.wait_ge(cond_in, 16)
        act.activation(sc_tmp[:], sc_rows[:], ACT.Exp, scale=-1.0).then_inc(sc_exp, 1)
        for c in range(KC):
            copy_out(MCH + c, m_f[c][:], pro_bank(MCH + c)[:, :])
        copy_out(SCT, sc_t[:].rearrange("p k b -> p (k b)"), pro_bank(SCT)[:, 0:KC * NBATCH])
        act.wait_ge(pro_full, BCOL + 1)
        act.activation(bias_col[:], pro_bank(BCOL)[:, 0:3 * KC], ACT.Copy)
        act.activation(bk_cols[:], pro_bank(BCOL)[:, KC:2 * KC].unsqueeze(2).to_broadcast([P, KC, NBATCH]),
                       ACT.Copy).then_inc(pro_evac, 1)
        copy_out(UROW, u_row[:], pro_bank(UROW)[0:1, :])
        copy_out(V4, modr[:, VC, :], pro_bank(V4)[0:NBATCH, :])
        copy_out(UCOL, u_col[:], pro_bank(UCOL)[:, 0:KC])
        def modulation_row(m):
            copy_out(MODS[m], modr[:, m, :], pro_bank(MODS[m])[0:NBATCH, :])

        modulation_row(SA)
        modulation_row(CA)
        for c in range(KC):
            copy_out(WOT + c, wo_t[:, c, :], pro_bank(WOT + c)[:, :])
        act.wait_ge(gsum_rstd, 2)
        act.activation(g_a[:], g_x[:], ACT.Identity, bias=NR2[0:NSEG, 0:1], scale=RS2[0:NSEG, 0:1]).then_inc(gsum_xn, 1)
        copy_out(MCOL, mod_col[:].rearrange("p i k b -> p (i k b)"), pro_bank(MCOL)[:, 0:2 * KC * NBATCH])
        for c in range(KC):
            copy_out(VCH + c, vo_f[:, c, :], pro_bank(VCH + c)[:, :])

        def modulate(g):
            for k in range(KC):
                act.wait_ge(t1_full, 4 * g.n + k + 1)
                act.wait_ge(pro_evac, MCOL + 1)
                act.activation(ht[g.par][:, k, :], big[k][:, :], ACT.Identity,
                               bias=mod_col[:, 0, k, bass.ds(batch_of(g), 1)],
                               scale=mod_col[:, 1, k, bass.ds(batch_of(g), 1)]).then_inc(ht_full, 1)

        def add_u(g, j):
            act.wait_ge(gt_full, 4 * g.n + j + 1)
            act.activation(gt[:, j, :], big[j][:, :], ACT.Identity, bias=u_col[:, j:j + 1]).then_inc(gt_done, 1)

        modulate(Group(0, 0))
        modulation_row(GA)
        act.wait_ge(pro_full, HGT + 1)
        for k in range(KC):
            for b in range(NBATCH):
                seg = slice(b * (NSEG // NBATCH), (b + 1) * (NSEG // NBATCH))
                ins = act.activation(hg_t[:, k, seg], pro_bank(HGT)[:, k * NSEG + seg.start:k * NSEG + seg.stop],
                                     ACT.Identity, bias=mod_col[:, 0, k, b:b + 1], scale=mod_col[:, 1, k, b:b + 1])
        ins.then_inc(pro_evac, 1)
        add_u(Group(0, 0), 0)
        add_u(Group(0, 0), 1)
        copy_out(GROW, g_x[:], pro_bank(GROW)[0:NSEG, :])
        add_u(Group(0, 0), 2)
        act.wait_ge(pro_full, GGT + 1)
        for k in range(KC):
            ins = act.activation(gg_t[:, k, :], pro_bank(GGT)[:, k * NSEG:(k + 1) * NSEG], ACT.Identity,
                                 bias=u_col[:, k:k + 1])
        ins.then_inc(pro_evac, 1)
        modulation_row(SB)
        copy_out(SG, sg[:], pro_bank(SG)[0:NSEG, 0:NSEG])
        act.wait_ge(gsum_step, 4)
        copy_out(UG, g_b[:], pro_bank(UG)[0:NSEG, :])
        act.wait_ge(gsum_negb, 1)
        act.activation(pg[:, 0:NSEG], sg[:], ACT.Exp, bias=NEGB[0:NSEG, 0:1], scale=SCALE,
                       accum_out=PSUMS[0:NSEG, 0:1]).then_inc(gsum_exp, 1)
        copy_out(BROW, brow[:], pro_bank(BROW)[0:1, :], scale=2.0)
        add_u(Group(0, 0), 3)
        copy_out(PGT, pg_t[:], pro_bank(PGT)[0:NSEG, 0:NSEG])
        modulation_row(CB)
        copy_out(TG, g_a[:], pro_bank(TG)[0:NSEG, :])
        copy_out(B1T, b1_col[:], pro_bank(B1T)[:, 0:2 * P])
        modulation_row(GB)

        def iteration(i, cur, prev, prev2, nxt, prev3):
            n = i.n
            p1, p2 = i.plus(-1), i.plus(-2)

            g_tiles = cur and not (isinstance(n, int) and n == 0)

            def empty_u(s):
                act.wait_ge(u_full, 4 * n + s + 1)
                act.activation(u_hi[:, s, :], big[s][:, :], ACT.Copy).then_inc(u_hi_done, 1)

            def empty_parts():
                act.wait_ge(parts_full, p2.n + 1)
                act.activation(logit_parts[:], lg_bank[0:2 * E, :], ACT.Copy).then_inc(parts_out, 1)

            def normalise2(s):
                act.activation(h2[p1.par][:, s, :], xr[p1.par][:, s, :], ACT.Identity, bias=NR2[:, s:s + 1],
                               scale=RS2[:, s:s + 1]).then_inc(xn2_done, 1)

            if prev:
                act.wait_ge(negb_ready, p1.n + 1)
                for s in range(GS):
                    act.activation(prob[:, s, :], s_bank[:, chunk(s)], ACT.Exp, bias=NEGB[:, s:s + 1], scale=SCALE,
                                   accum_out=PSUMS[:, s:s + 1]).then_inc(exp_done, 1)
            if prev3:
                p3 = i.plus(-3)
                act.wait_ge(route, RT * p3.n + 3)
                act.activation(lg_e[:], lg_d[:], ACT.Exp).then_inc(route_exp, 1)
            if g_tiles:
                add_u(i, 0)
                add_u(i, 1)
            if prev2:
                for k in range(KC):
                    act.wait_ge(h2t_full, 4 * p2.n + k + 1)
                    act.activation(h2t_hi[:, k, :], big[(k + 2) % 4][:, :], ACT.Copy).then_inc(h2t_hi_done, 1)
            if g_tiles:
                add_u(i, 2)
            if prev:
                act.wait_ge(pt_full, p1.n + 1)
                act.activation(pt_hi[:].rearrange("p s t -> p (s t)"), pt_bank[:, :], ACT.Copy).then_inc(pt_hi_done, 1)
            if g_tiles:
                add_u(i, 3)
            if cur:
                empty_u(0)
                empty_u(1)
                empty_u(2)
            if prev2 and not cur:
                empty_parts()
            if prev:
                act.wait_ge(ln2_rstd, 2 * p1.n + 2)
                normalise2(0)
                normalise2(1)
                normalise2(2)
            if cur:
                empty_u(3)
            if prev:
                normalise2(3)
            if prev2 and cur:
                empty_parts()
            if nxt:
                modulate(i.plus(1))

        iteration(Group(0, 0), True, False, False, True, False)
        iteration(Group(0, 1), True, True, False, True, False)
        iteration(Group(1, 0), True, True, True, True, False)
        iteration(Group(1, 1), True, True, True, True, True)
        with act.Fori(2, NG // 2 - 1) as half:
            for par in range(2):
                iteration(Group(half, par), True, True, True, True, True)
        iteration(Group(NG // 2 - 1, 0), True, True, True, True, True)
        iteration(Group(NG // 2 - 1, 1), True, True, True, False, True)
        iteration(Group(NG // 2, 0), False, True, True, False, True)
        iteration(Group(NG // 2, 1), False, False, True, False, True)
        iteration(Group(NG // 2 + 1, 0), False, False, False, False, True)

        def w2_high(n, e, b):
            act.wait_ge(w2_in[b % 2], 16 * (NB // 2 * e + b // 2 + 1))
            results_done(act, e, b)
            act.activation(w2_hi[b % 2][:], raw[2 * (b % 2) + 1][:], ACT.Copy).then_inc(w2_hi_done, 1)

        def relu(e, b, j):
            n = NB * e + b
            act.wait_ge(h1_full, 4 * n + j + 1)
            if j == 0:
                results_done(act, e, b)
            wait_past(act, h1_split, 4 * n + j - 3)
            stand_alone(act, act_passed)
            bias = b1_col[:, bass.ds(e * (H // P) + b * HC + j, 1)]
            act.activation(h1_hi[b % 2][:, j, :], h_bank[j][:, :], ACT.Relu, bias=bias)
            act.activation(h1_f[:, j, :], h_bank[j][:, :], ACT.Relu, bias=bias).then_inc(relu_done, 1)

        def gate_rows(e):
            act.wait_ge(gate_ready, e + 1)
            act.wait_ge(gb_in, 16 * GS * (e + 1))
            for j in range(GS):
                act.activation(gb_rows[:, j, :], gb_rows[:, j, :], ACT.Copy, scale=gate_x[:, j:j + 1]) \
                    .then_inc(gb_gated, 1)

        def rows_high(e):
            for k in range(KC):
                act.wait_ge(bt_full, 4 * e + k + 1)
                act.activation(bt_hi[:, k, :], h_bank[k][:, :], ACT.Copy).then_inc(bt_hi_done, 1)

        rows_high(0)

        def expert(e, first, last):
            for b in range(NB):
                n = NB * e + b
                relu(e, b, 0)
                relu(e, b, 1)
                relu(e, b, 2)
                relu(e, b, 3)
                w2_high(n, e, b)
                if b == 0 and not first:
                    gate_rows(e - 1)
            if not last:
                rows_high(e + 1)

        expert(0, True, False)
        with act.Fori(1, E - 1) as e:
            expert(e, False, False)
        expert(E - 1, False, True)
        gate_rows(E - 1)

    @block.vector
    def _(dve):
        dve.memset(table_init[:, :, 0:1], NO_TOKEN).then_inc(init_made, 1)
        dve.memset(table_init[:, :, 1:2], 0).then_inc(init_made, 1)
        dve.memset(count[:], 0.0).then_inc(init_made, 1)
        dve.memset(grows[0][:], 0.0).then_inc(init_made, 1)
        dve.memset(grows[1][:], 0.0).then_inc(init_made, 1)
        dve.memset(pg[:], 0.0).then_inc(init_made, 1)
        dve.memset(half_neg[:], -0.5).then_inc(init_made, 1)
        dve.memset(one_row[:], 1.0).then_inc(init_made, 1)
        dve.wait_ge(init_made, DVE_MADE)
        dve.wait_ge(sc_exp, 1)
        dve.tensor_scalar(sc_tmp[:], sc_tmp[:], 1.0, None, ALU.add).then_inc(sc_step, 1)
        dve.wait_ge(sc_step, 1)
        dve.reciprocal(sc_tmp[:], sc_tmp[:]).then_inc(sc_step, 1)
        dve.wait_ge(sc_step, 2)
        dve.tensor_tensor(sc_rows[:], sc_rows[:], sc_tmp[:], ALU.mult).then_inc(sc_ready, 1)

        def layer_stats(g, rows, step, ready, per_step, st, mvt, ve, mn, used, parts=P, segs=GS):
            used()
            for s in range(segs):
                dve.bn_stats(st[0:parts, s, :], rows[:, s, :]).then_inc(step, 1)
            dve.wait_ge(step, per_step * g + segs)
            stand_alone(dve, dve_passed)
            for s in range(segs):
                dve.bn_aggr(mvt[0:parts, s, :], st[0:parts, s, :]).then_inc(step, 1)
            dve.wait_ge(step, per_step * g + 2 * segs)
            dve.tensor_scalar(ve[0:parts, 0:segs], mvt[0:parts, 0:segs, 1], EPS, None, ALU.add).then_inc(ready, 1)
            dve.tensor_scalar(mn[0:parts, 0:segs], mvt[0:parts, 0:segs, 0], -1.0, None, ALU.mult).then_inc(ready, 1)

        def stats1(g):
            dve.wait_ge(x_in[g.par], 16 * (g.half + 1))
            layer_stats(g.n, xa[g.par], ln1_step, ln1_ready, 8, stats[0], mv[0], VE1, MN1,
                        lambda: wait_past(dve, xn_done, 4 * g.n))

        def split_weights(q, src, hi, lo, done, step):
            for c in range(KC):
                dve.wait_ge(pro_evac, q + c + 1)
                dve.tensor_copy(hi[:, c, :], src[c]).then_inc(step, 1)
                dve.wait_ge(step, c + 1)
                dve.tensor_tensor(lo[:, c, :], src[c], hi[:, c, :].bitcast(F32), ALU.subtract).then_inc(done, 1)

        stats1(Group(0, 0))
        split_weights(MCH, [t[:] for t in m_f], m_hi, m_lo, m_split, m_step)
        dve.wait_ge(summ_in, 16)
        layer_stats(0, g_x[:].unsqueeze(1), gsum_step, gsum_stats, 0, stats[1], mv[1], VE2, MN2, lambda: None, NSEG, 1)
        fix = [0]

        def link(ins):
            fix[0] += 1
            ins.then_inc(fix_step, 1)
            dve.wait_ge(fix_step, fix[0])

        dve.wait_ge(pro_evac, V4 + 1)
        dve.wait_ge(bqk_in, 32)
        link(dve.scalar_tensor_tensor(out=sc_tmp[:], in0=bqk[:, 0, :], scalar=1.0, in1=bqk[:, 1, :], op0=ALU.mult,
                                      op1=ALU.mult, accum_out=q_const[0:NBATCH, 1:2]))
        dve.wait_ge(pro_evac, MODS[SA] + 1)
        link(dve.scalar_tensor_tensor(out=sc_tmp[:], in0=modr[:, VC, :], scalar=1.0, in1=modr[:, SA, :], op0=ALU.mult,
                                      op1=ALU.mult, accum_out=q_const[0:NBATCH, 2:3]))
        link(dve.tensor_tensor(q_const[0:NBATCH, 0:1], q_const[0:NBATCH, 1:2], q_const[0:NBATCH, 2:3], ALU.add))
        dve.wait_ge(pro_evac, MODS[CA] + 1)
        link(dve.tensor_scalar(modr[:, CA, :], modr[:, CA, :], 1.0, None, ALU.add))
        dve.tensor_tensor(modr[:, VC, :], modr[:, VC, :], modr[:, CA, :], ALU.mult).then_inc(mod_fixed, 1)

        def floor_gate(row):
            dve.wait_ge(pro_evac, MODS[row] + 1)
            link(dve.tensor_scalar(sc_tmp[:], modr[:, row, :], 0.0, 2.0, ALU.is_ge, ALU.mult))
            link(dve.tensor_scalar(sc_tmp[:], sc_tmp[:], -1.0, None, ALU.add))
            link(dve.tensor_tensor(modr[:, row, :], modr[:, row, :], sc_tmp[:], ALU.mult))
            link(dve.scalar_tensor_tensor(out=modr[:, row, :], in0=modr[:, row, :], scalar=GATE_FLOOR, in1=sc_tmp[:],
                                          op0=ALU.max, op1=ALU.mult))

        dve.wait_ge(wg_in, 16)
        dve.tensor_copy(wg_split[:, :, 0:E], wg_s[:]).then_inc(wg_ready, 1)
        dve.wait_ge(wg_ready, 1)
        dve.tensor_tensor(wg_split[:, :, E:2 * E], wg_s[:], wg_split[:, :, 0:E].bitcast(F32), ALU.subtract) \
            .then_inc(wg_ready, 1)
        split_weights(VCH, [vo_f[:, c, :] for c in range(KC)], v_hi, v_lo, v_split, v_step)

        def split_rows(g):
            for k in range(KC):
                dve.wait_ge(ht_full, 4 * g.n + k + 1)
                dve.tensor_copy(ht_hi[:, k, :], ht[g.par][:, k, :]).then_inc(ht_hi_done, 1)
                dve.wait_ge(ht_hi_done, 4 * g.n + k + 1)
                dve.tensor_tensor(ht_lo[:, k, :], ht[g.par][:, k, :], ht_hi[:, k, :].bitcast(F32), ALU.subtract) \
                    .then_inc(ht_split, 1)

        split_rows(Group(0, 0))
        dve.wait_ge(gsum_xn, 1)
        dve.wait_ge(vcg_in, 16 * NBATCH)
        dve.scalar_tensor_tensor(out=g_c[:], in0=g_a[:], scalar=1.0, in1=g_b[:], op0=ALU.mult, op1=ALU.mult,
                                 accum_out=q_const[0:NSEG, 3:4]).then_inc(gsum_step, 1)
        dve.wait_ge(gsum_step, 3)
        dve.wait_ge(qcg_in, 16 * NBATCH)
        dve.tensor_scalar(q_const[0:NSEG, 3:4], q_const[0:NSEG, 3:4], q_const_g[:, 0:1], SCALE, ALU.add, ALU.mult) \
            .then_inc(gsum_step, 1)
        floor_gate(GA)
        dve.wait_ge(gsum_masked, 2)
        dve.reduce_max(MX[0:NSEG, 0:1], sg[:], AX_X).then_inc(gsum_step, 1)
        dve.wait_ge(gsum_step, 5)
        dve.scalar_tensor_tensor(out=MXC[0:NSEG, 0:1], in0=MX[0:NSEG, 0:1], scalar=SCALE, in1=q_const[0:NSEG, 3:4],
                                 op0=ALU.mult, op1=ALU.add).then_inc(gsum_step, 1)
        dve.wait_ge(gsum_step, 6)
        dve.tensor_tensor(NEGB[0:NSEG, 0:1], q_const[0:NSEG, 3:4], MXC[0:NSEG, 0:1], ALU.subtract).then_inc(gsum_negb, 1)
        dve.wait_ge(gsum_exp, 1)
        dve.reciprocal(PREC[0:NSEG, 0:1], PSUMS[0:NSEG, 0:1]).then_inc(gsum_step, 1)
        dve.wait_ge(gsum_step, 7)
        dve.tensor_scalar(pg[:, 0:NSEG], pg[:, 0:NSEG], PREC[0:NSEG, 0:1], None, ALU.mult).then_inc(gsum_prob, 1)
        dve.wait_ge(pro_evac, BROW + 1)
        dve.wait_ge(bo_in, 16)
        dve.tensor_tensor(brow[:], brow[:], bo_row[:], ALU.add).then_inc(brow_ready, 1)
        dve.wait_ge(pro_evac, MODS[CB] + 1)
        link(dve.tensor_scalar(modr[:, CB, :], modr[:, CB, :], 1.0, None, ALU.add))
        dve.wait_ge(pro_evac, TG + 1)
        dve.tensor_copy(g_split[:, 0, :], g_a[:]).then_inc(gsum_step, 1)
        dve.wait_ge(gsum_step, 8)
        dve.tensor_tensor(g_x[:], g_a[:], g_split[:, 0, :], ALU.subtract).then_inc(gsum_step, 1)
        dve.wait_ge(gsum_step, 9)
        dve.tensor_copy(g_split[:, 1, :], g_x[:]).then_inc(gsum_step, 1)
        dve.wait_ge(gsum_step, 10)
        dve.tensor_tensor(g_split[:, 2, :], g_x[:], g_split[:, 1, :], ALU.subtract).then_inc(g_split_done, 1)
        floor_gate(GB)
        dve.sem_inc(mod_fixed, 1)
        dve.wait_ge(pro_evac, PRO_END)
        dve.wait_ge(tab_in, 16)
        dve.wait_ge(qc_in, 16)
        dve.wait_ge(bg_in, 16)
        dve.wait_ge(made, POOL_MADE)

        def query_const(g):
            b = batch_of(g)
            for s in range(GS):
                if s > 0:
                    dve.wait_ge(qc_raw, 4 * g.n + s)
                dve.scalar_tensor_tensor(out=qc_junk, in0=xa[g.par][:, s, :], scalar=1.0,
                                         in1=vc_tab[:, bass.ds(b, 1), :].rearrange("p b d -> p (b d)"), op0=ALU.mult,
                                         op1=ALU.mult, accum_out=QRAW[:, s:s + 1]).then_inc(qc_raw, 1)
            dve.wait_ge(qc_raw, 4 * g.n + 4)
            dve.tensor_scalar(QCS2[g.par], QRAW, qc_bc[:, bass.ds(b, 1)], SCALE, ALU.add, ALU.mult) \
                .then_inc(qc_ready, 1)

        dve.wait_ge(g_split_done, 1)
        tok4 = [P, GS, E]

        def route_logits(g):
            r = RT * g.n
            dve.wait_ge(lg_full, g.n + 1)
            parts = pt_bank[:, 0:GS * 2 * E].rearrange("p (s c) -> p s c", c=2 * E)
            dve.tensor_tensor(lg[:], parts[:, :, 0:E], bg_bc[:].unsqueeze(1).to_broadcast(tok4), ALU.add) \
                .then_inc(lg_step, 1)
            dve.wait_ge(lg_step, g.n + 1)
            dve.tensor_tensor(lg[:], lg[:], parts[:, :, E:2 * E], ALU.add).then_inc(route, 1)
            dve.wait_ge(route, r + 1)
            dve.reduce_max(LG_MX, lg[:], AX_X).then_inc(route, 1)
            dve.wait_ge(route, r + 2)
            dve.tensor_tensor(lg_d[:], lg[:], LG_MX.unsqueeze(2).to_broadcast(tok4), ALU.subtract).then_inc(route, 1)
            dve.wait_ge(route, r + 3)
            dve.scalar_tensor_tensor(out=lg_v[:], in0=lg_d[:], scalar=0.0, in1=eidx[:], op0=ALU.is_ge,
                                     op1=ALU.mult).then_inc(route, 1)
            dve.wait_ge(route, r + 4)
            dve.tensor_reduce(V_MIN, lg_v[:], AX_X, ALU.min).then_inc(route, 1)
            dve.wait_ge(route, r + 5)
            dve.tensor_tensor(onehot[:], lg_v[:], V_MIN.unsqueeze(2).to_broadcast(tok4), ALU.is_equal) \
                .then_inc(route, 1)

        def route_slots(g):
            r = RT * g.n
            dve.wait_ge(pos_full, g.n + 1)
            dve.wait_ge(route, r + 6)
            dve.tensor_tensor(lg_r[:], pos_bank[:, 0:GS * E].rearrange("p (s e) -> p s e", e=E), onehot[:], ALU.mult) \
                .then_inc(route, 1)
            dve.wait_ge(route, r + 7)
            dve.reduce_sum(RANK, lg_r[:], AX_X).then_inc(route, 1)
            dve.wait_ge(route, r + 8)
            dve.tensor_scalar(OVER, RANK, float(CAP), float(NO_TOKEN), ALU.is_ge, ALU.mult).then_inc(route, 1)
            dve.tensor_tensor(over_tile[:], RANK.unsqueeze(2).to_broadcast([P, GS, GS - 1]), tile_ends[:], ALU.is_ge) \
                .then_inc(route, 1)
            dve.wait_ge(route, r + 9)
            dve.scalar_tensor_tensor(out=SLOT_A, in0=RANK, scalar=float(GS), in1=OVER, op0=ALU.mult, op1=ALU.add) \
                .then_inc(route, 1)
            dve.wait_ge(route, r + 10)
            dve.reduce_sum(TILE, over_tile[:], AX_X).then_inc(route, 1)
            dve.wait_ge(route, r + 11)
            dve.scalar_tensor_tensor(out=SLOT_B, in0=V_MIN, scalar=float(CAP), in1=SLOT_A, op0=ALU.mult, op1=ALU.add) \
                .then_inc(route, 1)
            dve.wait_ge(route, r + 13)
            dve.scalar_tensor_tensor(out=SLOT_A, in0=TILE, scalar=1.0 - GS * P, in1=SLOT_B, op0=ALU.mult, op1=ALU.add) \
                .then_inc(route, 1)
            dve.wait_ge(route, r + 14)
            wait_past(dve, scattered[g.par], 16 * GS * g.half)
            dve.tensor_scalar(slot_i[g.par][:], SLOT_A, float(E * CAP), None, ALU.add).then_inc(route, 1)
            dve.tensor_reduce(osum[:], onehot[:].rearrange("p s e -> p e s"), AX_X, ALU.add).then_inc(route, 1)
            dve.wait_ge(route, r + 16)
            dve.tensor_tensor(count[:], count[:], osum[:], ALU.add).then_inc(route, 1)
            dve.wait_ge(route_exp, g.n + 1)
            dve.reduce_sum(LG_SUM, lg_e[:], AX_X).then_inc(route, 1)
            dve.wait_ge(route, r + 18)
            dve.reciprocal(pay[g.par][:, :, 1].bitcast(F32), LG_SUM).then_inc(route, 1)
            dve.tensor_copy(pay[g.par][:, :, 0], tokids[:, bass.ds(g.n * GS, GS)]).then_inc(route, 1)

        def iteration(i, cur, prev, prev2, nxt, prev3):
            n = i.n
            p1, p2, p3 = i.plus(-1), i.plus(-2), i.plus(-3)
            if prev:
                dve.wait_ge(s_full, p1.n + 1)
                dve.reduce_max(MX, s_bank[:, :].rearrange("p (s t) -> p s t", t=P), AX_X).then_inc(mx_step, 1)
                dve.wait_ge(mx_step, 2 * p1.n + 1)
                dve.wait_ge(qc_ready, p1.n + 1)
                dve.scalar_tensor_tensor(out=MXC, in0=MX, scalar=SCALE, in1=QCS2[p1.par], op0=ALU.mult, op1=ALU.add) \
                    .then_inc(mx_step, 1)
                dve.wait_ge(mx_step, 2 * p1.n + 2)
                dve.tensor_tensor(NEGB, QCS2[p1.par], MXC, ALU.subtract).then_inc(negb_ready, 1)
            if prev3:
                route_logits(p3)
            if prev:
                dve.wait_ge(exp_done, 4 * p1.n + 4)
                dve.reciprocal(PREC, PSUMS).then_inc(prec_ready, 1)
                dve.wait_ge(prec_ready, p1.n + 1)
                dve.tensor_tensor(prob[:], prob[:], PREC.unsqueeze(2).to_broadcast([P, GS, P]), ALU.mult) \
                    .then_inc(prob_ready, 1)
            if prev2:
                for k in range(KC):
                    dve.wait_ge(h2t_hi_done, 4 * p2.n + k + 1)
                    dve.tensor_tensor(h2t_lo[:, k, :], big[(k + 2) % 4][:, :], h2t_hi[:, k, :].bitcast(F32),
                                      ALU.subtract).then_inc(h2t_split, 1)
            if nxt:
                stats1(i.plus(1))
            if prev:
                dve.wait_ge(pt_hi_done, p1.n + 1)
                dve.tensor_tensor(pt_lo[:].rearrange("p s t -> p (s t)"), pt_bank[:, :],
                                  pt_hi[:].rearrange("p s t -> p (s t)").bitcast(F32), ALU.subtract).then_inc(pt_split, 1)
            if prev3:
                route_slots(p3)
            if prev:
                if isinstance(n, int) and n == 1:
                    dve.wait_ge(late_tab_in, 48)
                if not isinstance(n, int) or n >= 3:
                    dve.wait_ge(h2_stored[p1.par], 16 * p1.half)
                dve.wait_ge(xr_in[p1.par], 16 * (p1.half + 1))
                for s in range(GS):
                    dve.wait_ge(av_full, 4 * p1.n + s + 1)
                    dve.tensor_tensor(h2[p1.par][:, s, :], big[s][:, :],
                                      ga_tab[:, bass.ds(batch_of(p1), 1), :].rearrange("p b d -> p (b d)"), ALU.mult) \
                        .then_inc(av_taken, 1)
                    dve.wait_ge(av_taken, 4 * p1.n + s + 1)
                    dve.tensor_tensor(xr[p1.par][:, s, :], xr[p1.par][:, s, :], h2[p1.par][:, s, :], ALU.add) \
                        .then_inc(x2_ready, 1)
                dve.wait_ge(x2_ready, 4 * p1.n + 4)
                layer_stats(p1.n, xr[p1.par], ln2_step, ln2_ready, 8, stats[1], mv[1], VE2, MN2,
                            lambda: wait_past(dve, xn2_done, 4 * p1.n))
            if prev and not cur:
                for s in range(LAST_POOL_SEG):
                    rows = h2[p1.par][:, s, :]
                    dve.wait_ge(xn2_done, 4 * p1.n + s + 1)
                    dve.tensor_tensor(rows, rows, cb_tab[:, batch_of(p1), :], ALU.mult).then_inc(last_scaled, 1)
                    dve.wait_ge(last_scaled, s + 1)
                    dve.tensor_tensor(rows, rows, sb_tab[:, batch_of(p1), :], ALU.add).then_inc(h2_ready, 1)
            if cur:
                for s in range(GS):
                    if s == 2:
                        query_const(i)
                    dve.wait_ge(u_hi_done, 4 * n + s + 1)
                    dve.tensor_tensor(u_lo[:, s, :], big[s][:, :], u_hi[:, s, :].bitcast(F32), ALU.subtract) \
                        .then_inc(u_split, 1)
            if nxt:
                split_rows(i.plus(1))

        def split_w1(n, e, b):
            dve.wait_ge(w1_in[b % 2], 16 * (NB // 2 * e + b // 2 + 1))
            wait_past(dve, h1_full, 4 * n - 4)
            dve.tensor_copy(w1_hi[b % 2][:], raw[2 * (b % 2)][:]).then_inc(w1_hi_done, 1)
            dve.wait_ge(w1_hi_done, n + 1)
            dve.tensor_tensor(w1_lo[b % 2][:], raw[2 * (b % 2)][:], w1_hi[b % 2][:].bitcast(F32), ALU.subtract) \
                .then_inc(w1_split, 1)

        iteration(Group(0, 0), True, False, False, True, False)
        iteration(Group(0, 1), True, True, False, True, False)
        iteration(Group(1, 0), True, True, True, True, False)
        iteration(Group(1, 1), True, True, True, True, True)
        iteration(Group(2, 0), True, True, True, True, True)
        iteration(Group(2, 1), True, True, True, True, True)
        with dve.Fori(3, NG // 2 - 1) as half:
            for par in range(2):
                iteration(Group(half, par), True, True, True, True, True)
        iteration(Group(NG // 2 - 1, 0), True, True, True, True, True)
        iteration(Group(NG // 2 - 1, 1), True, True, True, False, True)
        iteration(Group(NG // 2, 0), False, True, True, False, True)
        iteration(Group(NG // 2, 1), False, False, True, False, True)
        iteration(Group(NG // 2 + 1, 0), False, False, False, False, True)

        def w2_low(n, b):
            dve.wait_ge(w2_hi_done, n + 1)
            dve.tensor_tensor(w2_lo[b % 2][:], raw[2 * (b % 2) + 1][:], w2_hi[b % 2][:].bitcast(F32), ALU.subtract) \
                .then_inc(w2_split, 1)

        def split_hidden(e, b, j):
            n = NB * e + b
            dve.wait_ge(relu_done, 4 * n + j + 1)
            if j == 0:
                results_done(dve, e, b)
            dve.tensor_tensor(h1_lo[b % 2][:, j, :], h1_f[:, j, :], h1_hi[b % 2][:, j, :].bitcast(F32), ALU.subtract) \
                .then_inc(h1_split, 1)

        def rows_low(e):
            for k in range(KC):
                dve.wait_ge(bt_hi_done, 4 * e + k + 1)
                dve.tensor_tensor(bt_lo[:, k, :], h_bank[k][:, :], bt_hi[:, k, :].bitcast(F32), ALU.subtract) \
                    .then_inc(bt_split, 1)

        def result_rows(e, finish=False):
            if finish:
                dve.wait_ge(gb_gated, 4 * e + GS)
                dve.wait_ge(xo_in, 16 * GS * (e + 1))
            for i in range(GS):
                q, j = 4 * e + i, GS - 1 - i
                if i == 0:
                    dve.wait_ge(b2_in, 16 * (e + 1))
                dve.wait_ge(y_full, q + 1)
                wait_past(dve, y_sent[j], 16 * e)
                dve.tensor_tensor(yo[:, j, :], y_bank[j][:, :], b2_bc[:], ALU.add).then_inc(y_taken, 1)
                if finish:
                    dve.wait_ge(y_taken, q + 1)
                    dve.tensor_tensor(yo[:, j, :], yo[:, j, :], gb_rows[:, j, :], ALU.mult).then_inc(y_scaled, 1)
                    dve.wait_ge(y_scaled, q + 1)
                    dve.tensor_tensor(yo[:, j, :], yo[:, j, :], xo[:, j, :], ALU.add).then_inc(y_ready, 1)

        dve.wait_ge(count_full, 1)
        dve.tensor_copy(expert_rows[:], pos_bank[0:1, 0:E]).then_inc(rows_counted, 1)
        dve.memset(xh[:], 0.0).then_inc(rows_cleared, 1)
        split_w1(0, 0, 0)
        dve.wait_ge(table_in, 16)
        tok = table[:].rearrange("p e j c -> p (e j) c")
        dve.tensor_copy(tok_h[:], tok[:, 0:GS, 0]).then_inc(tok_h_ready, 1)
        dve.tensor_copy(tok_f[:], tok[:, :, 0]).then_inc(index_step, 1)
        dve.wait_ge(index_step, 1)
        dve.tensor_scalar(batch_f[:, 0, :], tok_f[:], float(L), None, ALU.is_ge).then_inc(index_step, 1)
        for b in range(2, NBATCH + 1):
            dve.wait_ge(index_step, b)
            dve.scalar_tensor_tensor(out=batch_f[:, b - 1, :], in0=tok_f[:], scalar=float(L * b),
                                     in1=batch_f[:, b - 2, :], op0=ALU.is_ge, op1=ALU.add).then_inc(index_step, 1)
        dve.wait_ge(index_step, NBATCH + 1)
        dve.tensor_scalar(gb_index[:], batch_f[:, NBATCH - 1, :], 7.0, float(GB), ALU.mult, ALU.add) \
            .then_inc(index_step, 1)
        dve.wait_ge(index_step, NBATCH + 2)
        rows_low(0)
        dve.memset(xo[:], 0.0).then_inc(rows_cleared, 1)
        dve.memset(gb_rows[:], 0.0).then_inc(rows_cleared, 1)

        def expert(e, first, last):
            for b in range(NB):
                n = NB * e + b
                if b == 0 and not last:
                    for j in range(GS):
                        dve.wait_ge(xh_in[j], 16 * (e + 1))
                    stand_alone(dve, dve_passed)
                    dve.tensor_copy(tok_h[:], tok[:, bass.ds(GS * (e + 1), GS), 0]).then_inc(tok_h_ready, 1)
                split_hidden(e, b, 0)
                if b + 1 < NB:
                    split_w1(n + 1, e, b + 1)
                elif not last:
                    split_w1(n + 1, e + 1, 0)
                for j in range(1, HC):
                    split_hidden(e, b, j)
                w2_low(n, b)
                if b == 0 and not first:
                    result_rows(e - 1)
                if b == 2:
                    if not first:
                        for j in range(GS):
                            dve.wait_ge(y_sent[j], 16 * e)
                        dve.wait_ge(gb_gated, 4 * e)
                        stand_alone(dve, dve_passed)
                    dve.tensor_copy(tok_x[:], tok[:, bass.ds(GS * e, GS), 0]).then_inc(tok_x_ready, 1)
                    dve.tensor_copy(tok_g[:], gb_index[:, bass.ds(GS * e, GS)]).then_inc(tok_x_ready, 1)
                    dve.tensor_copy(gate_x[:], tok[:, bass.ds(GS * e, GS), 1].bitcast(F32)).then_inc(gate_ready, 1)
            if not last:
                rows_low(e + 1)

        expert(0, True, False)
        expert(1, False, False)
        with dve.Fori(2, E - 1) as e:
            expert(e, False, False)
        expert(E - 1, False, True)
        result_rows(E - 1, True)

    @block.gpsimd
    def _(pool):
        pool.memset(ident[:], 0.0).then_inc(ident_made, 1)
        pool.wait_ge(ident_made, 1)
        pool.affine_select(out=ident[:], in_=ident[:], compare_op=ALU.not_equal, fill=1.0, base=0, pattern=[[-1, P]],
                           channel_multiplier=1).then_inc(ident_made, 1)
        pool.memset(tri[:], 1.0).then_inc(made, 1)
        pool.memset(ones[:], 1.0).then_inc(made, 1)
        pool.memset(seg_sel[:], 1.0).then_inc(made, 1)
        pool.wait_ge(made, 3)
        pool.affine_select(out=tri[:], in_=tri[:], compare_op=ALU.is_gt, fill=0.0, base=0, pattern=[[1, P]],
                           channel_multiplier=-1).then_inc(made, 1)
        pool.affine_select(out=seg_sel[:], in_=seg_sel[:], compare_op=ALU.is_ge, fill=0.0, base=0,
                           pattern=[[-3, GS], [0, P]], channel_multiplier=1).then_inc(made, 1)
        pool.wait_ge(made, 5)
        pool.affine_select(out=seg_sel[:], in_=seg_sel[:], compare_op=ALU.is_ge, fill=0.0, base=2,
                           pattern=[[3, GS], [0, P]], channel_multiplier=-1).then_inc(made, 1)
        pool.iota(tokids[:], pattern=[[P, NSEG]], base=0, channel_multiplier=1).then_inc(made, 1)
        pool.iota(eidx[:], pattern=[[0, GS], [1, E]], base=-E, channel_multiplier=0,
                  allow_small_or_imprecise_dtypes=True).then_inc(made, 1)
        pool.iota(tile_ends[:], pattern=[[0, GS], [P, GS - 1]], base=P, channel_multiplier=0,
                  allow_small_or_imprecise_dtypes=True).then_inc(made, 1)
        pool.wait_ge(made, POOL_MADE)
        pool.wait_ge(init_made, DVE_MADE)

        def inverse_root(g, ready, step, ve, mn, rs, nr, parts=P, segs=GS):
            pool.wait_ge(ready, 2 * g + 2)
            pool.tensor_tensor(rs[0:parts, 0:segs], ve[0:parts, 0:segs], half_neg[0:parts, 0:segs], ALU.pow) \
                .then_inc(step, 1)
            pool.wait_ge(step, 2 * g + 1)
            pool.tensor_tensor(nr[0:parts, 0:segs], mn[0:parts, 0:segs], rs[0:parts, 0:segs], ALU.mult).then_inc(step, 1)

        def normalise1(g):
            inverse_root(g.n, ln1_ready, ln1_rstd, VE1, MN1, RS1, NR1)
            pool.wait_ge(ln1_rstd, 2 * g.n + 2)
            stand_alone(pool, pool_passed)
            for s in range(GS):
                pool.tensor_scalar(xa[g.par][:, s, :], xa[g.par][:, s, :], RS1[:, s:s + 1], NR1[:, s:s + 1], ALU.mult,
                                   ALU.add).then_inc(xn_done, 1)

        normalise1(Group(0, 0))
        pool.wait_ge(table_cleared, 16)
        inverse_root(0, gsum_stats, gsum_rstd, VE2, MN2, RS2, NR2, NSEG, 1)
        pool.wait_ge(pro_evac, SG + 1)
        blocks = sg[:].rearrange("p (b r) -> p b r", b=NBATCH)
        pool.affine_select(out=blocks, in_=blocks, compare_op=ALU.is_ge, fill=FAR_BELOW, base=0,
                           pattern=[[-(NSEG // NBATCH), NBATCH], [0, NSEG // NBATCH]], channel_multiplier=1) \
            .then_inc(gsum_masked, 1)
        pool.wait_ge(gsum_masked, 1)
        pool.affine_select(out=blocks, in_=blocks, compare_op=ALU.is_ge, fill=FAR_BELOW, base=NSEG // NBATCH - 1,
                           pattern=[[NSEG // NBATCH, NBATCH], [0, NSEG // NBATCH]], channel_multiplier=-1) \
            .then_inc(gsum_masked, 1)

        def scatter(g):
            pool.wait_ge(route, RT * g.n + RT)
            stand_alone(pool, pool_passed)
            for s in range(GS):
                pool.indirect_dma_start(out=table_dram, out_offset=bass.IndirectOffsetOnAxis(slot_i[g.par][:, s:s + 1], 0),
                                        in_=pay[g.par][:, s, :], in_offset=None, bounds_check=E * CAP - 1,
                                        oob_is_err=False).then_inc(scattered[g.par], 16)

        def iteration(i, prev, nxt, prev3):
            p1 = i.plus(-1)
            b = batch_of(p1)
            if nxt:
                normalise1(i.plus(1))
            if prev3:
                scatter(i.plus(-3))
            if prev:
                inverse_root(p1.n, ln2_ready, ln2_rstd, VE2, MN2, RS2, NR2)
                if isinstance(i.n, int) and i.n == 1:
                    pool.wait_ge(late_tab_in, 48)
                last_group = isinstance(p1.n, int) and p1.n == NG - 1
                first_seg = LAST_POOL_SEG if last_group else 0
                for s in range(first_seg, GS):
                    rows = h2[p1.par][:, s, :]
                    pool.wait_ge(xn2_done, 4 * p1.n + s + 1)
                    stand_alone(pool, pool_passed)
                    pool.tensor_tensor(rows, rows, cb_tab[:, bass.ds(b, 1), :].rearrange("p b d -> p (b d)"), ALU.mult) \
                        .then_inc(h2_scaled, 1)
                    pool.wait_ge(h2_scaled, 4 * p1.n + s + 1 - first_seg)
                    stand_alone(pool, pool_passed)
                    pool.tensor_tensor(rows, rows, sb_tab[:, bass.ds(b, 1), :].rearrange("p b d -> p (b d)"), ALU.add) \
                        .then_inc(h2_ready, 1)

        iteration(Group(0, 0), False, True, False)
        iteration(Group(0, 1), True, True, False)
        iteration(Group(1, 0), True, True, False)
        iteration(Group(1, 1), True, True, True)
        with pool.Fori(2, NG // 2 - 1) as half:
            for par in range(2):
                iteration(Group(half, par), True, True, True)
        iteration(Group(NG // 2 - 1, 0), True, True, True)
        iteration(Group(NG // 2 - 1, 1), True, False, True)
        iteration(Group(NG // 2, 0), True, False, True)
        iteration(Group(NG // 2, 1), False, False, True)
        iteration(Group(NG // 2 + 1, 0), False, False, True)

        def gather(rows, source, tokens, done, n=T):
            for j in range(GS - 1, -1, -1):
                pool.indirect_dma_start(out=rows[:, j, :], out_offset=None, in_=source,
                                        in_offset=bass.IndirectOffsetOnAxis(tokens[:, j:j + 1], 0), bounds_check=n - 1,
                                        oob_is_err=False).then_inc(done[j] if isinstance(done, list) else done, 16)

        def gather_h(e):
            wait_past(pool, bt_full, 4 * e)
            pool.wait_ge(tok_h_ready, e + 1)
            stand_alone(pool, pool_passed)
            gather(xh, h2_dram, tok_h, xh_in)

        def gather_x(e):
            pool.wait_ge(tok_x_ready, 2 * e + 2)
            wait_past(pool, y_scaled, 4 * e)
            stand_alone(pool, pool_passed)
            gather(gb_rows, mod_dram.rearrange("b r d -> (b r) d"), tok_g, gb_in, NBATCH * 7)
            gather(xo, out_rows, tok_x, xo_in)

        def finish_rows(e):
            pool.wait_ge(xo_in, 16 * GS * (e + 1))
            for i in range(GS):
                q, j = 4 * e + i, GS - 1 - i
                if not (isinstance(e, int) and e == E - 1):
                    pool.wait_ge(gb_gated, 4 * e + j + 1)
                    pool.wait_ge(y_taken, q + 1)
                    pool.tensor_tensor(yo[:, j, :], yo[:, j, :], gb_rows[:, j, :], ALU.mult).then_inc(y_scaled, 1)
                    pool.wait_ge(y_scaled, q + 1)
                    pool.tensor_tensor(yo[:, j, :], yo[:, j, :], xo[:, j, :], ALU.add).then_inc(y_ready, 1)
                pool.wait_ge(y_ready, q + 1)
                stand_alone(pool, pool_passed)
                pool.indirect_dma_start(out=out_rows, out_offset=bass.IndirectOffsetOnAxis(tok_x[:, j:j + 1], 0),
                                        in_=yo[:, j, :], in_offset=None, bounds_check=T - 1, oob_is_err=False) \
                    .then_inc(y_sent[j], 16)

        for par in range(2):
            pool.wait_ge(h2_stored[par], 16 * (NG // 2))
            pool.wait_ge(x2_stored[par], 16 * (NG // 2))
        pool.wait_ge(rows_cleared, 1)
        gather_h(0)
        gather_h(1)
        pool.wait_ge(rows_cleared, 3)
        gather_x(0)
        with pool.Fori(1, E - 1) as e:
            gather_h(e + 1)
            finish_rows(e - 1)
            gather_x(e)
        finish_rows(E - 2)
        gather_x(E - 1)
        finish_rows(E - 1)

    stack.close()


_INS = ["L0_attn_x", "L0_attn_Wq", "L0_attn_bq", "L0_attn_Wk", "L0_attn_bk", "L0_attn_Wv", "L0_attn_bv",
        "L0_attn_Wo", "L0_attn_bo", "L0_ffn_Wg", "L0_ffn_bg", "L0_ffn_W1", "L0_ffn_b1", "L0_ffn_W2", "L0_ffn_b2",
        "L0_c", "L0_wmod"]


def kernel(**inputs):
    import numpy as _np
    import concourse.bacc as _bacc
    from concourse import mybir as _mybir
    from concourse.bass_utils import run_bass_kernel_spmd as _run

    nc = _bacc.Bacc("TRN2", target_bir_lowering=False, num_devices=1)
    arrays, args = {}, []
    for name in _INS:
        a = _np.ascontiguousarray(inputs[name])
        arrays[f"in_{name}_dram"] = a
        args.append(nc.dram_tensor(f"in_{name}_dram", a.shape, _mybir.dt.from_np(a.dtype), kind="ExternalInput").ap())
    shape = inputs["L0_attn_x"].shape
    out = nc.dram_tensor("out_0_dram", shape, _mybir.dt.float32, kind="ExternalOutput").ap()
    build_block(nc, *args, out)
    r = _run(nc, [arrays], core_ids=[0])
    return r.results[0]["out_0_dram"]
```
